# Optimizing a Trainium2 kernel written in Bass

```python
import numpy as np
import jax
import jax.numpy as jnp

def _softmax(x, axis=-1):
    return jax.nn.softmax(x, axis=axis)

def _gelu(x):
    return jax.nn.gelu(x, approximate=True)

def _silu(x):
    return jax.nn.silu(x)

def _sigmoid(x):
    return jax.nn.sigmoid(x)

def _layernorm(x, axis=-1, eps=1e-05):
    m = jnp.mean(x, axis=axis, keepdims=True)
    v = jnp.var(x, axis=axis, keepdims=True)
    return (x - m) / jnp.sqrt(v + eps)

def _scatter_add(tgt, idx, src, axis=0):
    return tgt.at[idx].add(src)

def _segment_sum(src, seg, n):
    return jax.ops.segment_sum(src, seg, n)
kernel_name = 'mk_sandwich_d1_jaxref_r4_fad10a'

def setup_inputs(seed: int=0):
    np.random.seed(seed)
    _w = jnp.asarray

    def _L0_attn_setup():
        import jax, jax.numpy as jnp
        import numpy as np
        N_EMBD = 256
        N_HEAD = 16
        HEAD_DIM = N_EMBD // N_HEAD
        LATENT_DIM = N_EMBD // 2
        B, T = (4, 512)
        key = jax.random.key(seed)
        ks = jax.random.split(key, 5)

        def init(k, fan_in, fan_out):
            bound = 1.0 / np.sqrt(fan_in)
            return jax.random.uniform(k, (fan_in, fan_out), jnp.float32, -bound, bound)
        return {'x': jax.random.normal(ks[0], (B, T, N_EMBD), jnp.float32), 'Wc_down': init(ks[1], N_EMBD, LATENT_DIM), 'Wq_up': init(ks[2], LATENT_DIM, N_EMBD), 'Wkv_up': init(ks[3], LATENT_DIM, 2 * HEAD_DIM), 'Wc_proj': init(ks[4], N_EMBD, N_EMBD)}
    _L0_attn_in = _L0_attn_setup()

    def _L0_ffn_setup():
        import jax, jax.numpy as jnp
        import numpy as np
        E = 8
        D = 256
        F = 1024
        S, B = (512, 2)
        LN_EPS = 1e-05

        def _moe_forward(input_features, centroids, ln_g, ln_b, W1, b1, W2, b2):
            s, b, d = input_features.shape
            x = jnp.swapaxes(input_features, 0, 1).reshape(-1, d)
            logits = x.astype(jnp.float32) @ centroids.astype(jnp.float32).T
            assign = jnp.argmax(logits, axis=-1)
            onehot = jax.nn.one_hot(assign, E, dtype=x.dtype)
            disp = jnp.einsum('te,td->etd', onehot, x)
            mu = disp.mean(-1, keepdims=True)
            var = disp.var(-1, keepdims=True)
            xn = (disp - mu) * jax.lax.rsqrt(var + LN_EPS)
            xn = xn * ln_g[:, None, :] + ln_b[:, None, :]
            h = jax.nn.relu(jnp.einsum('etd,edf->etf', xn, W1) + b1[:, None, :])
            y = jnp.einsum('etf,efd->etd', h, W2) + b2[:, None, :]
            y = disp + y
            out = jnp.einsum('te,etd->td', onehot, y)
            return jnp.swapaxes(out.reshape(b, s, d), 0, 1)
        key = jax.random.key(seed)
        ks = jax.random.split(key, 8)
        scale_in = 1.0 / np.sqrt(D)
        scale_ff = 1.0 / np.sqrt(F)
        return {'input_features': jax.random.normal(ks[0], (S, B, D), dtype=jnp.float32), 'centroids': jax.random.normal(ks[1], (E, D), dtype=jnp.float32) * scale_in, 'ln_g': jnp.ones((E, D), dtype=jnp.float32), 'ln_b': jnp.zeros((E, D), dtype=jnp.float32), 'W1': jax.random.normal(ks[2], (E, D, F), dtype=jnp.float32) * scale_in, 'b1': jax.random.normal(ks[3], (E, F), dtype=jnp.float32) * 0.01, 'W2': jax.random.normal(ks[4], (E, F, D), dtype=jnp.float32) * scale_ff, 'b2': jax.random.normal(ks[5], (E, D), dtype=jnp.float32) * 0.01}
    _L0_ffn_in = _L0_ffn_setup()
    _d = {'L0_attn_x': _L0_attn_in['x'], 'L0_attn_Wc_down': _L0_attn_in['Wc_down'], 'L0_attn_Wq_up': _L0_attn_in['Wq_up'], 'L0_attn_Wkv_up': _L0_attn_in['Wkv_up'], 'L0_attn_Wc_proj': _L0_attn_in['Wc_proj'], 'L0_ffn_centroids': _L0_ffn_in['centroids'], 'L0_ffn_ln_g': _L0_ffn_in['ln_g'], 'L0_ffn_ln_b': _L0_ffn_in['ln_b'], 'L0_ffn_W1': _L0_ffn_in['W1'], 'L0_ffn_b1': _L0_ffn_in['b1'], 'L0_ffn_W2': _L0_ffn_in['W2'], 'L0_ffn_b2': _L0_ffn_in['b2']}
    _x0 = _d['L0_attn_x']
    _d['L0_attn_x'] = jax.random.normal(jax.random.fold_in(jax.random.key(seed), 1), (4, 1024, 256), dtype=_x0.dtype)
    del _x0
    return _d

def reference(L0_attn_x, L0_attn_Wc_down, L0_attn_Wq_up, L0_attn_Wkv_up, L0_attn_Wc_proj, L0_ffn_centroids, L0_ffn_ln_g, L0_ffn_ln_b, L0_ffn_W1, L0_ffn_b1, L0_ffn_W2, L0_ffn_b2):

    def _L0_attn_ref(x, Wc_down, Wq_up, Wkv_up, Wc_proj):
        import jax, jax.numpy as jnp
        import numpy as np
        N_EMBD = 256
        N_HEAD = 16
        HEAD_DIM = N_EMBD // N_HEAD
        LATENT_DIM = N_EMBD // 2
        B, T = (4, 512)
        Bsz, Tlen, C = x.shape
        latent = x @ Wc_down
        q = (latent @ Wq_up).reshape(Bsz, Tlen, N_HEAD, HEAD_DIM)
        kv = latent @ Wkv_up
        k, v = (kv[..., :HEAD_DIM], kv[..., HEAD_DIM:])
        scale = 1.0 / np.sqrt(HEAD_DIM)
        att = jnp.einsum('bthd,bsd->bhts', q, k) * scale
        causal = jnp.tril(jnp.ones((Tlen, Tlen), dtype=bool))
        att = jnp.where(causal[None, None], att, -jnp.inf)
        att = jax.nn.softmax(att, axis=-1)
        y = jnp.einsum('bhts,bsd->bthd', att, v).reshape(Bsz, Tlen, C)
        return y @ Wc_proj

    def _L0_ffn_ref(input_features, centroids, ln_g, ln_b, W1, b1, W2, b2):
        import jax, jax.numpy as jnp
        import numpy as np
        E = 8
        D = 256
        F = 1024
        S, B = (512, 2)
        LN_EPS = 1e-05

        def _moe_forward(input_features, centroids, ln_g, ln_b, W1, b1, W2, b2):
            s, b, d = input_features.shape
            x = jnp.swapaxes(input_features, 0, 1).reshape(-1, d)
            logits = x.astype(jnp.float32) @ centroids.astype(jnp.float32).T
            assign = jnp.argmax(logits, axis=-1)
            onehot = jax.nn.one_hot(assign, E, dtype=x.dtype)
            disp = jnp.einsum('te,td->etd', onehot, x)
            mu = disp.mean(-1, keepdims=True)
            var = disp.var(-1, keepdims=True)
            xn = (disp - mu) * jax.lax.rsqrt(var + LN_EPS)
            xn = xn * ln_g[:, None, :] + ln_b[:, None, :]
            h = jax.nn.relu(jnp.einsum('etd,edf->etf', xn, W1) + b1[:, None, :])
            y = jnp.einsum('etf,efd->etd', h, W2) + b2[:, None, :]
            y = disp + y
            out = jnp.einsum('te,etd->td', onehot, y)
            return jnp.swapaxes(out.reshape(b, s, d), 0, 1)
        return _moe_forward(input_features, centroids, ln_g, ln_b, W1, b1, W2, b2)
    x = L0_attn_x
    x = x + _layernorm(_L0_attn_ref(_layernorm(x, axis=-1), L0_attn_Wc_down, L0_attn_Wq_up, L0_attn_Wkv_up, L0_attn_Wc_proj), axis=-1)
    x = x + _layernorm(_L0_ffn_ref(_layernorm(x, axis=-1), L0_ffn_centroids, L0_ffn_ln_g, L0_ffn_ln_b, L0_ffn_W1, L0_ffn_b1, L0_ffn_W2, L0_ffn_b2), axis=-1)
    return x

_drawn_inputs = setup_inputs


def setup_inputs(seed=0):
    import zlib

    import numpy as np

    out = dict(_drawn_inputs(seed))
    spreads = {'L0_ffn_ln_g': (1.0, 0.2), 'L0_ffn_ln_b': (0.0, 0.311)}
    factors = {'L0_ffn_b1': 22.597, 'L0_ffn_b2': 8.0}
    for name, (base, spread) in spreads.items():
        noise = np.random.default_rng([zlib.crc32(name.encode()), seed]).standard_normal(out[name].shape)
        drawn = base * np.exp(spread * noise) if base else spread * noise
        out[name] = jnp.asarray(drawn.astype(out[name].dtype))
    for name, factor in factors.items():
        out[name] = (out[name] * factor).astype(out[name].dtype)
    return out
```

```python
from contextlib import ExitStack

import concourse.bass as bass
import concourse.mybir as mybir

F32 = mybir.dt.float32
BF16 = mybir.dt.bfloat16
I32 = mybir.dt.int32
U32 = mybir.dt.uint32
ALU = mybir.AluOpType
ACT = mybir.ActivationFunctionType
AX = mybir.AxisListType.X
ds = bass.ds

P = 128
B, T, D = 4, 1024, 256
NTOK = B * T
NT = NTOK // P
TB = T // P
NH, HD = 16, 16
LAT = D // 2
GH = 4
NG = NH // GH
NQ = 512
QC = T // NQ
DC = D // P
EPS = 1e-5
SCALE = 1.0 / HD ** 0.5
LOWEST = -3.0e38
E, F = 8, 1024
FC = F // P
NS = NT + E - 1

QPART = (0, 0, 0, 1, 1, 2)
KPART = (0, 1, 2, 0, 1, 0)
NR = len(QPART) * HD
KR = NR + 3

STEPS = [(c, j, max(0, j - c * (NQ // P)) * P) for c in range(QC) for j in range((c + 1) * (NQ // P))]
DIAG = [s for s, (c, j, off) in enumerate(STEPS) if j >= c * (NQ // P)]
LAST = len(STEPS) - 1
C0 = NQ // P - 1
MAXES = []
for i in range(TB):
    full, rest = divmod((i + 1) * P, NQ)
    MAXES += [(i, c, NQ, rest == 0 and c == full - 1) for c in range(full)]
    MAXES += [(i, full, rest, True)] if rest else []
NM = GH * len(MAXES)
MAX_AT = [round(NM * sum(NQ - o for _, _, o in STEPS[:s + 1]) / sum(NQ - o for _, _, o in STEPS))
          for s in range(len(STEPS))]
MAX_OF = [MAX_AT[s] - (MAX_AT[s - 1] if s else 0) for s in range(len(STEPS))]

PIECES = ("q00", "q01", "kv0", "kv1", "q10", "q11")
MISC = (
    (("m", 2), ("q00", 4), ("o0", 6), ("q01", 7), ("kv0", 9), ("o1", 99)),
    (("m", 2), ("kv1", 4), ("o0", 6), ("vt", 8), ("q10", 9), ("o1", 99)),
    (("m", 2), ("q11", 4), ("o0", 6), ("o1", 99)),
    (("m", 2), ("o0", 6), ("o1", 99)),
)
MISC_FIRST = PIECES[:4] + ("vt",) + PIECES[4:] + ("m",)
MISC_BATCH = sum(len(m) for m in MISC)


def misc_events(g, more):
    return [(n, s) for n, s in MISC[g] if more or n in ("o0", "o1") or (n == "m" and g < NG - 1)]


def misc_at(b, g, name, more):
    before = [n for k in range(g) for n, _ in misc_events(k, more)]
    before += [n for n, _ in misc_events(g, more)]
    k = len([n for kk in range(g) for n, _ in misc_events(kk, more)])
    return len(MISC_FIRST) + b * MISC_BATCH + before.index(name, k)


def past(eng, sem, n):
    if not isinstance(n, int) or n > 0:
        eng.wait_ge(sem, n)


def alone(eng, spare):
    eng.sem_inc(spare, 1)


def build(nc, x, Wc_down, Wq_up, Wkv_up, Wc_proj, centroids, ln_g, ln_b, W1, b1, W2, b2, out):
    with ExitStack() as ctx:
        sb = lambda name, shape, dt=F32: ctx.enter_context(nc.sbuf_tensor(name, shape, dt))
        sem = lambda name: ctx.enter_context(nc.semaphore(name))
        x1_dram = nc.dram_tensor("x1_rows", (NTOK, D), F32, kind="Internal").ap()
        W1s = sb("W1s", [P, DC, E * F])
        ident = sb("ident", [P, P])
        identb = sb("identb", [P, P], BF16)
        eps = sb("eps", [P, 1])
        IDX = sb("IDX", [P, NS], I32)
        EX = sb("EX", [P, NS], I32)
        started = sem("started")
        spare = sem("spare")
        w1_in = sem("w1_in")
        w2_in = sem("w2_in")
        w1_v = W1.rearrange("e (c p) f -> e p c f", p=P)
        w2_v = W2.rearrange("e (c p) d -> e p c d", p=P)
        Y = sb("Y", [P, NT * D])
        attention(nc, eps, started, spare, x, Wc_down, Wq_up, Wkv_up, ident, identb, Y, W1s, w1_v, w1_in)
        with ExitStack() as fctx:
            W2s = fctx.enter_context(nc.sbuf_tensor("W2s", [P, E, FC * D], F32))
            route(nc, started, spare, x, Wc_proj, centroids, ident, eps, Y, W2s, w2_v, w2_in, x1_dram, IDX, EX)
            experts(nc, started, spare, ln_g, ln_b, b1, b2, ident, eps, W1s, w1_in, W2s, w2_in, x1_dram, IDX, EX, out)


def attention(nc, eps, started, spare, x, Wc_down, Wq_up, Wkv_up, ident, identb, Y, W1s, w1_v, w1_in):
    with ExitStack() as ctx:
        sb = lambda name, shape, dt=F32: ctx.enter_context(nc.sbuf_tensor(name, shape, dt))
        sem = lambda name: ctx.enter_context(nc.semaphore(name))
        psum = lambda name, shape, dt=F32: ctx.enter_context(nc.psum_tensor(name, shape, dt))
        causal = sb("causal", [P, NQ])
        LT = sb("LT", [P, NTOK])
        Wq = sb("Wq", [P, D])
        Wkv = sb("Wkv", [P, 2 * HD])
        Q = sb("Q", [P, NH, T], BF16)
        KN = sb("KN", [P, T], BF16)
        KC = sb("KC", [P, T], BF16)
        VN = sb("VN", [P, TB, 2 * HD])
        VC = sb("VC", [P, TB, 2 * HD])
        T1, T2, T3 = (sb(f"T{k}", [P, 2, T], BF16) for k in (1, 2, 3))
        K1, K2, K3 = (sb(f"K{k}", [2 * HD, T], BF16) for k in (1, 2, 3))
        R1 = sb("R1", [P, NQ])
        KV = sb("KV", [2 * HD, T])
        MP = [sb(f"MP{k}", [P, 2, GH, TB]) for k in range(2)]
        mx = sb("mx", [P, GH * TB])
        mr = sb("mr", [P, GH * TB])
        NMX = sb("NMX", [P, 3, GH * TB], BF16)
        MT = sb("MT", [3 * GH * TB, P], BF16)
        junk = sb("junk", [P, 2, NQ], BF16)
        rden = sb("rden", [P, NQ // P, GH])
        small_pool = 0

        s_id = sem("s_id")
        s_w = sem("s_w")
        s_mask = sem("s_mask")
        ones_set = sem("ones_set")

        with ExitStack() as c2:
            sb2 = lambda name, shape, dt=F32: c2.enter_context(nc.sbuf_tensor(name, shape, dt))
            ps2 = lambda name, shape, dt=F32: c2.enter_context(nc.psum_tensor(name, shape, dt))
            sem2 = lambda name: c2.enter_context(nc.semaphore(name))
            QT = 4
            X = [sb2(f"X{k}", [P, QT, D]) for k in range(2)]
            XN = sb2("XN", [P, QT, D])
            XT = sb2("XT", [P, DC, QT * P])
            Wd = sb2("Wd", [P, DC, LAT])
            st = sb2("st", [P, QT, 6])
            mv = sb2("mv", [P, QT, 2])
            rs = sb2("rs", [P, QT])
            sd = sb2("sd", [P, QT])
            xtp = [ps2(f"xtp{k}", [P, QT * P]) for k in range(DC)]
            ltp = ps2("ltp", [P, QT * P])
            x_in = [sem2(f"x_in{k}") for k in range(2)]
            stats = sem2("stats")
            aggr = sem2("aggr")
            sd_ready = sem2("sd_ready")
            rstd = sem2("rstd")
            xn_ready = sem2("xn_ready")
            xt_ready = sem2("xt_ready")
            xt_copied = sem2("xt_copied")
            lt_ready = sem2("lt_ready")
            lt_copied = sem2("lt_copied")
            N1 = NT // QT
            xv = x.rearrange("b (i p) d -> p (b i) d", p=P)
            block = c2.enter_context(nc.Block())

            @block.sync
            def _(sp):
                sp.dma_start(X[0][:, :, :], xv[:, 0:QT, :]).then_inc(x_in[0], 16)
                sp.dma_start(X[1][:, :, :], xv[:, QT:2 * QT, :]).then_inc(x_in[1], 16)
                sp.dma_start(Wd[:, :, :], Wc_down.rearrange("(c p) n -> p c n", p=P)).then_inc(s_w, 16)
                sp.dma_start(Wq[:, :], Wq_up[:, :]).then_inc(s_w, 16)
                sp.dma_start(Wkv[:, :], Wkv_up[:, :]).then_inc(s_w, 16)
                for t in range(2, N1):
                    sp.wait_ge(xn_ready, QT * (t - 1))
                    sp.dma_start(X[t % 2][:, :, :], xv[:, t * QT:(t + 1) * QT, :]).then_inc(x_in[t % 2], 16)

            @block.gpsimd
            def _(pool):
                pool.memset(ident[:, :], 0.0).then_inc(s_id, 1)
                pool.memset(identb[:, :], 0.0).then_inc(s_id, 1)
                pool.memset(causal[:, :], 0.0).then_inc(s_id, 1)
                pool.wait_ge(s_id, 3)
                for m in (ident, identb):
                    pool.affine_select(out=m[:, :], in_=m[:, :], compare_op=ALU.not_equal, fill=1.0, base=0,
                                       pattern=[[-1, P]], channel_multiplier=1).then_inc(s_id, 1)
                m = causal[:, NQ - P:NQ]
                pool.affine_select(out=m, in_=m, compare_op=ALU.is_ge, fill=LOWEST, base=0,
                                   pattern=[[-1, P]], channel_multiplier=1).then_inc(s_id, 1)
                pool.memset(KN[:, :], 1.0).then_inc(ones_set, 1)
                pool.memset(VN[:, :, :], 1.0).then_inc(ones_set, 1)
                for k in range(2):
                    pool.memset(MP[k][:, :, :, :], LOWEST).then_inc(ones_set, 1)

            @block.vector
            def _(dve):
                dve.memset(eps[:, :], EPS).then_inc(started, 1)
                with dve.Fori(0, N1 // 2) as t2:
                    for k in range(2):
                        t = 2 * t2 + k
                        dve.wait_ge(x_in[k], 16 * (t2 + 1))
                        for i in range(QT):
                            dve.bn_stats(st[:, i, :], X[k][:, i, :]).then_inc(stats, 1)
                        for i in range(QT):
                            dve.wait_ge(stats, QT * t + i + 1)
                            alone(dve, spare)
                            dve.bn_aggr(mv[:, i, :], st[:, i, :]).then_inc(aggr, 1)
                        dve.wait_ge(sd_ready, t + 1)
                        dve.reciprocal(rs[:, :], sd[:, :]).then_inc(rstd, 1)
                        dve.wait_ge(rstd, t + 1)
                        for i in range(QT):
                            dve.tensor_scalar(XN[:, i, :], X[k][:, i, :], mv[:, i, 0:1], rs[:, i:i + 1],
                                              ALU.subtract, ALU.mult).then_inc(xn_ready, 1)
                        dve.wait_ge(xn_ready, QT * (t + 1))

            @block.tensor
            def _(pe):
                pe.wait_ge(s_id, 6)
                pe.wait_ge(s_w, 48)
                with pe.Fori(0, N1) as t:
                    for i in range(QT):
                        pe.wait_ge(xn_ready, QT * t + i + 1)
                        for c in range(DC):
                            last = pe.transpose(xtp[c][:, i * P:(i + 1) * P], XN[:, i, c * P:(c + 1) * P], ident[:, :])
                    last.then_inc(xt_ready, 1)
                    for c in range(DC):
                        pe.wait_ge(xt_copied, DC * t + c + 1)
                        mm = pe.matmul(ltp[:, :], Wd[:, c, :], XT[:, c, :], start=c == 0, stop=c == DC - 1)
                    mm.then_inc(lt_ready, 1)

            @block.scalar
            def _(act):
                act.wait_ge(started, 1)
                with act.Fori(0, N1) as t:
                    act.wait_ge(aggr, QT * (t + 1))
                    act.activation(sd[:, :], mv[:, :, 1], ACT.Sqrt, bias=eps[:, :]).then_inc(sd_ready, 1)
                    act.wait_ge(xt_ready, t + 1)
                    for c in range(DC):
                        act.activation(XT[:, c, :], xtp[c][:, :], ACT.Copy).then_inc(xt_copied, 1)
                    act.wait_ge(lt_ready, t + 1)
                    act.activation(LT[:, ds(t * (QT * P), QT * P)], ltp[:, :], ACT.Copy).then_inc(lt_copied, 1)

        PR = [sb(f"PR{k}", [P, GH, NQ]) for k in range(2)]
        OS = [sb(f"OS{k}", [P, NQ]) for k in range(QC)]
        ST = [psum(f"ST{k}", [P, 2, NQ]) for k in range(2)]
        SM = [psum(f"SM{k}", [P, NQ]) for k in range(2)]
        OB = psum("OB", [P, NQ])
        misc = psum("misc", [P, NQ])

        misc_ready = sem("misc_ready")
        misc_free = sem("misc_free")
        part1 = sem("part1")
        kv_copied = sem("kv_copied")
        resid = sem("resid")
        part2 = sem("part2")
        part3 = sem("part3")
        k_in = sem("k_in")
        q_in = [sem(f"q_in{g}") for g in range(NG)]
        m_in = [sem(f"m_in{g}") for g in range(NG)]
        v_next = sem("v_next")
        kv_now = sem("kv_now")
        sm_ready = sem("sm_ready")
        sm_done = sem("sm_done")
        m_step = sem("m_step")
        mt_ready = sem("mt_ready")
        st_ready = sem("st_ready")
        exp_done = sem("exp_done")
        masked = sem("masked")
        pv_done = sem("pv_done")
        o_copied = sem("o_copied")
        o_step = sem("o_step")
        NMS = 5

        block = ctx.enter_context(nc.Block())

        def piece_no(b, name):
            return b * len(PIECES) + PIECES.index(name)

        def is_kv(name):
            return name.startswith("kv")

        def parts(name):
            c = int(name[-1])
            if is_kv(name):
                return [t[:, c * NQ:(c + 1) * NQ] for t in (K1, K2, K3)]
            return [t[:, int(name[1]), c * NQ:(c + 1) * NQ] for t in (T1, T2, T3)]

        def rows_of(name):
            return 2 * HD if is_kv(name) else P

        def parts_sent(eng, bn, name):
            if is_kv(name):
                eng.wait_ge(k_in, 16 * len(QPART) * bn)
            else:
                for g in (2 * int(name[1]), 2 * int(name[1]) + 1):
                    eng.wait_ge(q_in[g], 16 * GH * len(QPART) * bn)

        def loops(eng, body):
            with eng.Fori(0, B - 1) as b:
                for g in range(NG):
                    body(b, g, True)
            for g in range(NG):
                body(B - 1, g, False)

        @block.tensor
        def _(pe):
            def misc_use(k):
                pe.wait_ge(misc_free, k)

            def piece(bn, name, k):
                misc_use(k)
                c = int(name[-1])
                alone(pe, spare)
                w = Wkv[:, :] if is_kv(name) else Wq[:, int(name[1]) * P:(int(name[1]) + 1) * P]
                pe.matmul(misc[0:rows_of(name), :], w, LT[:, ds(bn * T + c * NQ, NQ)], start=True, stop=True)\
                  .then_inc(misc_ready, 1)

            def values(bn, k):
                misc_use(k)
                pe.wait_ge(kv_copied, 2 * (bn + 1))
                alone(pe, spare)
                for j in range(TB):
                    last = pe.transpose(misc[:, j * 2 * HD:(j + 1) * 2 * HD], KV[:, j * P:(j + 1) * P],
                                        ident[0:2 * HD, 0:2 * HD])
                last.then_inc(misc_ready, 1)

            def neg_max(r, k):
                misc_use(k)
                pe.wait_ge(m_step, NMS * (r + 1))
                pe.transpose(misc[0:3 * GH * TB, 0:P // 2].bitcast(BF16), NMX[:, :, :], identb[:, :])\
                  .then_inc(misc_ready, 1)

            def maxes(r, g, key, n):
                h, (i, c, w, _) = n // len(MAXES), MAXES[n % len(MAXES)]
                if n >= 2 or not isinstance(r, int) or r:
                    pe.wait_ge(sm_done, NM * r + n - 1)
                pe.matmul(SM[n % 2][:, 0:w], Q[0:NR, g * GH + h, i * P:(i + 1) * P],
                          key[0:NR, c * NQ:c * NQ + w], start=True, stop=True).then_inc(sm_ready, 1)

            def out_t(n, c, k):
                misc_use(k)
                pe.wait_ge(o_copied, QC * n + c + 1)
                for t in range(NQ // P):
                    last = pe.transpose(misc[:, t * P:(t + 1) * P], OS[c][:, t * P:(t + 1) * P], ident[:, :])
                last.then_inc(misc_ready, 1)

            def pv(n, s):
                c, j, off = STEPS[s]
                pe.wait_ge(exp_done, 2 * (len(STEPS) * n + s + 1))
                if s in DIAG:
                    pe.wait_ge(masked, len(DIAG) * n + DIAG.index(s) + 1)
                if s == C0 + 1:
                    pe.wait_ge(o_copied, QC * n + 1)
                for h in range(GH):
                    last = pe.matmul(OB[32 * h:32 * h + 32, off:NQ], VC[:, j, :], PR[s % 2][:, h, off:NQ],
                                     start=j == 0, stop=s in (C0, LAST))
                last.then_inc(pv_done, 1)

            def group(b, g, more):
                n = b * NG + g
                after = g + 2
                bm, gm, key = (b, after, KC) if after < NG else (b + 1, after - NG, KN)
                take = after < NG or more
                pe.wait_ge(q_in[g], 16 * GH * len(QPART) * (b + 1))
                if take:
                    pe.wait_ge(q_in[gm], 16 * GH * len(QPART) * (bm + 1))
                    pe.wait_ge(k_in, 16 * len(QPART) * (bm + 1))
                if g == 0:
                    pe.wait_ge(kv_now, 2 * (b + 1))
                pe.wait_ge(m_in[g], 3 * 16 * (b + 1))
                done = 0
                for s, (c, j, off) in enumerate(STEPS):
                    for name, at in misc_events(g, more):
                        k = misc_at(b, g, name, more)
                        if at == s:
                            if name == "m":
                                neg_max(n + 1, k)
                            elif name == "o0":
                                out_t(n, 0, k)
                            elif name == "vt":
                                values(b + 1, k)
                            else:
                                piece(b + 1, name, k)
                    for u in range(GH):
                        if s and u % 2 == 0:
                            pe.wait_ge(exp_done, 2 * (len(STEPS) * n + s - 1) + u // 2 + 1)
                        mm = pe.matmul(ST[u // 2][:, u % 2, off:NQ], KC[0:KR, j * P:(j + 1) * P],
                                       Q[0:KR, g * GH + u, c * NQ + off:(c + 1) * NQ], start=True, stop=True)
                        if u % 2:
                            mm.then_inc(st_ready, 1)
                        if take and done < MAX_AT[s] - 1:
                            maxes(n + 2, gm, key, done)
                            done += 1
                    if s:
                        pv(n, s - 1)
                    while take and done < MAX_AT[s] - (3 if s == LAST else 0):
                        maxes(n + 2, gm, key, done)
                        done += 1
                pv(n, LAST)
                while take and done < NM:
                    maxes(n + 2, gm, key, done)
                    done += 1
                out_t(n, 1, misc_at(b, g, "o1", more))

            pe.wait_ge(s_id, 6)
            k = 0
            for name in MISC_FIRST:
                if name == "vt":
                    values(0, k)
                elif name != "m":
                    piece(0, name, k)
                k += 1
            pe.wait_ge(k_in, 16 * len(QPART))
            for g in range(2):
                pe.wait_ge(q_in[g], 16 * GH * len(QPART))
                for n in range(NM):
                    maxes(g, g, KN, n)
                if g == 0:
                    neg_max(0, k - 1)
            loops(pe, group)

        @block.scalar
        def _(act):
            def piece(bn, name, k):
                act.wait_ge(misc_ready, k + 1)
                if not isinstance(bn, int) or bn:
                    parts_sent(act, bn, name)
                p1, _, _ = parts(name)
                act.activation(p1, misc[0:rows_of(name), :], ACT.Copy).then_inc(part1, 1)
                if is_kv(name):
                    c = int(name[-1])
                    if not isinstance(bn, int) or bn:
                        act.wait_ge(v_next, bn)
                    act.activation(KV[:, c * NQ:(c + 1) * NQ], misc[0:2 * HD, :], ACT.Copy).then_inc(kv_copied, 1)

            def out_copy(n, c, s):
                act.wait_ge(pv_done, len(STEPS) * n + s + 1)
                act.activation(OS[c][:, :], OB[:, :], ACT.Copy).then_inc(o_copied, 1)

            def group(b, g, more):
                n = b * NG + g
                for s, (c, j, off) in enumerate(STEPS):
                    for name, at in misc_events(g, more):
                        if at == s and name in PIECES:
                            piece(b + 1, name, misc_at(b, g, name, more))
                    for u in range(2):
                        act.wait_ge(st_ready, 2 * (len(STEPS) * n + s) + u + 1)
                        if s >= 2 and u == 0:
                            act.wait_ge(pv_done, len(STEPS) * n + s - 1)
                        act.activation(PR[s % 2][:, 2 * u:2 * u + 2, off:NQ], ST[u][:, :, off:NQ], ACT.Exp,
                                       scale=SCALE).then_inc(exp_done, 1)
                    if s == C0 + 1:
                        out_copy(n, 0, C0)
                out_copy(n, 1, LAST)

            for k, name in enumerate(MISC_FIRST):
                if name in PIECES:
                    piece(0, name, k)
            loops(act, group)

        @block.vector
        def _(dve):
            def piece(bn, name, k):
                dve.wait_ge(part1, piece_no(bn, name) + 1)
                if is_kv(name):
                    dve.wait_ge(kv_copied, 2 * bn + int(name[-1]) + 1)
                if not isinstance(bn, int) or piece_no(bn, name):
                    dve.wait_ge(part3, piece_no(bn, name))
                p1, _, _ = parts(name)
                rows = rows_of(name)
                dve.tensor_tensor(R1[0:rows, :], misc[0:rows, :], p1, ALU.subtract).then_inc(resid, 1)
                dve.wait_ge(resid, piece_no(bn, name) + 1)
                dve.engine_nop().then_inc(misc_free, 1) if False else dve.sem_inc(misc_free, 1)

            def values(bn, k):
                dve.wait_ge(misc_ready, k + 1)
                if not isinstance(bn, int) or bn:
                    dve.wait_ge(kv_now, 2 * bn)
                v = misc[:, 0:TB * 2 * HD].rearrange("p (j d) -> p j d", j=TB)
                dve.tensor_copy(VN[:, :, 0:HD], v[:, :, HD:2 * HD]).then_inc(v_next, 1)
                dve.wait_ge(v_next, bn + 1)
                dve.sem_inc(misc_free, 1)

            def take_max(r, n):
                h, (i, c, w, diag) = n // len(MAXES), MAXES[n % len(MAXES)]
                dve.wait_ge(sm_ready, NM * r + n + 1)
                par = r_parity[0]
                dst = MP[par][:, c, h, i:i + 1]
                if diag:
                    if n >= 2 or not isinstance(r, int) or r:
                        dve.wait_ge(sm_done, NM * r + n - 1)
                    alone(dve, spare)
                    op = dve.tensor_tensor_reduce(junk[:, n % 2, 0:w], SM[n % 2][:, 0:w], causal[:, NQ - w:NQ], 1.0, LOWEST,
                                                  ALU.add, ALU.max, dst)
                else:
                    op = dve.tensor_reduce(dst, SM[n % 2][:, 0:w], AX, ALU.max)
                op.then_inc(sm_done, 1)

            r_parity = [0]

            def neg_max(r, par):
                mp = MP[par]
                dve.wait_ge(sm_done, NM * (r + 1))
                if not isinstance(r, int) or r:
                    dve.wait_ge(mt_ready, r)
                m0, m1 = (mp[:, c, :, :].rearrange("p h i -> p (h i)") for c in range(2))
                dve.tensor_tensor(mx[:, :], m0, m1, ALU.max).then_inc(m_step, 1)
                dve.wait_ge(m_step, NMS * r + 1)
                dve.tensor_scalar(NMX[:, 0, :], mx[:, :], -1.0, None, ALU.mult).then_inc(m_step, 1)
                dve.wait_ge(m_step, NMS * r + 2)
                dve.scalar_tensor_tensor(out=mr[:, :], in0=mx[:, :], scalar=-1.0, in1=NMX[:, 0, :],
                                         op0=ALU.mult, op1=ALU.subtract).then_inc(m_step, 1)
                dve.wait_ge(m_step, NMS * r + 3)
                dve.tensor_copy(NMX[:, 1, :], mr[:, :]).then_inc(m_step, 1)
                dve.wait_ge(m_step, NMS * r + 4)
                dve.tensor_tensor(NMX[:, 2, :], mr[:, :], NMX[:, 1, :], ALU.subtract).then_inc(m_step, 1)

            def max_rows(r, k, g):
                dve.wait_ge(misc_ready, k + 1)
                dve.tensor_copy(MT[:, :], misc[0:3 * GH * TB, 0:P // 2].bitcast(BF16)).then_inc(mt_ready, 1)
                dve.wait_ge(mt_ready, r + 1)
                dve.sem_inc(misc_free, 1)

            def out_norm(b, g, c, k):
                n = b * NG + g
                dve.wait_ge(misc_ready, k + 1)
                o = misc[:, :].rearrange("p (t h d) -> p t h d", t=NQ // P, h=GH)
                dve.reciprocal(rden[:, :, :], o[:, :, :, HD]).then_inc(o_step, 1)
                dve.wait_ge(o_step, 2 * (QC * n + c) + 1)
                y = Y[:, ds((b * TB + c * (NQ // P)) * D + g * GH * HD, (NQ // P - 1) * D + GH * HD)]
                y = Y[:, ds((b * TB + c * (NQ // P)) * D, (NQ // P) * D)]\
                    .rearrange("p (t h d) -> p t h d", t=NQ // P, d=HD)[:, :, g * GH:(g + 1) * GH, :]
                rb = rden[:, :, :].rearrange("p t (h u) -> p t h u", u=1).broadcast_to([P, NQ // P, GH, HD])
                dve.tensor_tensor(y, o[:, :, :, 0:HD], rb, ALU.mult).then_inc(o_step, 1)
                dve.wait_ge(o_step, 2 * (QC * n + c) + 2)
                dve.sem_inc(misc_free, 1)

            def r_batch(r, g):
                return r

            def keys_now(b):
                dve.wait_ge(k_in, 16 * len(QPART) * (b + 1))
                dve.wait_ge(v_next, b + 1)
                dve.tensor_copy(KC[0:KR, :], KN[0:KR, :]).then_inc(kv_now, 1)
                dve.tensor_copy(VC[:, :, :], VN[:, :, :]).then_inc(kv_now, 1)

            def group(b, g, more):
                n = b * NG + g
                take = g + 2 < NG or more
                if g == 0:
                    keys_now(b)
                done = 0
                for s in range(len(STEPS)):
                    for name, at in misc_events(g, more):
                        k = misc_at(b, g, name, more)
                        if name == "m" and s == 0:
                            neg_max(n + 1, (g + 1) % 2)
                        if name == "m" and s == at + 1:
                            dve.wait_ge(misc_ready, k + 1)
                            dve.wait_ge(m_in[g], 3 * 16 * (b + 1))
                            dve.tensor_copy(MT[:, :], misc[0:3 * GH * TB, 0:P // 2].bitcast(BF16)).then_inc(mt_ready, 1)
                            dve.wait_ge(mt_ready, n + 2)
                            dve.sem_inc(misc_free, 1)
                        if at == s and name == "o0":
                            out_norm(b, g, 0, k)
                        if at == s and name == "vt":
                            values(b + 1, k)
                        if at == s and name in PIECES:
                            piece(b + 1, name, k)
                    r_parity[0] = g % 2
                    last = NM if s == LAST else MAX_AT[s]
                    while take and done < last:
                        take_max(n + 2, done)
                        done += 1
                out_norm(b, g, 1, misc_at(b, g, "o1", more))

            dve.wait_ge(ones_set, 4)
            for k, name in enumerate(MISC_FIRST):
                if name == "vt":
                    values(0, k)
                elif name != "m":
                    piece(0, name, k)
            for g in range(2):
                r_parity[0] = g
                for n in range(NM):
                    take_max(g, n)
                if g == 0:
                    neg_max(0, 0)
                    max_rows(0, len(MISC_FIRST) - 1, 0)
            loops(dve, group)

        @block.gpsimd
        def _(pool):
            def piece(bn, name):
                k = piece_no(bn, name)
                rows = rows_of(name)
                _, p2, p3 = parts(name)
                pool.wait_ge(resid, k + 1)
                if not isinstance(bn, int) or bn:
                    parts_sent(pool, bn, name)
                alone(pool, spare)
                pool.tensor_copy(p2, R1[0:rows, :]).then_inc(part2, 1)
                pool.wait_ge(part2, k + 1)
                pool.tensor_tensor(p3, R1[0:rows, :], p2, ALU.subtract).then_inc(part3, 1)

            def group(b, g, more):
                n = b * NG + g
                for s, (c, j, off) in enumerate(STEPS):
                    for name, at in misc_events(g, more):
                        if at == s and name in PIECES:
                            piece(b + 1, name)
                    if s in DIAG:
                        pool.wait_ge(exp_done, 2 * (len(STEPS) * n + s + 1))
                        alone(pool, spare)
                        p = PR[s % 2][:, :, off:off + P]
                        pool.affine_select(out=p, in_=p, compare_op=ALU.is_ge, fill=0.0, base=0,
                                           pattern=[[0, GH], [1, P]], channel_multiplier=-1).then_inc(masked, 1)

            for name in PIECES:
                piece(0, name)
            loops(pool, group)

        @block.sync
        def _(sp):
            def send_keys(b):
                sp.wait_ge(ones_set, 4)
                sp.wait_ge(part3, piece_no(b, "kv1") + 1)
                for r, part in enumerate(KPART):
                    sp.dma_start(KN[r * HD:(r + 1) * HD, :], (K1, K2, K3)[part][0:HD, :]).then_inc(k_in, 16)

            def send_queries(b, g):
                half, quarter = divmod(g, 2)
                sp.wait_ge(part3, piece_no(b, f"q{half}1") + 1)
                for h in range(GH):
                    row = (quarter * GH + h) * HD
                    for r, part in enumerate(QPART):
                        sp.dma_start(Q[r * HD:(r + 1) * HD, g * GH + h, :],
                                     (T1, T2, T3)[part][row:row + HD, half, :]).then_inc(q_in[g], 16)

            def send_max(r, g):
                sp.wait_ge(mt_ready, r + 1)
                for a in range(3):
                    sp.dma_start(Q[NR + a:NR + a + 1, g * GH:(g + 1) * GH, :].rearrange("u h (i q) -> u (h i) q", i=TB),
                                 MT[a * GH * TB:(a + 1) * GH * TB, :]).then_inc(m_in[g], 16)

            def group(b, g, more):
                n = b * NG + g
                if g < NG - 1:
                    send_max(n + 1, g + 1)
                elif more:
                    send_max(n + 1, 0)
                if more:
                    if g == 1:
                        sp.wait_ge(kv_now, 2 * (b + 1))
                        alone(sp, spare)
                        send_keys(b + 1)
                    sp.wait_ge(pv_done, len(STEPS) * (n + 1))
                    alone(sp, spare)
                    send_queries(b + 1, g)

            for g in range(2):
                send_queries(0, g)
                if g == 0:
                    send_keys(0)
            for e in range(E):
                sp.dma_start(W1s[:, :, e * F:(e + 1) * F], w1_v[e]).then_inc(w1_in, 16)
            for g in range(2, NG):
                send_queries(0, g)
            send_max(0, 0)
            loops(sp, group)


def route(nc, started, spare, x, Wc_proj, centroids, ident, eps, Y, W2s, w2_v, w2_in, x1_dram, IDX, EX):
    with ExitStack() as ctx:
        sb = lambda name, shape, dt=F32: ctx.enter_context(nc.sbuf_tensor(name, shape, dt))
        sem = lambda name: ctx.enter_context(nc.semaphore(name))
        psum = lambda name, shape, dt=F32: ctx.enter_context(nc.psum_tensor(name, shape, dt))
        QT = 4
        NQD = NT // QT
        CT = sb("CT", [P, DC, E])
        ef = sb("ef", [P, NT])
        with ExitStack() as c2:
            sb2 = lambda name, shape, dt=F32: c2.enter_context(nc.sbuf_tensor(name, shape, dt))
            sem2 = lambda name: c2.enter_context(nc.semaphore(name))
            ps2 = lambda name, shape, dt=F32: c2.enter_context(nc.psum_tensor(name, shape, dt))
            YS = sb2("YS", [P, QT, D])
            YT = sb2("YT", [P, DC, QT * P])
            Wp = sb2("Wp", [P, DC, D])
            Cn = sb2("Cn", [E, D])
            X = [sb2(f"XQ{k}", [P, QT, D]) for k in range(2)]
            XF = sb2("XF", [P, QT, D])
            XFT = sb2("XFT", [P, DC, QT * P])
            st = sb2("st2", [P, QT, 6])
            mv = sb2("mv2", [P, QT, 2])
            sd = sb2("sd2", [P, QT])
            rs = sb2("rs2", [P, QT])
            nt = [sb2(f"nt{k}", [P, QT]) for k in range(3)]
            m8 = sb2("m8", [P, QT, 8])
            i8 = sb2("i8", [P, QT, 8], U32)
            lg = sb2("lg", [P, QT, E])
            ytp = [ps2(f"ytp{c}", [P, QT * P]) for c in range(DC)]
            pj = ps2("pj", [P, QT, D])
            xtp = [ps2(f"xftp{c}", [P, QT * P]) for c in range(DC)]
            lgp = ps2("lgp", [P, QT * E])
            w_in = sem2("wp_in")
            c_ready = sem2("c_ready")
            c_copied = sem2("c_copied")
            x_in = [sem2(f"xq_in{k}") for k in range(2)]
            ys_ready = sem2("ys_ready")
            yt_ready = sem2("yt_ready")
            yt_copied = sem2("yt_copied")
            pj_ready = sem2("pj_ready")
            ln = sem2("ln")
            sd_ready = sem2("sd2_ready")
            x1_out = [sem2(f"x1_out{k}") for k in range(2)]
            xf_ready = sem2("xf_ready")
            xft_ready = sem2("xft_ready")
            xft_copied = sem2("xft_copied")
            lg_ready = sem2("lg_ready")
            top = sem2("top")
            xv = x.rearrange("b (i p) d -> p (b i) d", p=P)
            x1v = x1_dram.rearrange("(i p) d -> p i d", p=P)
            HALF = 3 * QT + 5
            LN = 2 * HALF + 1
            TOP = 2 * QT + 2
            X1 = HALF + 1
            block = c2.enter_context(nc.Block())

            @block.sync
            def _(sp):
                sp.dma_start(Wp[:, :, :], Wc_proj.rearrange("(c p) n -> p c n", p=P)).then_inc(w_in, 16)
                sp.dma_start(Cn[:, :], centroids[:, :]).then_inc(w_in, 16)
                for k in range(2):
                    sp.dma_start(X[k][:, :, :], xv[:, k * QT:(k + 1) * QT, :]).then_inc(x_in[k], 16)

                for t in range(NQD):
                    k = t % 2
                    sp.wait_ge(ln, LN * t + X1)
                    sp.dma_start(x1v[:, t * QT:(t + 1) * QT, :], X[k][:, :, :]).then_inc(x1_out[k], 16)
                    if t + 2 < NQD:
                        sp.wait_ge(x1_out[k], 16 * (t // 2 + 1))
                        sp.wait_ge(ln, LN * (t + 1))
                        sp.dma_start(X[k][:, :, :], xv[:, (t + 2) * QT:(t + 3) * QT, :]).then_inc(x_in[k], 16)
                for k in range(2):
                    sp.wait_ge(x1_out[k], 16 * (NQD // 2))
                for e in range(E):
                    sp.dma_start(W2s[:, e, :].rearrange("p (c d) -> p c d", c=FC), w2_v[e]).then_inc(w2_in, 16)

            @block.gpsimd
            def _(pool):
                with pool.Fori(0, NQD) as t:
                    pool.tensor_copy(YS[:, :, :].rearrange("p t d -> p (t d)"), Y[:, ds(t * (QT * D), QT * D)])\
                        .then_inc(ys_ready, 1)
                    pool.wait_ge(yt_ready, t + 1)
                    alone(pool, spare)

            @block.tensor
            def _(pe):
                pe.sem_inc(lg_ready, 1)
                pe.wait_ge(w_in, 32)
                for c in range(DC):
                    last = pe.transpose(lgp[:, c * E:(c + 1) * E], Cn[:, c * P:(c + 1) * P], ident[0:E, 0:E])
                last.then_inc(c_ready, 1)

                def front(t):
                    pe.wait_ge(ys_ready, t + 1)
                    for c in range(DC):
                        for i in range(QT):
                            last = pe.transpose(ytp[c][:, i * P:(i + 1) * P], YS[:, i, c * P:(c + 1) * P], ident[:, :])
                    last.then_inc(yt_ready, 1)
                    pe.wait_ge(yt_copied, DC * (t + 1))
                    past(pe, ln, LN * t)
                    for i in range(QT):
                        for c in range(DC):
                            mm = pe.matmul(pj[:, i, :], YT[:, c, i * P:(i + 1) * P], Wp[:, c, :],
                                           start=c == 0, stop=c == DC - 1)
                    mm.then_inc(pj_ready, 1)

                def back(t):
                    pe.wait_ge(ln, LN * (t + 1))
                    for c in range(DC):
                        for i in range(QT):
                            last = pe.transpose(xtp[c][:, i * P:(i + 1) * P], XF[:, i, c * P:(c + 1) * P], ident[:, :])
                    last.then_inc(xft_ready, 1)
                    pe.wait_ge(xft_copied, DC * (t + 1))
                    pe.wait_ge(top, TOP * t + 1)
                    pe.wait_ge(c_copied, 1)
                    for i in range(QT):
                        for c in range(DC):
                            mm = pe.matmul(lgp[:, i * E:(i + 1) * E], XFT[:, c, i * P:(i + 1) * P], CT[:, c, :],
                                           start=c == 0, stop=c == DC - 1)
                    mm.then_inc(lg_ready, 1)

                front(0)
                with pe.Fori(0, NQD - 1) as t:
                    front(t + 1)
                    back(t)
                back(NQD - 1)

            @block.scalar
            def _(act):
                def yt(t):
                    act.wait_ge(yt_ready, t + 1)
                    past(act, pj_ready, t)
                    for c in range(DC):
                        act.activation(YT[:, c, :], ytp[c][:, :], ACT.Copy).then_inc(yt_copied, 1)

                def xft(t):
                    act.wait_ge(xft_ready, t + 1)
                    act.wait_ge(lg_ready, t + 1)
                    for c in range(DC):
                        act.activation(XFT[:, c, :], xtp[c][:, :], ACT.Copy).then_inc(xft_copied, 1)

                def roots(t):
                    for k in range(2):
                        act.wait_ge(ln, LN * t + k * (HALF + 1) + 2 * QT)
                        act.activation(sd[:, :], mv[:, :, 1], ACT.Sqrt, bias=eps[:, :]).then_inc(sd_ready, 1)

                yt(0)
                roots(0)
                with act.Fori(0, NQD - 1) as t:
                    yt(t + 1)
                    xft(t)
                    roots(t + 1)
                xft(NQD - 1)

            @block.vector
            def _(dve):
                dve.sem_inc(top, 1)
                dve.wait_ge(c_ready, 1)
                dve.tensor_copy(CT[:, :, :].rearrange("p c e -> p (c e)"), lgp[:, 0:DC * E]).then_inc(c_copied, 1)

                def norm(base, k2, src, dst):
                    for i in range(QT):
                        dve.bn_stats(st[:, i, :], src[:, i, :]).then_inc(ln, 1)
                    dve.wait_ge(ln, base + QT)
                    alone(dve, spare)
                    for i in range(QT):
                        dve.bn_aggr(mv[:, i, :], st[:, i, :]).then_inc(ln, 1)
                    dve.wait_ge(ln, base + 2 * QT)
                    dve.wait_ge(sd_ready, k2)
                    n = base + 2 * QT
                    dve.reciprocal(rs[:, :], sd[:, :]).then_inc(ln, 1)
                    dve.wait_ge(ln, n + 1)
                    dve.scalar_tensor_tensor(out=nt[0][:, :], in0=mv[:, :, 1], scalar=EPS, in1=rs[:, :],
                                             op0=ALU.add, op1=ALU.mult).then_inc(ln, 1)
                    dve.wait_ge(ln, n + 2)
                    dve.tensor_tensor(nt[1][:, :], nt[0][:, :], rs[:, :], ALU.mult).then_inc(ln, 1)
                    dve.wait_ge(ln, n + 3)
                    dve.tensor_scalar(nt[2][:, :], nt[1][:, :], -0.5, 1.5, ALU.mult, ALU.add).then_inc(ln, 1)
                    dve.wait_ge(ln, n + 4)
                    dve.tensor_tensor(nt[0][:, :], nt[2][:, :], rs[:, :], ALU.mult).then_inc(ln, 1)
                    dve.wait_ge(ln, n + 5)
                    for i in range(QT):
                        dve.tensor_scalar(dst[:, i, :], src[:, i, :], mv[:, i, 0:1], nt[0][:, i:i + 1],
                                          ALU.subtract, ALU.mult).then_inc(ln, 1)

                def norms(t, k, seen):
                    dve.wait_ge(pj_ready, t + 1)
                    past(dve, xft_ready, t)
                    past(dve, ln, LN * t)
                    norm(LN * t, 2 * t + 1, pj, XF)
                    dve.wait_ge(ln, LN * t + HALF)
                    dve.wait_ge(x_in[k], seen)
                    dve.tensor_tensor(X[k][:, :, :], X[k][:, :, :], XF[:, :, :], ALU.add).then_inc(ln, 1)
                    dve.wait_ge(ln, LN * t + X1)
                    norm(LN * t + X1, 2 * t + 2, X[k], XF)

                def argmax(t):
                    base = TOP * t + 1
                    dve.wait_ge(lg_ready, t + 2)
                    dve.tensor_copy(lg[:, :, :].rearrange("p t e -> p (t e)"), lgp[:, :]).then_inc(top, 1)
                    dve.wait_ge(top, base + 1)
                    alone(dve, spare)
                    for i in range(QT):
                        dve.max(m8[:, i, :], lg[:, i, :]).then_inc(top, 1)
                    for i in range(QT):
                        dve.wait_ge(top, base + 1 + QT)
                        alone(dve, spare)
                        dve.max_index(i8[:, i, :], m8[:, i, :], lg[:, i, :]).then_inc(top, 1)
                    dve.wait_ge(top, base + 1 + 2 * QT)
                    dve.tensor_copy(ef[:, ds(t * QT, QT)], i8[:, :, 0]).then_inc(top, 1)

                norms(0, 0, 16)
                with dve.Fori(0, NQD // 2 - 1) as t2:
                    norms(2 * t2 + 1, 1, 16 * (t2 + 1))
                    argmax(2 * t2)
                    norms(2 * t2 + 2, 0, 16 * (t2 + 2))
                    argmax(2 * t2 + 1)
                norms(NQD - 1, 1, 16 * (NQD // 2))
                argmax(NQD - 2)
                argmax(NQD - 1)

        with ExitStack() as c3:
            sb3 = lambda name, shape, dt=F32: c3.enter_context(nc.sbuf_tensor(name, shape, dt))
            sem3 = lambda name: c3.enter_context(nc.semaphore(name))
            ps3 = lambda name, shape, dt=F32: c3.enter_context(nc.psum_tensor(name, shape, dt))
            below = sb3("below", [P, P], BF16)
            ones = sb3("ones", [P, P], BF16)
            ints = sb3("ints", [P, P], I32)
            intp = sb3("intp", [P, 1], I32)
            iota = sb3("iota", [P, P])
            part = sb3("part", [P, 1])
            OH = sb3("OH", [P, NT, E], BF16)
            keep = sb3("keep", [P, E, NT])
            cum = sb3("cum", [P, E * NT])
            cnt = sb3("cnt", [P, E, NT])
            slot = sb3("slot", [P, E, NT])
            full = sb3("full", [P, E, NT])
            tiles = sb3("tiles", [P, E])
            tend = sb3("tend", [P, E])
            tbeg = sb3("tbeg", [P, E])
            dest = sb3("dest", [P, NT])
            di = sb3("di", [P, NT], I32)
            ai = sb3("ai", [P, NT], I32)
            bi = sb3("bi", [P, NT], I32)
            af = sb3("af", [P, NT])
            bf = sb3("bf", [P, NT])
            OB = sb3("OBs", [P, NT, P], BF16)
            OA = sb3("OAs", [P, NT, 3 * NS], BF16)
            sl = sb3("sl", [P, 3 * NS])
            tok = sb3("tok", [P, NS])
            gap = sb3("gap", [P, NS])
            exc = sb3("exc", [P, NS, E - 1])
            exf = sb3("exf", [P, NS])
            pfx = ps3("pfx", [P, E * NT])
            tot = ps3("tot", [P, E * NT])
            slp = ps3("slp", [P, 3 * NS])
            made = sem3("made")
            rt = sem3("rt")
            oh_ready = sem3("oh_ready")
            counts = sem3("counts")
            oab_ready = sem3("oab_ready")
            sl_ready = sem3("sl_ready")
            block = c3.enter_context(nc.Block())

            @block.gpsimd
            def _(pool):
                pool.memset(below[:, :], 1.0).then_inc(made, 1)
                pool.memset(ones[:, :], 1.0).then_inc(made, 1)
                pool.memset(keep[:, :, :], 1.0).then_inc(made, 1)
                pool.iota(ints[:, :], pattern=[[1, P]], base=0, channel_multiplier=0).then_inc(made, 1)
                pool.iota(intp[:, :], pattern=[[0, 1]], base=0, channel_multiplier=1).then_inc(made, 1)
                pool.wait_ge(made, 5)
                pool.affine_select(out=below[:, :], in_=below[:, :], compare_op=ALU.is_gt, fill=0.0, base=0,
                                   pattern=[[1, P]], channel_multiplier=-1).then_inc(made, 1)
                pool.memset(keep[:, :, 0:1], 0.0).then_inc(made, 1)

            @block.tensor
            def _(pe):
                pe.wait_ge(made, 7)
                pe.wait_ge(oh_ready, 1)
                oh = OH[:, :, :].rearrange("p t e -> p e t")
                pe.matmul(pfx[:, :], below[:, :], oh, start=True, stop=True).then_inc(counts, 1)
                pe.matmul(tot[:, :], ones[:, :], oh, start=True, stop=True).then_inc(counts, 1)
                pe.wait_ge(oab_ready, 4)
                for t in range(NT):
                    mm = pe.matmul(slp[:, :], OB[:, t, :], OA[:, t, :], start=t == 0, stop=t == NT - 1)
                mm.then_inc(sl_ready, 1)

            @block.vector
            def _(dve):
                n = [0]

                def then(ins):
                    n[0] += 1
                    ins.then_inc(rt, 1)
                    dve.wait_ge(rt, n[0])

                def over(ap, shape, axis):
                    return ap.unsqueeze(axis).broadcast_to(shape)

                dve.wait_ge(made, 7)
                dve.tensor_copy(iota[:, :], ints[:, :]).then_inc(rt, 1)
                dve.tensor_copy(part[:, :], intp[:, :]).then_inc(rt, 1)
                n[0] = 2
                dve.wait_ge(rt, n[0])
                dve.tensor_tensor(OH[:, :, :], over(ef[:, :], [P, NT, E], 2), over(iota[:, 0:E], [P, NT, E], 1),
                                  ALU.is_equal).then_inc(oh_ready, 1)
                dve.wait_ge(oh_ready, 1)
                dve.wait_ge(counts, 2)
                then(dve.tensor_tensor_scan(cum[:, :], keep[:, :, :].rearrange("p e t -> p (e t)"), tot[:, :], 0.0,
                                            ALU.mult, ALU.add))
                cv = cum[:, :].rearrange("p (e t) -> p e t", e=E)
                then(dve.tensor_tensor(cnt[:, :, :], cv, tot[:, :].rearrange("p (e t) -> p e t", e=E), ALU.subtract))
                then(dve.tensor_tensor(slot[:, :, :], cnt[:, :, :], pfx[:, :].rearrange("p (e t) -> p e t", e=E),
                                       ALU.add))
                then(dve.tensor_scalar(dest[:, :], iota[:, 0:NT], float(P), None, ALU.mult))
                then(dve.tensor_tensor(full[:, :, :], cv[:, :, NT - 1:NT].broadcast_to([P, E, NT]),
                                       over(dest[:, :], [P, E, NT], 1), ALU.is_gt))
                then(dve.tensor_reduce(tiles[:, :], full[:, :, :], AX, ALU.add))
                then(dve.tensor_tensor_scan(tend[:, :], ones[:, 0:E], tiles[:, :], 0.0, ALU.mult, ALU.add))
                then(dve.tensor_tensor(tbeg[:, :], tend[:, :], tiles[:, :], ALU.subtract))
                then(dve.scalar_tensor_tensor(out=cnt[:, :, :], in0=over(tbeg[:, :], [P, E, NT], 2), scalar=float(P),
                                              in1=slot[:, :, :], op0=ALU.mult, op1=ALU.add))
                then(dve.tensor_tensor(full[:, :, :], cnt[:, :, :], OH[:, :, :].rearrange("p t e -> p e t"),
                                       ALU.mult))
                then(dve.tensor_reduce(dest[:, :], full[:, :, :].rearrange("p e t -> p t e"), AX, ALU.add))
                then(dve.tensor_copy(di[:, :], dest[:, :]))
                then(dve.tensor_single_scalar(ai[:, :], di[:, :], 7, ALU.arith_shift_right))
                then(dve.tensor_single_scalar(bi[:, :], di[:, :], P - 1, ALU.bitwise_and))
                then(dve.tensor_copy(af[:, :], ai[:, :]))
                then(dve.tensor_copy(bf[:, :], bi[:, :]))
                dve.tensor_tensor(OB[:, :, :], over(bf[:, :], [P, NT, P], 2), over(iota[:, :], [P, NT, P], 1),
                                  ALU.is_equal).then_inc(oab_ready, 1)
                dve.tensor_tensor(OA[:, :, 0:NS], over(af[:, :], [P, NT, NS], 2), over(iota[:, 0:NS], [P, NT, NS], 1),
                                  ALU.is_equal).then_inc(oab_ready, 1)
                dve.wait_ge(oab_ready, 2)
                dve.tensor_scalar(OA[:, :, NS:2 * NS], OA[:, :, 0:NS], part[:, 0:1], None, ALU.mult)\
                   .then_inc(oab_ready, 1)
                dve.tensor_tensor(OA[:, :, 2 * NS:3 * NS], OA[:, :, 0:NS], over(iota[:, 0:NT], [P, NT, NS], 2),
                                  ALU.mult).then_inc(oab_ready, 1)
                then(dve.tensor_tensor(exc[:, :, :], over(iota[:, 0:NS], [P, NS, E - 1], 2),
                                       over(tend[:, 0:E - 1], [P, NS, E - 1], 1), ALU.is_ge))
                then(dve.tensor_reduce(exf[:, :], exc[:, :, :], AX, ALU.add))
                then(dve.tensor_copy(EX[:, :], exf[:, :]))
                dve.wait_ge(sl_ready, 1)
                then(dve.tensor_copy(sl[:, :], slp[:, :]))
                then(dve.scalar_tensor_tensor(out=tok[:, :], in0=sl[:, 2 * NS:3 * NS], scalar=float(P),
                                              in1=sl[:, NS:2 * NS], op0=ALU.mult, op1=ALU.add))
                then(dve.tensor_scalar(gap[:, :], sl[:, 0:NS], -float(NTOK), float(NTOK), ALU.mult, ALU.add))
                then(dve.tensor_tensor(exf[:, :], tok[:, :], gap[:, :], ALU.add))
                then(dve.tensor_copy(IDX[:, :], exf[:, :]))


def experts(nc, started, spare, ln_g, ln_b, b1, b2, ident, eps, W1s, w1_in, W2s, w2_in, x1_dram, IDX, EX, out):
    with ExitStack() as ctx:
        sb = lambda name, shape, dt=F32: ctx.enter_context(nc.sbuf_tensor(name, shape, dt))
        sem = lambda name: ctx.enter_context(nc.semaphore(name))
        psum = lambda name, shape, dt=F32: ctx.enter_context(nc.psum_tensor(name, shape, dt))
        RING = 6
        FH = F // NQ
        NPAR = 2 * DC + FC
        PT = sb("PT", [P, NPAR, E])
        b2s = sb("b2s", [P, E * D])
        XG = sb("XG", [P, D])
        X1 = sb("X1r", [P, RING * D])
        XF = sb("XFr", [P, RING * D])
        XN = sb("XNf", [P, D])
        XNT = sb("XNT", [P, DC, P])
        HS = sb("HS", [P, F])
        HT = sb("HT", [P, FC, P])
        z0 = sb("z0", [P, D])
        z1 = sb("z1", [P, D])
        on = sb("on", [P, D])
        O = sb("O", [P, D])
        ig = sb("ig", [P, 1], I32)
        io = sb("io", [P, 1], I32)
        st, st2 = sb("stf", [P, 6]), sb("stb", [P, 6])
        mv, mv2 = sb("mvf", [P, 2]), sb("mvb", [P, 2])
        sd, sd2 = sb("sdf", [P, 1]), sb("sdb", [P, 1])
        rs, rs2 = sb("rsf", [P, 1]), sb("rsb", [P, 1])
        xp = psum("xp", [P, DC * P])
        hp = psum("hp", [P, F])
        tp = [psum(f"tp{k}", [P, FC // 2, P]) for k in range(2)]
        yp = psum("yp", [P, D])
        par_in = sem("par_in")
        par_t = sem("par_t")
        par_ready = sem("par_ready")
        zeroed = sem("zeroed")
        ig_set = sem("ig_set")
        gathered = sem("gathered")
        x1_kept = sem("x1_kept")
        fr = sem("fr")
        fsd = sem("fsd")
        xt_ready = sem("xt2_ready")
        xnt_ready = sem("xnt_ready")
        h_ready = sem("h_ready")
        hs_ready = sem("hs_ready")
        ht_ready = sem("ht_ready")
        relu_a = sem("relu_a")
        relu_v = sem("relu_v")
        y_ready = sem("y_ready")
        bk = sem("bk")
        bsd = sem("bsd")
        io_set = sem("io_set")
        scattered = sem("scattered")
        FR, BK = 8, 7
        block = ctx.enter_context(nc.Block())

        def expert(eng, t):
            return eng.value_load(EX[0:1, ds(t, 1)], min_val=0, max_val=E - 1)

        def ring(buf, t):
            return buf[:, ds((t % RING) * D, D)]

        @block.sync
        def _(sp):
            sp.dma_start(HT[0:E, 0:DC, :].rearrange("e c p -> e (c p)"), ln_g[:, :]).then_inc(par_in, 16)
            sp.dma_start(HT[0:E, DC:2 * DC, :].rearrange("e c p -> e (c p)"), ln_b[:, :]).then_inc(par_in, 16)
            sp.dma_start(HS[0:E, :], b1[:, :]).then_inc(par_in, 16)
            sp.dma_start(b2s[:, :], b2.rearrange("(u e) d -> u (e d)", u=1).broadcast_to([P, E * D])).then_inc(par_in, 16)

        @block.gpsimd
        def _(pool):
            pool.memset(XG[:, :], 0.0).then_inc(zeroed, 1)
            pool.wait_ge(zeroed, 1)

            def gather(t):
                past(pool, x1_kept, t)
                alone(pool, spare)
                pool.tensor_copy(ig[:, :], IDX[:, ds(t, 1)]).then_inc(ig_set, 1)
                pool.wait_ge(ig_set, t + 1)
                alone(pool, spare)
                pool.indirect_dma_start(out=XG[:, :], out_offset=None, in_=x1_dram[:, :],
                                        in_offset=bass.IndirectOffsetOnAxis(ap=ig[:, :], axis=0),
                                        bounds_check=NTOK - 1, oob_is_err=False).then_inc(gathered, 16)

            def keep(t):
                pool.wait_ge(gathered, 16 * (t + 1))
                alone(pool, spare)
                pool.tensor_copy(ring(X1, t), XG[:, :]).then_inc(x1_kept, 1)

            def scatter(t):
                past(pool, scattered, 16 * t)
                alone(pool, spare)
                pool.tensor_copy(io[:, :], IDX[:, ds(t, 1)]).then_inc(io_set, 1)
                pool.wait_ge(io_set, t + 1)
                pool.wait_ge(bk, BK * (t + 1))
                alone(pool, spare)
                pool.indirect_dma_start(out=out.rearrange("b t d -> (b t) d"),
                                        out_offset=bass.IndirectOffsetOnAxis(ap=io[:, :], axis=0),
                                        in_=O[:, :], in_offset=None,
                                        bounds_check=NTOK - 1, oob_is_err=False).then_inc(scattered, 16)

            gather(0)
            for t in range(RING - 1):
                keep(t)
                gather(t + 1)
            keep(RING - 1)
            gather(RING)
            scatter(0)
            with pool.Fori(1, NS - RING) as t:
                keep(t + RING - 1)
                gather(t + RING)
                scatter(t)
            keep(NS - 1)
            with pool.Fori(NS - RING, NS) as t:
                scatter(t)
            pool.wait_ge(scattered, 16 * NS)

        @block.tensor
        def _(pe):
            pe.wait_ge(par_in, 64)
            for k in range(NPAR):
                src = HT[0:E, k, :] if k < 2 * DC else HS[0:E, (k - 2 * DC) * P:(k - 2 * DC + 1) * P]
                last = pe.transpose(tp[0][:, 0, k * E:(k + 1) * E], src, ident[0:E, 0:E])
            last.then_inc(par_t, 1)
            pe.wait_ge(par_ready, 1)
            pe.wait_ge(w1_in, 16 * E)
            pe.wait_ge(w2_in, 16 * E)

            def turn_x(t):
                pe.wait_ge(fr, FR * (t + 1))
                past(pe, xnt_ready, DC * t)
                for c in range(DC):
                    last = pe.transpose(xp[:, c * P:(c + 1) * P], XN[:, c * P:(c + 1) * P], ident[:, :])
                last.then_inc(xt_ready, 1)

            def up(t):
                e = expert(pe, t)
                pe.wait_ge(xnt_ready, DC * (t + 1))
                past(pe, hs_ready, FH * t)
                for c in range(DC):
                    for k in range(FH):
                        mm = pe.matmul(hp[:, k * NQ:(k + 1) * NQ], XNT[:, c, :],
                                       W1s[:, c, ds(e * F + k * NQ, NQ)], start=c == 0, stop=c == DC - 1)
                        if c == DC - 1:
                            mm.then_inc(h_ready, 1)

            def turn_h(t):
                pe.wait_ge(hs_ready, FH * (t + 1))
                for k in range(2):
                    past(pe, (relu_a, relu_v)[k], FC // 2 * t)
                    for c in range(FC // 2):
                        f = k * (FC // 2) + c
                        last = pe.transpose(tp[k][:, c, :], HS[:, f * P:(f + 1) * P], ident[:, :])
                    last.then_inc(ht_ready, 1)

            def down(t):
                e = expert(pe, t)
                if not isinstance(t, int) or t:
                    pe.wait_ge(bk, BK * (t - 1) + 1)
                for f in range(FC):
                    h = FC // 2
                    pe.wait_ge((relu_a, relu_v)[f // h], h * t + f % h + 1)
                    mm = pe.matmul(yp[:, :], HT[:, f, :], W2s[:, ds(e, 1), f * D:(f + 1) * D],
                                   start=f == 0, stop=f == FC - 1)
                mm.then_inc(y_ready, 1)

            turn_x(0)
            up(0)
            turn_x(1)

            def step(t):
                turn_h(t)
                up(t + 1)
                turn_x(t + 2)
                down(t)

            step(0)
            with pe.Fori(1, NS - 2) as t:
                step(t)
            turn_h(NS - 2)
            up(NS - 1)
            down(NS - 2)
            turn_h(NS - 1)
            down(NS - 1)

        @block.scalar
        def _(act):
            act.wait_ge(par_ready, 1)

            def roots(t):
                for k in range(2):
                    act.wait_ge(fr, FR * t + 4 * k + 2)
                    act.activation(sd[:, :], mv[:, 1:2], ACT.Sqrt, bias=eps[:, :]).then_inc(fsd, 1)

            def root(t):
                act.wait_ge(bk, BK * t + 4)
                act.activation(sd2[:, :], mv2[:, 1:2], ACT.Sqrt, bias=eps[:, :]).then_inc(bsd, 1)

            def copy_h(t):
                past(act, ht_ready, 2 * t)
                for k in range(FH):
                    act.wait_ge(h_ready, FH * t + k + 1)
                    act.activation(HS[:, k * NQ:(k + 1) * NQ], hp[:, k * NQ:(k + 1) * NQ], ACT.Copy)\
                       .then_inc(hs_ready, 1)

            def relu(t):
                e = expert(act, t)
                act.wait_ge(ht_ready, 2 * t + 1)
                past(act, y_ready, t)
                for f in range(FC // 2):
                    act.activation(HT[:, f, :], tp[0][:, f, :], ACT.Relu,
                                   bias=PT[:, 2 * DC + f, ds(e, 1)]).then_inc(relu_a, 1)

            for t in range(3):
                roots(t)
            copy_h(0)

            def step(t, first, up, front):
                relu(t)
                if not first:
                    root(t - 1)
                if up:
                    copy_h(t + 1)
                if front:
                    roots(t + 3)

            step(0, True, True, True)
            with act.Fori(1, NS - 3) as t:
                step(t, False, True, True)
            step(NS - 3, False, True, False)
            step(NS - 2, False, True, False)
            step(NS - 1, False, False, False)
            root(NS - 1)

        @block.vector
        def _(dve):
            dve.wait_ge(par_t, 1)
            dve.tensor_copy(PT[:, :, :].rearrange("p k e -> p (k e)"), tp[0][:, 0, 0:NPAR * E]).then_inc(par_ready, 1)
            dve.wait_ge(par_ready, 1)

            def norm(chain, base, root, nroot, st, mv, sd, rs, src, dst):
                alone(dve, spare)
                dve.bn_stats(st[:, :], src).then_inc(chain, 1)
                dve.wait_ge(chain, base + 1)
                alone(dve, spare)
                dve.bn_aggr(mv[:, :], st[:, :]).then_inc(chain, 1)
                dve.wait_ge(chain, base + 2)
                dve.wait_ge(root, nroot)
                dve.reciprocal(rs[:, :], sd[:, :]).then_inc(chain, 1)
                dve.wait_ge(chain, base + 3)
                dve.tensor_scalar(dst, src, mv[:, 0:1], rs[:, 0:1], ALU.subtract, ALU.mult).then_inc(chain, 1)

            def front(t):
                dve.wait_ge(x1_kept, t + 1)
                past(dve, fr, FR * t)
                norm(fr, FR * t, fsd, 2 * t + 1, st, mv, sd, rs, ring(X1, t), ring(XF, t))
                dve.wait_ge(fr, FR * t + 4)
                past(dve, xt_ready, t)
                norm(fr, FR * t + 4, fsd, 2 * t + 2, st, mv, sd, rs, ring(XF, t), XN[:, :])

            def affine(t):
                e = expert(dve, t)
                dve.wait_ge(xt_ready, t + 1)
                past(dve, h_ready, FH * t)
                for c in range(DC):
                    dve.tensor_scalar(XNT[:, c, :], xp[:, c * P:(c + 1) * P], PT[:, c, ds(e, 1)],
                                      PT[:, DC + c, ds(e, 1)], ALU.mult, ALU.add).then_inc(xnt_ready, 1)

            def relu(t):
                e = expert(dve, t)
                dve.wait_ge(ht_ready, 2 * t + 2)
                past(dve, y_ready, t)
                for f in range(FC // 2):
                    dve.tensor_scalar(HT[:, FC // 2 + f, :], tp[1][:, f, :], PT[:, 2 * DC + FC // 2 + f, ds(e, 1)],
                                      0.0, ALU.add, ALU.max).then_inc(relu_v, 1)

            def back(t):
                e = expert(dve, t)
                dve.wait_ge(y_ready, t + 1)
                past(dve, bk, BK * t)
                dve.tensor_tensor(z0[:, :], yp[:, :], b2s[:, ds(e * D, D)], ALU.add).then_inc(bk, 1)
                dve.wait_ge(bk, BK * t + 1)
                dve.tensor_tensor(z1[:, :], z0[:, :], ring(XF, t), ALU.add).then_inc(bk, 1)
                dve.wait_ge(bk, BK * t + 2)
                norm(bk, BK * t + 2, bsd, t + 1, st2, mv2, sd2, rs2, z1[:, :], on[:, :])
                dve.wait_ge(bk, BK * t + 6)
                past(dve, scattered, 16 * t)
                dve.tensor_tensor(O[:, :], on[:, :], ring(X1, t), ALU.add).then_inc(bk, 1)

            front(0)
            affine(0)
            front(1)
            affine(1)
            front(2)

            def step(t, first, aff, frt):
                relu(t)
                if not first:
                    back(t - 1)
                if aff:
                    affine(t + 2)
                if frt:
                    front(t + 3)

            step(0, True, True, True)
            step(1, False, True, True)
            with dve.Fori(2, NS - 3) as t:
                step(t, False, True, True)
            step(NS - 3, False, True, False)
            step(NS - 2, False, False, False)
            step(NS - 1, False, False, False)
            back(NS - 1)


_INS = ['L0_attn_x', 'L0_attn_Wc_down', 'L0_attn_Wq_up', 'L0_attn_Wkv_up', 'L0_attn_Wc_proj', 'L0_ffn_centroids',
        'L0_ffn_ln_g', 'L0_ffn_ln_b', 'L0_ffn_W1', 'L0_ffn_b1', 'L0_ffn_W2', 'L0_ffn_b2']
_OUTS = [((4, 1024, 256), 'float32')]


def kernel(**inputs):
    import numpy as _np
    import concourse.bacc as _bacc
    from concourse import mybir as _mybir
    from concourse.bass_utils import run_bass_kernel_spmd as _run

    nc = _bacc.Bacc("TRN2", target_bir_lowering=False, num_devices=1)
    arrays, args = {}, []
    for name in _INS:
        a = _np.ascontiguousarray(inputs[name])
        arrays[f"in_{name}_dram"] = a
        args.append(nc.dram_tensor(f"in_{name}_dram", a.shape, _mybir.dt.from_np(a.dtype), kind="ExternalInput").ap())
    for i, (shape, dtype) in enumerate(_OUTS):
        dt = _mybir.dt.from_np(_np.dtype(dtype))
        args.append(nc.dram_tensor(f"out_{i}_dram", shape, dt, kind="ExternalOutput").ap())
    build(nc, *args)
    r = _run(nc, [arrays], core_ids=[0])
    got = tuple(r.results[0][f"out_{i}_dram"] for i in range(len(_OUTS)))
    return got[0]
```

```python
from contextlib import ExitStack

import concourse.bass as bass
import concourse.mybir as mybir

F32 = mybir.dt.float32
BF16 = mybir.dt.bfloat16
I32 = mybir.dt.int32
U32 = mybir.dt.uint32
ALU = mybir.AluOpType
ACT = mybir.ActivationFunctionType
AX = mybir.AxisListType.X
ds = bass.ds

P = 128
B, T, D = 4, 1024, 256
NTOK = B * T
NT = NTOK // P
TB = T // P
NH, HD = 16, 16
LAT = D // 2
GH = 4
NG = NH // GH
NQ = 512
QC = T // NQ
DC = D // P
EPS = 1e-5
SCALE = 1.0 / HD ** 0.5
LOWEST = -3.0e38
E, F = 8, 1024
FC = F // P
NS = NT + E - 1

QPART = (0, 0, 0, 1, 1, 2)
KPART = (0, 1, 2, 0, 1, 0)
NR = len(QPART) * HD
KR = NR + 3

STEPS = [(c, j, max(0, j - c * (NQ // P)) * P) for c in range(QC) for j in range((c + 1) * (NQ // P))]
DIAG = [s for s, (c, j, off) in enumerate(STEPS) if j >= c * (NQ // P)]
LAST = len(STEPS) - 1
UNITS = [[(h,) for h in range(GH)] if NQ - off > NQ // 2 else [(h, h + 1) for h in range(0, GH, 2)]
         for _, _, off in STEPS]
UNIT_AT = [sum(len(u) for u in UNITS[:s]) for s in range(len(STEPS) + 1)]
NU = UNIT_AT[-1]
LAG = 2
RB = 3
C0 = NQ // P - 1
BW = NQ // P
WHOLE = [(i, c, NQ, (c + 1) * BW == i + 1) for i in range(TB) for c in range((i + 1) // BW)]
RESTS = {i: (i, (i + 1) // BW, (i + 1) % BW * P, True) for i in range(TB) if (i + 1) % BW}
PAIRS = []
while RESTS:
    i, rest = RESTS.popitem()
    mate = next(k for k in RESTS if RESTS[k][2] == NQ - rest[2])
    PAIRS.append([RESTS.pop(mate), rest])
MAXES = [[m] for m in WHOLE] + PAIRS
NM = GH * len(MAXES)
MAX_AT = [round(NM * sum(NQ - o for _, _, o in STEPS[:s + 1]) / sum(NQ - o for _, _, o in STEPS))
          for s in range(len(STEPS))]
MAX_OF = [MAX_AT[s] - (MAX_AT[s - 1] if s else 0) for s in range(len(STEPS))]

PIECES = ("q00", "q01", "kv0", "kv1", "q10", "q11")
MISC = (
    (("m", 1), ("q00", 4), ("q01", 6), ("o0", 7), ("kv0", 8)),
    (("m", 1), ("p1", 3), ("kv1", 4), ("q10", 6), ("o0", 7), ("vt", 8)),
    (("m", 1), ("p1", 3), ("q11", 5), ("o0", 7)),
    (("m", 1), ("p1", 3), ("o0", 7), ("o1", 99)),
)
MISC_FIRST = ("vt", "m")
MISC_BATCH = sum(len(m) for m in MISC)


def misc_events(g, more):
    return [(n, s) for n, s in MISC[g] if more or n in ("o0", "p1", "o1") or (n == "m" and g < NG - 1)]


def misc_at(b, g, name, more):
    before = [n for k in range(g) for n, _ in misc_events(k, more)]
    before += [n for n, _ in misc_events(g, more)]
    k = len([n for kk in range(g) for n, _ in misc_events(kk, more)])
    return len(MISC_FIRST) + b * MISC_BATCH + before.index(name, k)


def past(eng, sem, n):
    if not isinstance(n, int) or n > 0:
        eng.wait_ge(sem, n)


def alone(eng, spare):
    eng.sem_inc(spare, 1)


def build(nc, x, Wc_down, Wq_up, Wkv_up, Wc_proj, centroids, ln_g, ln_b, W1, b1, W2, b2, out):
    nc.disable_value_cache = True
    with ExitStack() as ctx:
        sb = lambda name, shape, dt=F32: ctx.enter_context(nc.sbuf_tensor(name, shape, dt))
        sem = lambda name: ctx.enter_context(nc.semaphore(name))
        x1_dram = nc.dram_tensor("x1_rows", (NTOK, D), F32, kind="Internal").ap()
        W1s = sb("W1s", [P, DC, E * F])
        ident = sb("ident", [P, P])
        identb = sb("identb", [P, P], BF16)
        eps = sb("eps", [P, 1])
        IDX = sb("IDX", [P, NS], I32)
        EX = sb("EX", [P, NS], I32)
        started = sem("started")
        spare = sem("spare")
        w1_in = sem("w1_in")
        w2_in = sem("w2_in")
        w1_v = W1.rearrange("e (c p) f -> e p c f", p=P)
        w2_v = W2.rearrange("e (c p) d -> e p c d", p=P)
        Y = sb("Y", [P, NT * D])
        attention(nc, eps, started, spare, x, Wc_down, Wq_up, Wkv_up, ident, identb, Y, W1s, w1_v, w1_in)
        with ExitStack() as fctx:
            W2s = fctx.enter_context(nc.sbuf_tensor("W2s", [P, E, FC * D], F32))
            route(nc, started, spare, x, Wc_proj, centroids, ident, eps, Y, W2s, w2_v, w2_in, x1_dram, IDX, EX)
            experts(nc, started, spare, ln_g, ln_b, b1, b2, ident, eps, Y, W1s, w1_in, W2s, w2_in, x1_dram, IDX, EX, out)


def attention(nc, eps, started, spare, x, Wc_down, Wq_up, Wkv_up, ident, identb, Y, W1s, w1_v, w1_in):
    with ExitStack() as ctx:
        sb = lambda name, shape, dt=F32: ctx.enter_context(nc.sbuf_tensor(name, shape, dt))
        sem = lambda name: ctx.enter_context(nc.semaphore(name))
        psum = lambda name, shape, dt=F32: ctx.enter_context(nc.psum_tensor(name, shape, dt))
        causal = sb("causal", [P, NQ])
        LT = sb("LT", [P, NTOK])
        Wq = sb("Wq", [P, D])
        Wkv = sb("Wkv", [P, 2 * HD])
        Q = sb("Q", [P, NH, T], BF16)
        KN = sb("KN", [P, T], BF16)
        KC = sb("KC", [P, T], BF16)
        VN = sb("VN", [P, TB, 2 * HD])
        VC = sb("VC", [P, TB, 2 * HD])
        T1, T2, T3 = (sb(f"T{k}", [P, 2, T], BF16) for k in (1, 2, 3))
        K1, K2, K3 = (sb(f"K{k}", [2 * HD, T], BF16) for k in (1, 2, 3))
        R1 = sb("R1", [P, NQ])
        KV = sb("KV", [2 * HD, T])
        MP = [sb(f"MP{k}", [P, 2, GH, TB]) for k in range(2)]
        mx = sb("mx", [P, GH * TB])
        mr = sb("mr", [P, GH * TB])
        NMX = sb("NMX", [P, 3, GH * TB], BF16)
        MT = sb("MT", [3 * GH * TB, P], BF16)
        junk = sb("junk", [P, 2, NQ], BF16)
        rden = sb("rden", [P, NQ // P, GH])
        small_pool = 0

        s_id = sem("s_id")
        s_w = sem("s_w")
        s_mask = sem("s_mask")
        ones_set = sem("ones_set")

        with ExitStack() as c2:
            sb2 = lambda name, shape, dt=F32: c2.enter_context(nc.sbuf_tensor(name, shape, dt))
            ps2 = lambda name, shape, dt=F32: c2.enter_context(nc.psum_tensor(name, shape, dt))
            sem2 = lambda name: c2.enter_context(nc.semaphore(name))
            QT = 4
            W = QT * D
            X = Y
            XN = [sb2(f"XN{k}", [P, QT, D]) for k in range(2)]
            XT = [sb2(f"XT{k}", [P, DC, QT * P]) for k in range(2)]
            Wd = sb2("Wd", [P, DC, LAT])
            st = [sb2(f"st{k}", [P, QT, 6]) for k in range(2)]
            mv = [sb2(f"mv{k}", [P, QT, 2]) for k in range(2)]
            rs = [sb2(f"rs{k}", [P, QT]) for k in range(2)]
            sd = [sb2(f"sd{k}", [P, QT]) for k in range(2)]
            xtp = [ps2(f"xtp{k}", [P, DC, QT * P]) for k in range(2)]
            ltp = [ps2(f"ltp{k}", [P, QT * P]) for k in range(2)]
            x_in = [sem2(f"x_in{k}") for k in range(2)]
            stats = sem2("stats")
            aggr = sem2("aggr")
            sd_ready = sem2("sd_ready")
            rstd = sem2("rstd")
            xn_ready = sem2("xn_ready")
            xt_ready = sem2("xt_ready")
            xt_copied = sem2("xt_copied")
            lt_ready = sem2("lt_ready")
            lt_copied = sem2("lt_copied")
            N1 = NT // QT
            xv = x.rearrange("b (i p) d -> p (b i) d", p=P)
            block = c2.enter_context(nc.Block())

            def passes(eng, step, start=0):
                if start == 0:
                    step(0, 0)
                with eng.Fori(0, N1 // 2 - 1) as t2:
                    step(2 * t2 + 1, 1)
                    step(2 * t2 + 2, 0)
                step(N1 - 1, 1)

            @block.sync
            def _(sp):
                for t in range(N1):
                    if t >= 2:
                        sp.wait_ge(x_in[t % 2], 16 * (t // 2))
                    sp.dma_start(X[:, t * W:(t + 1) * W].rearrange("p (i d) -> p i d", d=D),
                                 xv[:, t * QT:(t + 1) * QT, :]).then_inc(x_in[t % 2], 16)
                    if t == 1:
                        sp.dma_start(Wd[:, :, :], Wc_down.rearrange("(c p) n -> p c n", p=P)).then_inc(s_w, 16)
                        sp.dma_start(Wq[:, :], Wq_up[:, :]).then_inc(s_w, 16)
                        sp.dma_start(Wkv[:, :], Wkv_up[:, :]).then_inc(s_w, 16)

            @block.gpsimd
            def _(pool):
                pool.memset(ident[:, :], 0.0).then_inc(s_id, 1)
                pool.memset(identb[:, :], 0.0).then_inc(s_id, 1)
                pool.memset(causal[:, :], 0.0).then_inc(s_id, 1)
                pool.wait_ge(s_id, 3)
                for m in (ident, identb):
                    pool.affine_select(out=m[:, :], in_=m[:, :], compare_op=ALU.not_equal, fill=1.0, base=0,
                                       pattern=[[-1, P]], channel_multiplier=1).then_inc(s_id, 1)
                m = causal[:, NQ - P:NQ]
                pool.affine_select(out=m, in_=m, compare_op=ALU.is_ge, fill=LOWEST, base=0,
                                   pattern=[[-1, P]], channel_multiplier=1).then_inc(s_id, 1)
                pool.memset(KN[:, :], 1.0).then_inc(ones_set, 1)
                pool.memset(VN[:, :, :], 1.0).then_inc(ones_set, 1)
                for k in range(2):
                    pool.memset(MP[k][:, :, :, :], LOWEST).then_inc(ones_set, 1)

            @block.vector
            def _(dve):
                dve.memset(eps[:, :], EPS).then_inc(started, 1)

                def x_of(t, i):
                    return X[:, ds(t * W + i * D, D)]

                def statistics(t, k, seen):
                    dve.wait_ge(x_in[k], seen)
                    alone(dve, spare)
                    for i in range(QT):
                        last = dve.bn_stats(st[k][:, i, :], x_of(t, i))
                    last.then_inc(stats, 1)
                    dve.wait_ge(stats, t + 1)
                    past(dve, xn_ready, QT * (t - 1))
                    alone(dve, spare)
                    for i in range(QT):
                        last = dve.bn_aggr(mv[k][:, i, :], st[k][:, i, :])
                    last.then_inc(aggr, 1)

                def inverse(t, k):
                    dve.wait_ge(sd_ready, t + 1)
                    dve.reciprocal(rs[k][:, :], sd[k][:, :]).then_inc(rstd, 1)

                def step(t, k):
                    more = not isinstance(t, int) or t < N1 - 1
                    if more:
                        statistics(t + 1, 1 - k, 8 * (t + 2 + k))
                    dve.wait_ge(rstd, t + 1)
                    past(dve, xt_ready, t)
                    for i in range(QT):
                        dve.tensor_scalar(XN[k][:, i, :], x_of(t, i), mv[k][:, i, 0:1], rs[k][:, i:i + 1],
                                          ALU.subtract, ALU.mult).then_inc(xn_ready, 1)
                    if more:
                        inverse(t + 1, 1 - k)

                statistics(0, 0, 16)
                inverse(0, 0)
                passes(dve, step)

            @block.tensor
            def _(pe):
                pe.wait_ge(s_id, 6)
                pe.wait_ge(s_w, 48)
                pe.sem_inc(xt_ready, 1)

                def down(t, k):
                    pe.wait_ge(xt_copied, DC * (t + 1))
                    pe.wait_ge(lt_copied, t + 1)
                    for c in range(DC):
                        mm = pe.matmul(ltp[k][:, :], Wd[:, c, :], XT[k][:, c, :], start=c == 0, stop=c == DC - 1)
                    mm.then_inc(lt_ready, 1)

                def step(t, k):
                    for i in range(QT):
                        pe.wait_ge(xn_ready, QT * t + i + 1)
                        for c in range(DC):
                            last = pe.transpose(xtp[k][:, c, i * P:(i + 1) * P], XN[k][:, i, c * P:(c + 1) * P],
                                                ident[:, :])
                    last.then_inc(xt_ready, 1)
                    if not isinstance(t, int) or t:
                        down(t - 1, 1 - k)

                passes(pe, step)
                down(N1 - 1, 1)

            @block.scalar
            def _(act):
                act.wait_ge(started, 1)

                act.sem_inc(lt_copied, 2)

                def root(t, k):
                    act.wait_ge(aggr, t + 1)
                    act.activation(sd[k][:, :], mv[k][:, :, 1], ACT.Sqrt, bias=eps[:, :]).then_inc(sd_ready, 1)

                def latent(t, k):
                    act.wait_ge(lt_ready, t + 1)
                    act.activation(LT[:, ds(t * (QT * P), QT * P)], ltp[k][:, :], ACT.Copy).then_inc(lt_copied, 1)

                def step(t, k):
                    if not isinstance(t, int) or t < N1 - 1:
                        root(t + 1, 1 - k)
                    act.wait_ge(xt_ready, t + 2)
                    for c in range(DC):
                        act.activation(XT[k][:, c, :], xtp[k][:, c, :], ACT.Copy).then_inc(xt_copied, 1)
                    if not isinstance(t, int) or t:
                        latent(t - 1, 1 - k)

                root(0, 0)
                step(0, 0)
                for e in range(E):
                    act.dma_start(W1s[:, :, e * F:(e + 1) * F], w1_v[e]).then_inc(w1_in, 16)
                passes(act, step, 1)
                latent(N1 - 1, 1)

        PR = [sb(f"PR{k}", [P, GH, NQ]) for k in range(RB)]
        OS = sb("OS", [P, NQ])
        ST = [psum(f"ST{k}", [P, NQ]) for k in range(RB)]
        SM = [psum(f"SM{k}", [P, NQ]) for k in range(RB)]
        OB = psum("OB", [P, NQ])
        misc = psum("misc", [P, NQ])

        misc_ready = sem("misc_ready")
        misc_free = sem("misc_free")
        part1 = sem("part1")
        kv_copied = sem("kv_copied")
        resid = sem("resid")
        part2 = sem("part2")
        part3 = sem("part3")
        k_in = sem("k_in")
        q_in = [[sem(f"q_in{g}_{h}") for h in range(GH)] for g in range(NG)]
        first_ready = sem("first_ready")
        m_in = [sem(f"m_in{g}") for g in range(NG)]
        v_next = sem("v_next")
        kv_now = sem("kv_now")
        sm_ready = sem("sm_ready")
        sm_done = sem("sm_done")
        m_step = sem("m_step")
        mt_ready = sem("mt_ready")
        st_ready = sem("st_ready")
        exp_done = sem("exp_done")
        masked = sem("masked")
        pv_done = sem("pv_done")
        o_copied = sem("o_copied")
        o_step = sem("o_step")
        NMS = 5

        block = ctx.enter_context(nc.Block())

        def piece_no(b, name):
            return b * len(PIECES) + PIECES.index(name)

        def is_kv(name):
            return name.startswith("kv")

        def parts(name):
            c = int(name[-1])
            if is_kv(name):
                return [t[:, c * NQ:(c + 1) * NQ] for t in (K1, K2, K3)]
            return [t[:, int(name[1]), c * NQ:(c + 1) * NQ] for t in (T1, T2, T3)]

        def rows_of(name):
            return 2 * HD if is_kv(name) else P

        def queries_in(eng, g, n, heads=range(GH)):
            for h in heads:
                eng.wait_ge(q_in[g][h], 16 * len(QPART) * n)

        def room(name, first):
            i = PIECES.index(name)
            return ((ST + SM)[i], PR[i // GH][:, i % GH, :]) if first else (misc, R1)

        def parts_sent(eng, bn, name):
            if is_kv(name):
                eng.wait_ge(k_in, 16 * len(QPART) * bn)
            else:
                for g in (2 * int(name[1]), 2 * int(name[1]) + 1):
                    queries_in(eng, g, bn)

        def loops(eng, body):
            with eng.Fori(0, B - 1) as b:
                for g in range(NG):
                    body(b, g, True)
            for g in range(NG):
                body(B - 1, g, False)

        @block.tensor
        def _(pe):
            def misc_use(k):
                past(pe, misc_free, k)

            def piece(bn, name, k, first=False):
                if not first:
                    misc_use(k)
                    alone(pe, spare)
                c = int(name[-1])
                w = Wkv[:, :] if is_kv(name) else Wq[:, int(name[1]) * P:(int(name[1]) + 1) * P]
                bank, _ = room(name, first)
                pe.matmul(bank[0:rows_of(name), :], w, LT[:, ds(bn * T + c * NQ, NQ)], start=True, stop=True)\
                  .then_inc(first_ready if first else misc_ready, 1)

            def values(bn, k):
                misc_use(k)
                pe.wait_ge(kv_copied, 2 * (bn + 1))
                alone(pe, spare)
                for j in range(TB):
                    last = pe.transpose(misc[:, j * 2 * HD:(j + 1) * 2 * HD], KV[:, j * P:(j + 1) * P],
                                        ident[0:2 * HD, 0:2 * HD])
                last.then_inc(misc_ready, 1)

            def neg_max(r, k):
                misc_use(k)
                pe.wait_ge(m_step, NMS * (r + 1))
                pe.transpose(misc[0:3 * GH * TB, 0:P // 2].bitcast(BF16), NMX[:, :, :], identb[:, :])\
                  .then_inc(misc_ready, 1)

            def maxes(r, g, key, n):
                if n >= RB or not isinstance(r, int) or r:
                    pe.wait_ge(sm_done, NM * r + n - RB + 1)
                h, at = n // len(MAXES), 0
                for i, c, w, _ in MAXES[n % len(MAXES)]:
                    last = pe.matmul(SM[n % RB][:, at:at + w], Q[0:NR, g * GH + h, i * P:(i + 1) * P],
                                     key[0:NR, c * NQ:c * NQ + w], start=True, stop=True)
                    at += w
                last.then_inc(sm_ready, 1)

            def out_t(n, c, k):
                misc_use(k)
                pe.wait_ge(o_copied, QC * n + c + 1)
                for t in range(NQ // P):
                    last = pe.transpose(misc[:, t * P:(t + 1) * P], OS[:, t * P:(t + 1) * P], ident[:, :])
                last.then_inc(misc_ready, 1)

            def pv(n, s, first, flush=False):
                c, j, off = STEPS[s]
                if flush:
                    pe.wait_ge(exp_done, NU * n + UNIT_AT[s + 1])
                if s in DIAG:
                    pe.wait_ge(masked, len(DIAG) * n + DIAG.index(s) + 1)
                if s == C0 + 1:
                    pe.wait_ge(o_copied, QC * n + 1)
                if s == 0 and not first:
                    pe.wait_ge(o_copied, QC * n)
                for h in range(GH):
                    last = pe.matmul(OB[32 * h:32 * h + 32, off:NQ], VC[:, j, :], PR[s % RB][:, h, off:NQ],
                                     start=j == 0, stop=s in (C0, LAST))
                last.then_inc(pv_done, 1)

            def group(b, g, more):
                n = b * NG + g
                after = g + 2
                bm, gm, key = (b, after, KC) if after < NG else (b + 1, after - NG, KN)
                take = after < NG or more
                queries_in(pe, g, b + 1)
                if take:
                    queries_in(pe, gm, bm + 1)
                    pe.wait_ge(k_in, 16 * len(QPART) * (bm + 1))
                if g == 0:
                    pe.wait_ge(kv_now, 2 * (b + 1))
                pe.wait_ge(m_in[g], 3 * 16 * (b + 1))
                done = 0
                for s, (c, j, off) in enumerate(STEPS):
                    for k, heads in enumerate(UNITS[s]):
                        u = NU * g + UNIT_AT[s] + k
                        if u >= RB:
                            pe.wait_ge(exp_done, NU * NG * b + u - RB + 1)
                        for h in heads:
                            at = (h - heads[0]) * (NQ - off)
                            last = pe.matmul(ST[u % RB][:, at:at + NQ - off], KC[0:KR, j * P:(j + 1) * P],
                                             Q[0:KR, g * GH + h, c * NQ + off:(c + 1) * NQ], start=True, stop=True)
                        last.then_inc(st_ready, 1)
                        if take and done < MAX_AT[s] - 1:
                            maxes(n + 2, gm, key, done)
                            done += 1
                    for name, at in misc_events(g, more):
                        k = misc_at(b, g, name, more)
                        if at == s:
                            if name == "m":
                                neg_max(n + 1, k)
                            elif name == "o0":
                                out_t(n, 0, k)
                            elif name == "p1":
                                out_t(n - 1, 1, k)
                            elif name == "vt":
                                values(b + 1, k)
                            else:
                                piece(b + 1, name, k)
                    if s >= LAG:
                        pv(n, s - LAG, g == 0)
                    elif g:
                        pv(n - 1, len(STEPS) - LAG + s, False)
                    while take and done < MAX_AT[s]:
                        maxes(n + 2, gm, key, done)
                        done += 1
                if g == NG - 1:
                    for s in range(len(STEPS) - LAG, len(STEPS)):
                        pv(n, s, False, True)
                    out_t(n, 1, misc_at(b, g, "o1", more))

            pe.wait_ge(s_id, 6)
            for name in PIECES:
                piece(0, name, None, True)
            values(0, 0)
            pe.wait_ge(k_in, 16 * len(QPART))
            pe.wait_ge(resid, len(PIECES))
            for g in range(2):
                for n in range(NM):
                    if n % len(MAXES) == 0:
                        queries_in(pe, g, 1, [n // len(MAXES)])
                    maxes(g, g, KN, n)
                    if g == 1 and n == NMS:
                        neg_max(0, 1)
            loops(pe, group)

        @block.scalar
        def _(act):
            def piece(bn, name, k, first=False):
                if first:
                    act.wait_ge(first_ready, PIECES.index(name) + 1)
                else:
                    act.wait_ge(misc_ready, k + 1)
                    parts_sent(act, bn, name)
                p1, _, _ = parts(name)
                bank, _ = room(name, first)
                act.activation(p1, bank[0:rows_of(name), :], ACT.Copy).then_inc(part1, 1)
                if is_kv(name):
                    c = int(name[-1])
                    past(act, v_next, bn)
                    act.activation(KV[:, c * NQ:(c + 1) * NQ], bank[0:2 * HD, :], ACT.Copy).then_inc(kv_copied, 1)

            def piece2(bn, name, first=False):
                act.wait_ge(resid, piece_no(bn, name) + 1)
                _, p2, _ = parts(name)
                _, left = room(name, first)
                act.activation(p2, left[0:rows_of(name), :], ACT.Copy).then_inc(part2, 1)

            def out_copy(n, c, s):
                act.wait_ge(pv_done, len(STEPS) * n + s + 1)
                act.activation(OS[:, :], OB[:, :], ACT.Copy).then_inc(o_copied, 1)

            def group(b, g, more):
                n = b * NG + g
                for s, (c, j, off) in enumerate(STEPS):
                    for k, heads in enumerate(UNITS[s]):
                        u = NU * g + UNIT_AT[s] + k
                        act.wait_ge(st_ready, NU * NG * b + u + 1)
                        if k == 0 and (g or s >= RB):
                            act.wait_ge(pv_done, len(STEPS) * n + s - RB + 1)
                        act.activation(PR[s % RB][:, heads[0]:heads[-1] + 1, off:NQ],
                                       ST[u % RB][:, 0:len(heads) * (NQ - off)].rearrange("p (h q) -> p h q", h=len(heads)),
                                       ACT.Exp, scale=SCALE).then_inc(exp_done, 1)
                    for name, at in misc_events(g, more):
                        if name in PIECES and s == at:
                            piece(b + 1, name, misc_at(b, g, name, more))
                        if name in PIECES and s == at + 1:
                            piece2(b + 1, name)
                    if s == C0 + LAG:
                        out_copy(n, 0, C0)
                    if g and s == LAG - 1:
                        out_copy(n - 1, 1, LAST)
                if g == NG - 1:
                    out_copy(n, 1, LAST)

            piece(0, PIECES[0], None, True)
            for name, last in zip(PIECES[1:], PIECES):
                piece(0, name, None, True)
                piece2(0, last, True)
            piece2(0, PIECES[-1], True)
            act.wait_ge(part3, len(PIECES))
            loops(act, group)

        @block.vector
        def _(dve):
            def piece(bn, name, k, stage, first=False):
                if stage == 0:
                    dve.wait_ge(part1, piece_no(bn, name) + 1)
                    if is_kv(name):
                        dve.wait_ge(kv_copied, 2 * bn + int(name[-1]) + 1)
                    if not first:
                        dve.wait_ge(part3, piece_no(bn, name))
                    p1, _, _ = parts(name)
                    rows = rows_of(name)
                    bank, left = room(name, first)
                    dve.tensor_tensor(left[0:rows, :], bank[0:rows, :], p1, ALU.subtract).then_inc(resid, 1)
                else:
                    dve.wait_ge(resid, piece_no(bn, name) + 1)
                    dve.sem_inc(misc_free, 1)

            def values(bn, k, stage):
                if stage == 0:
                    dve.wait_ge(misc_ready, k + 1)
                    past(dve, kv_now, 2 * bn)
                    v = misc[:, 0:TB * 2 * HD].rearrange("p (j d) -> p j d", j=TB)
                    dve.tensor_copy(VN[:, :, 0:HD], v[:, :, HD:2 * HD]).then_inc(v_next, 1)
                else:
                    dve.wait_ge(v_next, bn + 1)
                    dve.sem_inc(misc_free, 1)

            def take_max(r, n, par):
                dve.wait_ge(sm_ready, NM * r + n + 1)
                h, at = n // len(MAXES), 0
                for i, c, w, diag in MAXES[n % len(MAXES)]:
                    dst, src = MP[par][:, c, h, i:i + 1], SM[n % RB][:, at:at + w]
                    if diag:
                        if n >= 2 or not isinstance(r, int) or r:
                            dve.wait_ge(sm_done, NM * r + n - 1)
                        alone(dve, spare)
                        op = dve.tensor_tensor_reduce(junk[:, n % 2, at:at + w], src, causal[:, NQ - w:NQ], 1.0, LOWEST,
                                                      ALU.add, ALU.max, dst)
                    else:
                        op = dve.tensor_reduce(dst, src, AX, ALU.max)
                    at += w
                op.then_inc(sm_done, 1)

            def neg_max(r, par, stage):
                if stage == 0:
                    dve.wait_ge(sm_done, NM * (r + 1))
                    past(dve, mt_ready, r)
                    m0, m1 = (MP[par][:, c, :, :].rearrange("p h i -> p (h i)") for c in range(2))
                    op = dve.tensor_tensor(mx[:, :], m0, m1, ALU.max)
                else:
                    dve.wait_ge(m_step, NMS * r + stage)
                if stage == 1:
                    op = dve.tensor_scalar(NMX[:, 0, :], mx[:, :], -1.0, None, ALU.mult)
                if stage == 2:
                    op = dve.scalar_tensor_tensor(out=mr[:, :], in0=mx[:, :], scalar=-1.0, in1=NMX[:, 0, :],
                                                  op0=ALU.mult, op1=ALU.subtract)
                if stage == 3:
                    op = dve.tensor_copy(NMX[:, 1, :], mr[:, :])
                if stage == 4:
                    op = dve.tensor_tensor(NMX[:, 2, :], mr[:, :], NMX[:, 1, :], ALU.subtract)
                op.then_inc(m_step, 1)

            def max_rows(r, g, k, stage):
                if stage == 0:
                    dve.wait_ge(misc_ready, k + 1)
                    if g is not None:
                        dve.wait_ge(m_in[g[0]], 3 * 16 * (g[1] + 1))
                    dve.tensor_copy(MT[:, :], misc[0:3 * GH * TB, 0:P // 2].bitcast(BF16)).then_inc(mt_ready, 1)
                else:
                    dve.wait_ge(mt_ready, r + 1)
                    dve.sem_inc(misc_free, 1)

            def out_norm(b, g, c, k, stage):
                o = misc[:, :].rearrange("p (t h d) -> p t h d", t=NQ // P, h=GH)
                if stage == 0:
                    dve.wait_ge(misc_ready, k + 1)
                    dve.wait_ge(misc_free, k)
                    dve.reciprocal(rden[:, :, :], o[:, :, :, HD]).then_inc(o_step, 1)
                else:
                    dve.wait_ge(o_step, QC * (b * NG + g) + c + 1)
                    y = Y[:, ds((b * TB + c * (NQ // P)) * D, (NQ // P) * D)]\
                        .rearrange("p (t h d) -> p t h d", t=NQ // P, d=HD)[:, :, g * GH:(g + 1) * GH, :]
                    rb = rden[:, :, :].rearrange("p t (h u) -> p t h u", u=1).broadcast_to([P, NQ // P, GH, HD])
                    dve.tensor_tensor(y, o[:, :, :, 0:HD], rb, ALU.mult).then_inc(misc_free, 1)

            def keys_now(b):
                dve.wait_ge(k_in, 16 * len(QPART) * (b + 1))
                dve.wait_ge(v_next, b + 1)
                dve.tensor_copy(KC[0:KR, :], KN[0:KR, :]).then_inc(kv_now, 1)
                dve.tensor_copy(VC[:, :, :], VN[:, :, :]).then_inc(kv_now, 1)

            def group(b, g, more):
                n = b * NG + g
                take = g + 2 < NG or more
                if g == 0:
                    keys_now(b)

                def use(name, stage):
                    k = misc_at(b, g, name, more)
                    if name == "m":
                        max_rows(n + 1, (g, b), k, stage)
                    elif name == "vt":
                        values(b + 1, k, stage)
                    elif name in PIECES:
                        piece(b + 1, name, k, stage)
                    else:
                        out_norm(b, g - 1 if name == "p1" else g, 0 if name == "o0" else 1, k, stage)

                have_m = g < NG - 1 or more
                done = 0
                for s in range(len(STEPS)):
                    count = MAX_OF[s] if take else 0
                    chain = NMS if have_m and s == 0 else 0
                    names = [name for name, at in misc_events(g, more) if at == s]
                    for i in range(max(count, chain, 2 if names else 0)):
                        if i < count:
                            take_max(n + 2, done, g % 2)
                            done += 1
                        if i < chain:
                            neg_max(n + 1, (g + 1) % 2, i)
                        for name in names:
                            if i >= max(count, 2) - 2:
                                use(name, i - max(count, 2) + 2)
                if g == NG - 1:
                    for stage in range(2):
                        use("o1", stage)

            dve.wait_ge(ones_set, 4)
            for name in PIECES:
                piece(0, name, None, 0, True)
            for stage in range(2):
                values(0, 0, stage)
            for g in range(2):
                for n in range(NM):
                    take_max(g, n, g)
                    if g == 1 and n < NMS:
                        neg_max(0, 0, n)
                    if g == 1 and NMS < n < NMS + 3:
                        max_rows(0, None, 1, n - NMS - 1)
            loops(dve, group)

        @block.gpsimd
        def _(pool):
            def piece(bn, name, first=False):
                k = piece_no(bn, name)
                rows = rows_of(name)
                _, p2, p3 = parts(name)
                if not first:
                    parts_sent(pool, bn, name)
                pool.wait_ge(part2, k + 1)
                _, left = room(name, first)
                pool.tensor_tensor(p3, left[0:rows, :], p2, ALU.subtract).then_inc(part3, 1)

            def group(b, g, more):
                n = b * NG + g
                for s, (c, j, off) in enumerate(STEPS):
                    if s in DIAG:
                        pool.wait_ge(exp_done, NU * n + UNIT_AT[s + 1])
                        alone(pool, spare)
                        p = PR[s % RB][:, :, off:off + P]
                        pool.affine_select(out=p, in_=p, compare_op=ALU.is_ge, fill=0.0, base=0,
                                           pattern=[[0, GH], [1, P]], channel_multiplier=-1).then_inc(masked, 1)
                    for name, at in misc_events(g, more):
                        if s == at + 1 and name in PIECES:
                            piece(b + 1, name)

            for name in PIECES:
                piece(0, name, True)
            loops(pool, group)

        @block.sync
        def _(sp):
            def send_keys(b):
                sp.wait_ge(ones_set, 4)
                sp.wait_ge(part3, piece_no(b, "kv1") + 1)
                for r, part in enumerate(KPART):
                    sp.dma_start(KN[r * HD:(r + 1) * HD, :], (K1, K2, K3)[part][0:HD, :]).then_inc(k_in, 16)

            def send_queries(b, g):
                half, quarter = divmod(g, 2)
                sp.wait_ge(part3, piece_no(b, f"q{half}1") + 1)
                for h in range(GH):
                    row = (quarter * GH + h) * HD
                    for r, part in enumerate(QPART):
                        sp.dma_start(Q[r * HD:(r + 1) * HD, g * GH + h, :],
                                     (T1, T2, T3)[part][row:row + HD, half, :]).then_inc(q_in[g][h], 16)

            def send_max(r, g):
                sp.wait_ge(mt_ready, r + 1)
                for a in range(3):
                    sp.dma_start(Q[NR + a:NR + a + 1, g * GH:(g + 1) * GH, :].rearrange("u h (i q) -> u (h i) q", i=TB),
                                 MT[a * GH * TB:(a + 1) * GH * TB, :]).then_inc(m_in[g], 16)

            def group(b, g, more):
                n = b * NG + g
                if g < NG - 1:
                    send_max(n + 1, g + 1)
                elif more:
                    send_max(n + 1, 0)
                if more:
                    if g == 1:
                        sp.wait_ge(kv_now, 2 * (b + 1))
                        alone(sp, spare)
                        send_keys(b + 1)
                    sp.wait_ge(exp_done, NU * (n + 1))
                    alone(sp, spare)
                    send_queries(b + 1, g)

            send_keys(0)
            for g in range(2):
                send_queries(0, g)
            send_max(0, 0)
            for g in range(2, NG):
                send_queries(0, g)
            loops(sp, group)


def route(nc, started, spare, x, Wc_proj, centroids, ident, eps, Y, W2s, w2_v, w2_in, x1_dram, IDX, EX):
    with ExitStack() as ctx:
        sb = lambda name, shape, dt=F32: ctx.enter_context(nc.sbuf_tensor(name, shape, dt))
        sem = lambda name: ctx.enter_context(nc.semaphore(name))
        psum = lambda name, shape, dt=F32: ctx.enter_context(nc.psum_tensor(name, shape, dt))
        QT = 4
        NQD = NT // QT
        CT = sb("CT", [P, DC, E])
        ef = sb("ef", [P, NT])
        with ExitStack() as c2:
            sb2 = lambda name, shape, dt=F32: c2.enter_context(nc.sbuf_tensor(name, shape, dt))
            sem2 = lambda name: c2.enter_context(nc.semaphore(name))
            ps2 = lambda name, shape, dt=F32: c2.enter_context(nc.psum_tensor(name, shape, dt))
            YS = sb2("YS", [P, QT, D])
            YT = sb2("YT", [P, DC, QT * P])
            Wp = sb2("Wp", [P, DC, D])
            Cn = sb2("Cn", [E, D])
            X = [sb2(f"XQ{k}", [P, QT, D]) for k in range(2)]
            XA = sb2("XA", [P, QT, D])
            XF = sb2("XF", [P, QT, D])
            XFT = sb2("XFT", [P, DC, QT * P])
            st = sb2("st2", [P, 2 * QT, 6])
            mv = sb2("mv2", [P, 2 * QT, 2])
            sd = sb2("sd2", [P, 2 * QT])
            rs = sb2("rs2", [P, 2 * QT])
            nt = [sb2(f"nt{k}", [P, 2 * QT]) for k in range(3)]
            m8 = sb2("m8", [P, QT, 8])
            i8 = sb2("i8", [P, QT, 8], U32)
            lg = sb2("lg", [P, QT, E])
            ytp = [ps2(f"ytp{c}", [P, QT * P]) for c in range(DC)]
            pj = ps2("pj", [P, QT, D])
            xtp = [ps2(f"xftp{c}", [P, QT * P]) for c in range(DC)]
            lgp = ps2("lgp", [P, QT * E])
            w_in = sem2("wp_in")
            c_ready = sem2("c_ready")
            c_copied = sem2("c_copied")
            x_in = [sem2(f"xq_in{k}") for k in range(2)]
            ys_ready = sem2("ys_ready")
            yt_ready = sem2("yt_ready")
            yt_copied = sem2("yt_copied")
            pj_ready = sem2("pj_ready")
            stats = sem2("stats2")
            aggr = sem2("aggr2")
            sd_ready = sem2("sd2_ready")
            root = sem2("root2")
            xa_ready = sem2("xa_ready")
            x1_ready = sem2("x1_ready")
            x1_out = [sem2(f"x1_out{k}") for k in range(2)]
            xf_ready = sem2("xf_ready")
            xft_ready = sem2("xft_ready")
            xft_copied = sem2("xft_copied")
            lg_ready = sem2("lg_ready")
            top = sem2("top")
            xv = x.rearrange("b (i p) d -> p (b i) d", p=P)
            x1v = x1_dram.rearrange("(i p) d -> p i d", p=P)
            ROOT = 5
            TOP = 2 * QT + 2
            block = c2.enter_context(nc.Block())

            @block.sync
            def _(sp):
                sp.dma_start(Wp[:, :, :], Wc_proj.rearrange("(c p) n -> p c n", p=P)).then_inc(w_in, 16)
                sp.dma_start(Cn[:, :], centroids[:, :]).then_inc(w_in, 16)
                for k in range(2):
                    sp.dma_start(X[k][:, :, :], xv[:, k * QT:(k + 1) * QT, :]).then_inc(x_in[k], 16)

                for t in range(NQD):
                    k = t % 2
                    sp.wait_ge(x1_ready, QT * (t + 1))
                    sp.dma_start(x1v[:, t * QT:(t + 1) * QT, :], X[k][:, :, :]).then_inc(x1_out[k], 16)
                    if t + 2 < NQD:
                        sp.wait_ge(x1_out[k], 16 * (t // 2 + 1))
                        sp.wait_ge(xf_ready, t + 1)
                        sp.dma_start(X[k][:, :, :], xv[:, (t + 2) * QT:(t + 3) * QT, :]).then_inc(x_in[k], 16)
                for k in range(2):
                    sp.wait_ge(x1_out[k], 16 * (NQD // 2))
                for e in range(E):
                    sp.dma_start(W2s[:, e, :].rearrange("p (c d) -> p c d", c=FC), w2_v[e]).then_inc(w2_in, 16)

            @block.gpsimd
            def _(pool):
                with pool.Fori(0, NQD // 2) as t2:
                    for k in range(2):
                        t = 2 * t2 + k
                        pool.wait_ge(x_in[k], 16 * (t2 + 1))
                        for i in range(QT):
                            pool.wait_ge(xa_ready, QT * t + i + 1)
                            pool.tensor_tensor(X[k][:, i, :], X[k][:, i, :], XA[:, i, :], ALU.add)\
                                .then_inc(x1_ready, 1)

            @block.tensor
            def _(pe):
                pe.wait_ge(w_in, 32)
                for c in range(DC):
                    last = pe.transpose(lgp[:, c * E:(c + 1) * E], Cn[:, c * P:(c + 1) * P], ident[0:E, 0:E])
                last.then_inc(c_ready, 1)

                def turn_y(t):
                    pe.wait_ge(ys_ready, t + 1)
                    for c in range(DC):
                        for i in range(QT):
                            last = pe.transpose(ytp[c][:, i * P:(i + 1) * P], YS[:, i, c * P:(c + 1) * P], ident[:, :])
                    last.then_inc(yt_ready, 1)

                def project(t):
                    pe.wait_ge(yt_copied, DC * (t + 1))
                    for i in range(QT):
                        if i % 2 == 0:
                            past(pe, xa_ready, QT * (t - 1) + i + 2)
                        for c in range(DC):
                            mm = pe.matmul(pj[:, i, :], YT[:, c, i * P:(i + 1) * P], Wp[:, c, :],
                                           start=c == 0, stop=c == DC - 1)
                    mm.then_inc(pj_ready, 1)

                def logits(t):
                    pe.wait_ge(xf_ready, t + 1)
                    for c in range(DC):
                        for i in range(QT):
                            last = pe.transpose(xtp[c][:, i * P:(i + 1) * P], XF[:, i, c * P:(c + 1) * P], ident[:, :])
                    last.then_inc(xft_ready, 1)
                    pe.wait_ge(xft_copied, DC * (t + 1))
                    pe.wait_ge(top, TOP * t + 1)
                    for i in range(QT):
                        for c in range(DC):
                            mm = pe.matmul(lgp[:, i * E:(i + 1) * E], XFT[:, c, i * P:(i + 1) * P], CT[:, c, :],
                                           start=c == 0, stop=c == DC - 1)
                    mm.then_inc(lg_ready, 1)

                turn_y(0)
                project(0)
                turn_y(1)
                project(1)
                turn_y(2)
                pe.wait_ge(c_copied, 1)
                with pe.Fori(0, NQD - 3) as t:
                    project(t + 2)
                    turn_y(t + 3)
                    logits(t)
                project(NQD - 1)
                logits(NQD - 3)
                logits(NQD - 2)
                logits(NQD - 1)

            @block.scalar
            def _(act):
                def ys(t):
                    past(act, yt_ready, t)
                    act.activation(YS[:, :, :].rearrange("p t d -> p (t d)"), Y[:, ds(t * (QT * D), QT * D)],
                                   ACT.Copy).then_inc(ys_ready, 1)

                def yt(t):
                    act.wait_ge(yt_ready, t + 1)
                    past(act, pj_ready, t)
                    for c in range(DC):
                        act.activation(YT[:, c, :], ytp[c][:, :], ACT.Copy).then_inc(yt_copied, 1)

                def xft(t):
                    act.wait_ge(xft_ready, t + 1)
                    past(act, lg_ready, t)
                    for c in range(DC):
                        act.activation(XFT[:, c, :], xtp[c][:, :], ACT.Copy).then_inc(xft_copied, 1)

                def roots(t, lo, hi):
                    act.wait_ge(aggr, t + 2)
                    act.activation(sd[:, lo:hi], mv[:, lo:hi, 1], ACT.Sqrt, bias=eps[:, :]).then_inc(sd_ready, 1)

                def step(t, lo=0):
                    roots(t, lo, 2 * QT)
                    if lo == 0 and (not isinstance(t, int) or t + 2 < NQD):
                        yt(t + 2)
                    if lo == 0 and (not isinstance(t, int) or t + 3 < NQD):
                        ys(t + 3)
                    xft(t)

                ys(0)
                yt(0)
                ys(1)
                yt(1)
                ys(2)
                roots(-1, 0, QT)
                step(0)
                with act.Fori(1, NQD - 3) as t:
                    step(t)
                step(NQD - 3)
                step(NQD - 2)
                step(NQD - 1, QT)

            @block.vector
            def _(dve):
                dve.sem_inc(top, 1)
                dve.wait_ge(c_ready, 1)
                dve.tensor_copy(CT[:, :, :].rearrange("p c e -> p (c e)"), lgp[:, 0:DC * E]).then_inc(c_copied, 1)

                def argmax(t, stage):
                    base = TOP * t + 1
                    if stage == 0:
                        dve.wait_ge(lg_ready, t + 1)
                        dve.wait_ge(top, base)
                        dve.tensor_copy(lg[:, :, :].rearrange("p t e -> p (t e)"), lgp[:, :]).then_inc(top, 1)
                    if stage == 1:
                        dve.wait_ge(top, base + 1)
                        alone(dve, spare)
                        for i in range(QT):
                            dve.max(m8[:, i, :], lg[:, i, :]).then_inc(top, 1)
                    if stage == 2:
                        dve.wait_ge(top, base + 1 + QT)
                        alone(dve, spare)
                        for i in range(QT):
                            dve.max_index(i8[:, i, :], m8[:, i, :], lg[:, i, :]).then_inc(top, 1)
                    if stage == 3:
                        dve.wait_ge(top, base + 1 + 2 * QT)
                        dve.tensor_copy(ef[:, ds(t * QT, QT)], i8[:, :, 0]).then_inc(top, 1)

                def step(t, k, lo=0, hi=2 * QT, seen=True):
                    if hi > QT:
                        past(dve, xa_ready, QT * (t + 1))
                        past(dve, xf_ready, t)
                        for i in range(QT):
                            dve.wait_ge(x1_ready, QT * t + i + 1)
                            alone(dve, spare)
                            last = dve.bn_stats(st[:, QT + i, :], X[k][:, i, :])
                            if seen:
                                argmax(t - 2, i)
                    if lo == 0:
                        dve.wait_ge(pj_ready, t + 2)
                        alone(dve, spare)
                        for i in range(QT):
                            last = dve.bn_stats(st[:, i, :], pj[:, i, :])
                    last.then_inc(stats, 1)
                    dve.wait_ge(stats, t + 2)
                    alone(dve, spare)
                    for i in range(lo, hi):
                        last = dve.bn_aggr(mv[:, i, :], st[:, i, :])
                    last.then_inc(aggr, 1)
                    n = ROOT * (t + 1)
                    dve.wait_ge(sd_ready, t + 2)
                    dve.reciprocal(rs[:, lo:hi], sd[:, lo:hi]).then_inc(root, 1)
                    dve.wait_ge(root, n + 1)
                    dve.scalar_tensor_tensor(out=nt[0][:, lo:hi], in0=mv[:, lo:hi, 1], scalar=EPS, in1=rs[:, lo:hi],
                                             op0=ALU.add, op1=ALU.mult).then_inc(root, 1)
                    dve.wait_ge(root, n + 2)
                    dve.tensor_tensor(nt[1][:, lo:hi], nt[0][:, lo:hi], rs[:, lo:hi], ALU.mult).then_inc(root, 1)
                    dve.wait_ge(root, n + 3)
                    dve.tensor_scalar(nt[2][:, lo:hi], nt[1][:, lo:hi], -0.5, 1.5, ALU.mult, ALU.add).then_inc(root, 1)
                    dve.wait_ge(root, n + 4)
                    dve.tensor_tensor(nt[0][:, lo:hi], nt[2][:, lo:hi], rs[:, lo:hi], ALU.mult).then_inc(root, 1)
                    dve.wait_ge(root, n + 5)

                    def apply(dst, src, j):
                        return dve.tensor_scalar(dst, src, mv[:, j, 0:1], nt[0][:, j:j + 1], ALU.subtract, ALU.mult)

                    if lo == 0:
                        for i in range(QT):
                            apply(XA[:, i, :], pj[:, i, :], i).then_inc(xa_ready, 1)
                    if hi > QT:
                        past(dve, xft_ready, t)
                        for i in range(QT):
                            last = apply(XF[:, i, :], X[k][:, i, :], QT + i)
                        last.then_inc(xf_ready, 1)

                step(-1, 1, hi=QT, seen=False)
                step(0, 0, seen=False)
                step(1, 1, seen=False)
                with dve.Fori(0, NQD // 2 - 2) as t2:
                    step(2 * t2 + 2, 0)
                    step(2 * t2 + 3, 1)
                step(NQD - 2, 0)
                step(NQD - 1, 1, lo=QT)
                for t in (NQD - 2, NQD - 1):
                    for stage in range(4):
                        argmax(t, stage)

        with ExitStack() as c3:
            sb3 = lambda name, shape, dt=F32: c3.enter_context(nc.sbuf_tensor(name, shape, dt))
            sem3 = lambda name: c3.enter_context(nc.semaphore(name))
            ps3 = lambda name, shape, dt=F32: c3.enter_context(nc.psum_tensor(name, shape, dt))
            below = sb3("below", [P, P], BF16)
            ones = sb3("ones", [P, P], BF16)
            ints = sb3("ints", [P, P], I32)
            intp = sb3("intp", [P, 1], I32)
            iota = sb3("iota", [P, P])
            part = sb3("part", [P, 1])
            OH = sb3("OH", [P, NT, E], BF16)
            keep = sb3("keep", [P, E, NT])
            cum = sb3("cum", [P, E * NT])
            cnt = sb3("cnt", [P, E, NT])
            slot = sb3("slot", [P, E, NT])
            full = sb3("full", [P, E, NT])
            tiles = sb3("tiles", [P, E])
            tend = sb3("tend", [P, E])
            tbeg = sb3("tbeg", [P, E])
            dest = sb3("dest", [P, NT])
            di = sb3("di", [P, NT], I32)
            ai = sb3("ai", [P, NT], I32)
            bi = sb3("bi", [P, NT], I32)
            af = sb3("af", [P, NT])
            bf = sb3("bf", [P, NT])
            OB = sb3("OBs", [P, NT, P], BF16)
            OA = sb3("OAs", [P, NT, 3 * NS], BF16)
            sl = sb3("sl", [P, 3 * NS])
            tok = sb3("tok", [P, NS])
            gap = sb3("gap", [P, NS])
            exc = sb3("exc", [P, NS, E - 1])
            exf = sb3("exf", [P, NS])
            pfx = ps3("pfx", [P, E * NT])
            tot = ps3("tot", [P, E * NT])
            slp = ps3("slp", [P, 3 * NS])
            made = sem3("made")
            rt = sem3("rt")
            oh_ready = sem3("oh_ready")
            counts = sem3("counts")
            oab_ready = sem3("oab_ready")
            sl_ready = sem3("sl_ready")
            block = c3.enter_context(nc.Block())

            @block.gpsimd
            def _(pool):
                pool.memset(below[:, :], 1.0).then_inc(made, 1)
                pool.memset(ones[:, :], 1.0).then_inc(made, 1)
                pool.memset(keep[:, :, :], 1.0).then_inc(made, 1)
                pool.iota(ints[:, :], pattern=[[1, P]], base=0, channel_multiplier=0).then_inc(made, 1)
                pool.iota(intp[:, :], pattern=[[0, 1]], base=0, channel_multiplier=1).then_inc(made, 1)
                pool.wait_ge(made, 5)
                pool.affine_select(out=below[:, :], in_=below[:, :], compare_op=ALU.is_gt, fill=0.0, base=0,
                                   pattern=[[1, P]], channel_multiplier=-1).then_inc(made, 1)
                pool.memset(keep[:, :, 0:1], 0.0).then_inc(made, 1)

            @block.tensor
            def _(pe):
                pe.wait_ge(made, 7)
                pe.wait_ge(oh_ready, 1)
                oh = OH[:, :, :].rearrange("p t e -> p e t")
                pe.matmul(pfx[:, :], below[:, :], oh, start=True, stop=True).then_inc(counts, 1)
                pe.matmul(tot[:, :], ones[:, :], oh, start=True, stop=True).then_inc(counts, 1)
                pe.wait_ge(oab_ready, 4)
                for t in range(NT):
                    mm = pe.matmul(slp[:, :], OB[:, t, :], OA[:, t, :], start=t == 0, stop=t == NT - 1)
                mm.then_inc(sl_ready, 1)

            @block.vector
            def _(dve):
                n = [0]

                def then(ins):
                    n[0] += 1
                    ins.then_inc(rt, 1)
                    dve.wait_ge(rt, n[0])

                def over(ap, shape, axis):
                    return ap.unsqueeze(axis).broadcast_to(shape)

                dve.wait_ge(made, 7)
                dve.tensor_copy(iota[:, :], ints[:, :]).then_inc(rt, 1)
                dve.tensor_copy(part[:, :], intp[:, :]).then_inc(rt, 1)
                n[0] = 2
                dve.wait_ge(rt, n[0])
                dve.tensor_tensor(OH[:, :, :], over(ef[:, :], [P, NT, E], 2), over(iota[:, 0:E], [P, NT, E], 1),
                                  ALU.is_equal).then_inc(oh_ready, 1)
                dve.wait_ge(oh_ready, 1)
                dve.wait_ge(counts, 2)
                then(dve.tensor_tensor_scan(cum[:, :], keep[:, :, :].rearrange("p e t -> p (e t)"), tot[:, :], 0.0,
                                            ALU.mult, ALU.add))
                cv = cum[:, :].rearrange("p (e t) -> p e t", e=E)
                then(dve.tensor_tensor(cnt[:, :, :], cv, tot[:, :].rearrange("p (e t) -> p e t", e=E), ALU.subtract))
                then(dve.tensor_tensor(slot[:, :, :], cnt[:, :, :], pfx[:, :].rearrange("p (e t) -> p e t", e=E),
                                       ALU.add))
                then(dve.tensor_scalar(dest[:, :], iota[:, 0:NT], float(P), None, ALU.mult))
                then(dve.tensor_tensor(full[:, :, :], cv[:, :, NT - 1:NT].broadcast_to([P, E, NT]),
                                       over(dest[:, :], [P, E, NT], 1), ALU.is_gt))
                then(dve.tensor_reduce(tiles[:, :], full[:, :, :], AX, ALU.add))
                then(dve.tensor_tensor_scan(tend[:, :], ones[:, 0:E], tiles[:, :], 0.0, ALU.mult, ALU.add))
                then(dve.tensor_tensor(tbeg[:, :], tend[:, :], tiles[:, :], ALU.subtract))
                then(dve.scalar_tensor_tensor(out=cnt[:, :, :], in0=over(tbeg[:, :], [P, E, NT], 2), scalar=float(P),
                                              in1=slot[:, :, :], op0=ALU.mult, op1=ALU.add))
                then(dve.tensor_tensor(full[:, :, :], cnt[:, :, :], OH[:, :, :].rearrange("p t e -> p e t"),
                                       ALU.mult))
                then(dve.tensor_reduce(dest[:, :], full[:, :, :].rearrange("p e t -> p t e"), AX, ALU.add))
                then(dve.tensor_copy(di[:, :], dest[:, :]))
                then(dve.tensor_single_scalar(ai[:, :], di[:, :], 7, ALU.arith_shift_right))
                then(dve.tensor_single_scalar(bi[:, :], di[:, :], P - 1, ALU.bitwise_and))
                then(dve.tensor_copy(af[:, :], ai[:, :]))
                then(dve.tensor_copy(bf[:, :], bi[:, :]))
                dve.tensor_tensor(OB[:, :, :], over(bf[:, :], [P, NT, P], 2), over(iota[:, :], [P, NT, P], 1),
                                  ALU.is_equal).then_inc(oab_ready, 1)
                dve.tensor_tensor(OA[:, :, 0:NS], over(af[:, :], [P, NT, NS], 2), over(iota[:, 0:NS], [P, NT, NS], 1),
                                  ALU.is_equal).then_inc(oab_ready, 1)
                dve.wait_ge(oab_ready, 2)
                dve.tensor_scalar(OA[:, :, NS:2 * NS], OA[:, :, 0:NS], part[:, 0:1], None, ALU.mult)\
                   .then_inc(oab_ready, 1)
                dve.tensor_tensor(OA[:, :, 2 * NS:3 * NS], OA[:, :, 0:NS], over(iota[:, 0:NT], [P, NT, NS], 2),
                                  ALU.mult).then_inc(oab_ready, 1)
                then(dve.tensor_tensor(exc[:, :, :], over(iota[:, 0:NS], [P, NS, E - 1], 2),
                                       over(tend[:, 0:E - 1], [P, NS, E - 1], 1), ALU.is_ge))
                then(dve.tensor_reduce(exf[:, :], exc[:, :, :], AX, ALU.add))
                then(dve.tensor_copy(EX[:, :], exf[:, :]))
                dve.wait_ge(sl_ready, 1)
                then(dve.tensor_copy(sl[:, :], slp[:, :]))
                then(dve.scalar_tensor_tensor(out=tok[:, :], in0=sl[:, 2 * NS:3 * NS], scalar=float(P),
                                              in1=sl[:, NS:2 * NS], op0=ALU.mult, op1=ALU.add))
                then(dve.tensor_scalar(gap[:, :], sl[:, 0:NS], -float(NTOK), float(NTOK), ALU.mult, ALU.add))
                then(dve.tensor_tensor(exf[:, :], tok[:, :], gap[:, :], ALU.add))
                then(dve.tensor_copy(IDX[:, :], exf[:, :]))


def experts(nc, started, spare, ln_g, ln_b, b1, b2, ident, eps, Y, W1s, w1_in, W2s, w2_in, x1_dram, IDX, EX, out):
    with ExitStack() as ctx:
        sb = lambda name, shape, dt=F32: ctx.enter_context(nc.sbuf_tensor(name, shape, dt))
        sem = lambda name: ctx.enter_context(nc.semaphore(name))
        psum = lambda name, shape, dt=F32: ctx.enter_context(nc.psum_tensor(name, shape, dt))
        RING = 8
        FH = F // NQ
        NPAR = 2 * DC + FC
        PT = sb("PT", [P, NPAR, E])
        b2s = sb("b2s", [P, E * D])
        XG = sb("XG", [P, D])
        X1, XF = Y[:, 0:RING * D], Y[:, RING * D:2 * RING * D]
        XN = sb("XNf", [P, D])
        XNT = sb("XNT", [P, DC, P])
        HS = sb("HS", [P, F])
        HT = sb("HT", [P, FC, P])
        z0 = sb("z0", [P, D])
        z1 = sb("z1", [P, D])
        on = sb("on", [P, D])
        O = sb("O", [P, D])
        ig = sb("ig", [P, 1], I32)
        io = sb("io", [P, 1], I32)
        st = sb("stf", [P, 3, 6])
        mv = sb("mvf", [P, 3, 2])
        sd = sb("sdf", [P, 3])
        rs = sb("rsf", [P, 3])
        xp = psum("xp", [P, DC * P])
        hp = psum("hp", [P, F])
        tp = [psum(f"tp{k}", [P, FC // 2, P]) for k in range(2)]
        yp = psum("yp", [P, D])
        par_in = sem("par_in")
        par_t = sem("par_t")
        par_ready = sem("par_ready")
        zeroed = sem("zeroed")
        ig_set = sem("ig_set")
        gathered = sem("gathered")
        x1_kept = sem("x1_kept")
        stats = sem("stats3")
        aggr = sem("aggr3")
        rooted = sem("rooted")
        inverted = sem("inverted")
        xf_ready = sem("xf3_ready")
        xn_ready = sem("xn3_ready")
        on_ready = sem("on_ready")
        xt_ready = sem("xt2_ready")
        xnt_ready = sem("xnt_ready")
        h_ready = sem("h_ready")
        hs_ready = sem("hs_ready")
        ht_ready = sem("ht_ready")
        relued = sem("relued")
        y_ready = sem("y_ready")
        z0_ready = sem("z0_ready")
        z1_ready = sem("z1_ready")
        o_ready = sem("o_ready")
        io_set = sem("io_set")
        scattered = sem("scattered")
        AHEAD = 4

        block = ctx.enter_context(nc.Block())

        def expert(eng, t):
            return eng.value_load(EX[0:1, ds(t, 1)], min_val=0, max_val=E - 1)

        def norms_of(t):
            have = [k for k, u in enumerate((t + AHEAD, t + AHEAD - 1, t - 1)) if 0 <= u < NS]
            return have[0], have[-1] + 1

        def ring(buf, t):
            return buf[:, ds((t % RING) * D, D)]

        @block.sync
        def _(sp):
            sp.dma_start(HT[0:E, 0:DC, :].rearrange("e c p -> e (c p)"), ln_g[:, :]).then_inc(par_in, 16)
            sp.dma_start(HT[0:E, DC:2 * DC, :].rearrange("e c p -> e (c p)"), ln_b[:, :]).then_inc(par_in, 16)
            sp.dma_start(HS[0:E, :], b1[:, :]).then_inc(par_in, 16)
            sp.dma_start(b2s[:, :], b2.rearrange("(u e) d -> u (e d)", u=1).broadcast_to([P, E * D])).then_inc(par_in, 16)

        @block.gpsimd
        def _(pool):
            pool.memset(XG[:, :], 0.0).then_inc(zeroed, 1)
            pool.wait_ge(zeroed, 1)

            def gather(t):
                past(pool, x1_kept, t)
                alone(pool, spare)
                pool.tensor_copy(ig[:, :], IDX[:, ds(t, 1)]).then_inc(ig_set, 1)
                pool.wait_ge(ig_set, t + 1)
                alone(pool, spare)
                pool.indirect_dma_start(out=XG[:, :], out_offset=None, in_=x1_dram[:, :],
                                        in_offset=bass.IndirectOffsetOnAxis(ap=ig[:, :], axis=0),
                                        bounds_check=NTOK - 1, oob_is_err=False).then_inc(gathered, 16)

            def keep(t):
                pool.wait_ge(gathered, 16 * (t + 1))
                alone(pool, spare)
                pool.tensor_copy(ring(X1, t), XG[:, :]).then_inc(x1_kept, 1)

            def scatter(t):
                past(pool, scattered, 16 * t)
                alone(pool, spare)
                pool.tensor_copy(io[:, :], IDX[:, ds(t, 1)]).then_inc(io_set, 1)
                pool.wait_ge(io_set, t + 1)
                pool.wait_ge(o_ready, t + 1)
                alone(pool, spare)
                pool.indirect_dma_start(out=out.rearrange("b t d -> (b t) d"),
                                        out_offset=bass.IndirectOffsetOnAxis(ap=io[:, :], axis=0),
                                        in_=O[:, :], in_offset=None,
                                        bounds_check=NTOK - 1, oob_is_err=False).then_inc(scattered, 16)

            gather(0)
            for t in range(RING - 1):
                keep(t)
                gather(t + 1)
            keep(RING - 1)
            gather(RING)
            scatter(0)
            with pool.Fori(1, NS - RING) as t:
                keep(t + RING - 1)
                gather(t + RING)
                scatter(t)
            keep(NS - 1)
            with pool.Fori(NS - RING, NS) as t:
                scatter(t)
            pool.wait_ge(scattered, 16 * NS)

        @block.tensor
        def _(pe):
            pe.wait_ge(par_in, 64)
            for k in range(NPAR):
                src = HT[0:E, k, :] if k < 2 * DC else HS[0:E, (k - 2 * DC) * P:(k - 2 * DC + 1) * P]
                last = pe.transpose(tp[0][:, 0, k * E:(k + 1) * E], src, ident[0:E, 0:E])
            last.then_inc(par_t, 1)
            pe.wait_ge(par_ready, 1)
            pe.wait_ge(w1_in, 16 * E)
            pe.wait_ge(w2_in, 16 * E)

            def turn_x(t):
                pe.wait_ge(xn_ready, t + 1)
                past(pe, xnt_ready, DC * t)
                for c in range(DC):
                    last = pe.transpose(xp[:, c * P:(c + 1) * P], XN[:, c * P:(c + 1) * P], ident[:, :])
                last.then_inc(xt_ready, 1)

            def up(t):
                e = expert(pe, t)
                pe.wait_ge(xnt_ready, DC * (t + 1))
                past(pe, hs_ready, FH * t)
                for k in range(FH):
                    for c in range(DC):
                        mm = pe.matmul(hp[:, k * NQ:(k + 1) * NQ], XNT[:, c, :],
                                       W1s[:, c, ds(e * F + k * NQ, NQ)], start=c == 0, stop=c == DC - 1)
                    mm.then_inc(h_ready, 1)

            def turn_h(t):
                for k in range(2):
                    pe.wait_ge(hs_ready, FH * t + k + 1)
                    past(pe, relued, FC * (t - 1) + FC // 2 * (k + 1))
                    for c in range(FC // 2):
                        f = k * (FC // 2) + c
                        last = pe.transpose(tp[k][:, c, :], HS[:, f * P:(f + 1) * P], ident[:, :])
                    last.then_inc(ht_ready, 1)

            def down(t):
                e = expert(pe, t)
                past(pe, z0_ready, t)
                for f in range(FC):
                    pe.wait_ge(relued, FC * t + f + 1)
                    mm = pe.matmul(yp[:, :], HT[:, f, :], W2s[:, ds(e, 1), f * D:(f + 1) * D],
                                   start=f == 0, stop=f == FC - 1)
                mm.then_inc(y_ready, 1)

            def step(t, turn=True, more=True):
                turn_h(t)
                if turn:
                    turn_x(t + 2)
                if more:
                    up(t + 1)
                down(t)

            turn_x(0)
            up(0)
            turn_x(1)
            step(0)
            with pe.Fori(1, NS - 2) as t:
                step(t)
            step(NS - 2, False)
            step(NS - 1, False, False)

        @block.scalar
        def _(act):
            act.wait_ge(par_ready, 1)

            def roots(t, lo, hi):
                act.wait_ge(aggr, t + AHEAD + 1)
                act.activation(sd[:, lo:hi], mv[:, lo:hi, 1], ACT.Sqrt, bias=eps[:, :]).then_inc(rooted, 1)

            def copy_h(t):
                past(act, ht_ready, 2 * t)
                for k in range(FH):
                    act.wait_ge(h_ready, FH * t + k + 1)
                    act.activation(HS[:, k * NQ:(k + 1) * NQ], hp[:, k * NQ:(k + 1) * NQ], ACT.Copy)\
                       .then_inc(hs_ready, 1)

            def relu(t):
                e = expert(act, t)
                past(act, y_ready, t)
                for k in range(2):
                    act.wait_ge(ht_ready, 2 * t + k + 1)
                    for f in range(FC // 2):
                        ff = k * (FC // 2) + f
                        act.activation(HT[:, ff, :], tp[k][:, f, :], ACT.Relu,
                                       bias=PT[:, 2 * DC + ff, ds(e, 1)]).then_inc(relued, 1)

            def step(t, lo, hi, more=True):
                relu(t)
                roots(t, lo, hi)
                if more:
                    copy_h(t + 1)

            for t in range(-AHEAD, 0):
                roots(t, *norms_of(t))
            copy_h(0)
            step(0, *norms_of(0))
            with act.Fori(1, NS - AHEAD) as t:
                step(t, 0, 3)
            for t in range(NS - AHEAD, NS):
                step(t, *norms_of(t), t < NS - 1)
            roots(NS, *norms_of(NS))

        @block.vector
        def _(dve):
            dve.wait_ge(par_t, 1)
            dve.tensor_copy(PT[:, :, :].rearrange("p k e -> p (k e)"), tp[0][:, 0, 0:NPAR * E]).then_inc(par_ready, 1)
            dve.wait_ge(par_ready, 1)

            def affine(t):
                e = expert(dve, t)
                dve.wait_ge(xt_ready, t + 1)
                past(dve, h_ready, FH * t)
                for c in range(DC):
                    dve.tensor_scalar(XNT[:, c, :], xp[:, c * P:(c + 1) * P], PT[:, c, ds(e, 1)],
                                      PT[:, DC + c, ds(e, 1)], ALU.mult, ALU.add).then_inc(xnt_ready, 1)

            def step(t, lo, hi, turn=True):
                k = t + AHEAD
                a, b, c = t + AHEAD, t + AHEAD - 1, t - 1
                if lo == 0:
                    dve.wait_ge(x1_kept, a + 1)
                    past(dve, xf_ready, a)
                    alone(dve, spare)
                    last = dve.bn_stats(st[:, 0, :], ring(X1, a))
                if lo <= 1 < hi:
                    dve.wait_ge(xf_ready, b + 1)
                    past(dve, xn_ready, b)
                    alone(dve, spare)
                    last = dve.bn_stats(st[:, 1, :], ring(XF, b))
                if hi == 3:
                    e = expert(dve, c)
                    dve.wait_ge(y_ready, c + 1)
                    dve.tensor_tensor(z0[:, :], yp[:, :], b2s[:, ds(e * D, D)], ALU.add).then_inc(z0_ready, 1)
                    dve.wait_ge(z0_ready, c + 1)
                    past(dve, on_ready, c)
                    dve.tensor_tensor(z1[:, :], z0[:, :], ring(XF, c), ALU.add).then_inc(z1_ready, 1)
                    dve.wait_ge(z1_ready, c + 1)
                    alone(dve, spare)
                    last = dve.bn_stats(st[:, 2, :], z1[:, :])
                last.then_inc(stats, 1)
                dve.wait_ge(stats, k + 1)
                alone(dve, spare)
                for i in range(lo, hi):
                    last = dve.bn_aggr(mv[:, i, :], st[:, i, :])
                last.then_inc(aggr, 1)
                dve.wait_ge(rooted, k + 1)
                dve.reciprocal(rs[:, lo:hi], sd[:, lo:hi]).then_inc(inverted, 1)
                dve.wait_ge(inverted, k + 1)

                def apply(i, dst, src):
                    return dve.tensor_scalar(dst, src, mv[:, i, 0:1], rs[:, i:i + 1], ALU.subtract, ALU.mult)

                if hi == 3:
                    past(dve, o_ready, c)
                    apply(2, on[:, :], z1[:, :]).then_inc(on_ready, 1)
                if lo == 0:
                    apply(0, ring(XF, a), ring(X1, a)).then_inc(xf_ready, 1)
                if lo <= 1 < hi:
                    past(dve, xt_ready, b)
                    apply(1, XN[:, :], ring(XF, b)).then_inc(xn_ready, 1)
                if hi == 3:
                    dve.wait_ge(on_ready, c + 1)
                    past(dve, scattered, 16 * c)
                    dve.tensor_tensor(O[:, :], on[:, :], ring(X1, c), ALU.add).then_inc(o_ready, 1)
                if turn:
                    affine(t + 2)

            for t in range(-AHEAD, 2):
                step(t, *norms_of(t), t + 2 >= 0)
            with dve.Fori(2, NS - AHEAD) as t:
                step(t, 0, 3)
            for t in range(NS - AHEAD, NS + 1):
                step(t, *norms_of(t), t + 2 < NS)


_INS = ['L0_attn_x', 'L0_attn_Wc_down', 'L0_attn_Wq_up', 'L0_attn_Wkv_up', 'L0_attn_Wc_proj', 'L0_ffn_centroids',
        'L0_ffn_ln_g', 'L0_ffn_ln_b', 'L0_ffn_W1', 'L0_ffn_b1', 'L0_ffn_W2', 'L0_ffn_b2']
_OUTS = [((4, 1024, 256), 'float32')]


def kernel(**inputs):
    import numpy as _np
    import concourse.bacc as _bacc
    from concourse import mybir as _mybir
    from concourse.bass_utils import run_bass_kernel_spmd as _run

    nc = _bacc.Bacc("TRN2", target_bir_lowering=False, num_devices=1)
    arrays, args = {}, []
    for name in _INS:
        a = _np.ascontiguousarray(inputs[name])
        arrays[f"in_{name}_dram"] = a
        args.append(nc.dram_tensor(f"in_{name}_dram", a.shape, _mybir.dt.from_np(a.dtype), kind="ExternalInput").ap())
    for i, (shape, dtype) in enumerate(_OUTS):
        dt = _mybir.dt.from_np(_np.dtype(dtype))
        args.append(nc.dram_tensor(f"out_{i}_dram", shape, dt, kind="ExternalOutput").ap())
    build(nc, *args)
    r = _run(nc, [arrays], core_ids=[0])
    got = tuple(r.results[0][f"out_{i}_dram"] for i in range(len(_OUTS)))
    return got[0]
```

```python
from contextlib import ExitStack

import concourse.bass as bass
import concourse.mybir as mybir

F32 = mybir.dt.float32
BF16 = mybir.dt.bfloat16
I32 = mybir.dt.int32
U32 = mybir.dt.uint32
ALU = mybir.AluOpType
ACT = mybir.ActivationFunctionType
AX = mybir.AxisListType.X
ds = bass.ds

P = 128
B, T, D = 4, 1024, 256
NTOK = B * T
NT = NTOK // P
TB = T // P
NH, HD = 16, 16
LAT = D // 2
GH = 4
NG = NH // GH
NQ = 512
QC = T // NQ
DC = D // P
EPS = 1e-5
SCALE = 1.0 / HD ** 0.5
LOWEST = -3.0e38
E, F = 8, 1024
FC = F // P
NPAR = 2 * DC + FC
NS = NT + E - 1

QPART = (0, 0, 0, 1, 1, 2)
KPART = (0, 1, 2, 0, 1, 0)
NR = len(QPART) * HD
KR = NR + 3

STEPS = [(c, j, max(0, j - c * (NQ // P)) * P) for c in range(QC) for j in range((c + 1) * (NQ // P))]
DIAG = [s for s, (c, j, off) in enumerate(STEPS) if j >= c * (NQ // P)]
LAST = len(STEPS) - 1
UNITS = [[(h,) for h in range(GH)] if NQ - off > NQ // 2 else [(h, h + 1) for h in range(0, GH, 2)]
         for _, _, off in STEPS]
UNIT_AT = [sum(len(u) for u in UNITS[:s]) for s in range(len(STEPS) + 1)]
NU = UNIT_AT[-1]
LAG = 2
RB = 3
C0 = NQ // P - 1
BW = NQ // P
WHOLE = [(i, c, NQ, (c + 1) * BW == i + 1) for i in range(TB) for c in range((i + 1) // BW)]
RESTS = {i: (i, (i + 1) // BW, (i + 1) % BW * P, True) for i in range(TB) if (i + 1) % BW}
PAIRS = []
while RESTS:
    i, rest = RESTS.popitem()
    mate = next(k for k in RESTS if RESTS[k][2] == NQ - rest[2])
    PAIRS.append([RESTS.pop(mate), rest])
MAXES = [[m] for m in WHOLE] + PAIRS
NM = GH * len(MAXES)
MAX_AT = [round(NM * sum(NQ - o for _, _, o in STEPS[:s + 1]) / sum(NQ - o for _, _, o in STEPS))
          for s in range(len(STEPS))]
MAX_OF = [MAX_AT[s] - (MAX_AT[s - 1] if s else 0) for s in range(len(STEPS))]

PIECES = ("q00", "q01", "kv0", "kv1", "q10", "q11")
FIRST = ("kv0", "kv1", "q00", "q01", "q10", "q11")
MISC = (
    (("m", 2), ("q00", 4), ("q01", 6), ("kv0", 8), ("o0", 9)),
    (("m", 2), ("p1", 4), ("kv1", 5), ("q10", 7), ("o0", 8), ("vt", 9)),
    (("m", 2), ("p1", 4), ("q11", 6), ("o0", 8)),
    (("m", 2), ("p1", 4), ("o0", 8), ("o1", 99)),
)
MISC_FIRST = ("vt", "m")
MISC_BATCH = sum(len(m) for m in MISC)


def misc_events(g, more):
    return [(n, s) for n, s in MISC[g] if more or n in ("o0", "p1", "o1") or (n == "m" and g < NG - 1)]


def misc_at(b, g, name, more):
    before = sum(len(misc_events(k, more)) for k in range(g))
    return len(MISC_FIRST) + b * MISC_BATCH + before + [n for n, _ in misc_events(g, more)].index(name)


def beyond(t, start):
    return not isinstance(t, int) or t > start


def inside(t, end):
    return not isinstance(t, int) or t < end


def past(eng, sem, n):
    if beyond(n, 0):
        eng.wait_ge(sem, n)


def alone(eng, spare):
    eng.sem_inc(spare, 1)


def build(nc, x, Wc_down, Wq_up, Wkv_up, Wc_proj, centroids, ln_g, ln_b, W1, b1, W2, b2, out):
    nc.disable_value_cache = True
    with ExitStack() as ctx:
        sb = lambda name, shape, dt=F32: ctx.enter_context(nc.sbuf_tensor(name, shape, dt))
        sem = lambda name: ctx.enter_context(nc.semaphore(name))
        x1_rows = nc.dram_tensor("x1_rows", (NTOK, D), F32, kind="Internal").ap()
        W1s = sb("W1s", [P, DC, E * F])
        ident = sb("ident", [P, P])
        identb = sb("identb", [P, P], BF16)
        eps = sb("eps", [P, 1])
        IDX = sb("IDX", [P, NS], I32)
        EX = sb("EX", [P, NS], I32)
        spare = sem("spare")
        w1_in = sem("w1_in")
        w2_in = sem("w2_in")
        w1_v = W1.rearrange("e (c p) f -> e p c f", p=P)
        w2_v = W2.rearrange("e (c p) d -> e p c d", p=P)
        Y = sb("Y", [P, NT * D])
        attention(nc, eps, spare, x, Wc_down, Wq_up, Wkv_up, ident, identb, Y, W1s, w1_v, w1_in)
        with ExitStack() as fctx:
            W2s = fctx.enter_context(nc.sbuf_tensor("W2s", [P, E, FC * D], F32))
            PT = fctx.enter_context(nc.sbuf_tensor("PT", [P, NPAR, E], F32))
            route(nc, spare, x, Wc_proj, centroids, (ln_g, ln_b, b1), ident, eps, Y, W2s, w2_v, w2_in, x1_rows,
                  IDX, EX, PT)
            experts(nc, spare, b2, ident, eps, Y, W1s, w1_in, W2s, w2_in, x1_rows, IDX, EX, PT, out)


def attention(nc, eps, spare, x, Wc_down, Wq_up, Wkv_up, ident, identb, Y, W1s, w1_v, w1_in):
    with ExitStack() as ctx:
        sb = lambda name, shape, dt=F32: ctx.enter_context(nc.sbuf_tensor(name, shape, dt))
        sem = lambda name: ctx.enter_context(nc.semaphore(name))
        psum = lambda name, shape, dt=F32: ctx.enter_context(nc.psum_tensor(name, shape, dt))
        causal = sb("causal", [P, NQ])
        LT = sb("LT", [P, NTOK])
        Wq = sb("Wq", [P, D])
        Wkv = sb("Wkv", [P, 2 * HD])
        Q = sb("Q", [P, NH, T], BF16)
        KN = sb("KN", [P, T], BF16)
        KC = sb("KC", [P, T], BF16)
        VN = sb("VN", [P, TB, 2 * HD])
        VC = sb("VC", [P, TB, 2 * HD])
        T1, T2, T3 = (sb(f"T{k}", [P, 2, T], BF16) for k in (1, 2, 3))
        K1, K2, K3 = (sb(f"K{k}", [2 * HD, T], BF16) for k in (1, 2, 3))
        R1 = sb("R1", [P, NQ])
        KV = sb("KV", [2 * HD, T])
        MP = [sb(f"MP{k}", [P, 2, GH, TB]) for k in range(2)]
        mx = sb("mx", [P, GH * TB])
        mr = sb("mr", [P, GH * TB])
        NMX = sb("NMX", [P, 3, GH * TB], BF16)
        MT = sb("MT", [3 * GH * TB, P], BF16)
        junk = sb("junk", [P, 2, NQ], BF16)
        rden = sb("rden", [P, NQ // P, GH])

        masks_made = sem("masks_made")
        w_in = sem("w_in")
        ones_set = sem("ones_set")
        eps_set = sem("eps_set")

        with ExitStack() as c2:
            sb2 = lambda name, shape, dt=F32: c2.enter_context(nc.sbuf_tensor(name, shape, dt))
            ps2 = lambda name, shape, dt=F32: c2.enter_context(nc.psum_tensor(name, shape, dt))
            sem2 = lambda name: c2.enter_context(nc.semaphore(name))
            QT = 4
            W = QT * D
            X = Y
            XN = [sb2(f"XN{k}", [P, QT, D]) for k in range(2)]
            XT = [sb2(f"XT{k}", [P, DC, QT * P]) for k in range(2)]
            Wd = sb2("Wd", [P, DC, LAT])
            st = [sb2(f"st{k}", [P, QT, 6]) for k in range(2)]
            mv = [sb2(f"mv{k}", [P, QT, 2]) for k in range(2)]
            rs = [sb2(f"rs{k}", [P, QT]) for k in range(2)]
            sd = [sb2(f"sd{k}", [P, QT]) for k in range(2)]
            xtp = [ps2(f"xtp{k}", [P, DC, QT * P]) for k in range(2)]
            ltp = [ps2(f"ltp{k}", [P, QT * P]) for k in range(2)]
            x_in = [sem2(f"x_in{k}") for k in range(2)]
            stats = sem2("stats")
            aggr = sem2("aggr")
            sd_ready = sem2("sd_ready")
            rstd = sem2("rstd")
            xn_ready = sem2("xn_ready")
            xt_ready = sem2("xt_ready")
            xt_copied = sem2("xt_copied")
            lt_ready = sem2("lt_ready")
            lt_copied = sem2("lt_copied")
            N1 = NT // QT
            xv = x.rearrange("b (i p) d -> p (b i) d", p=P)
            block = c2.enter_context(nc.Block())

            def passes(eng, step, start=0):
                if start == 0:
                    step(0, 0)
                with eng.Fori(0, N1 // 2 - 1) as t2:
                    step(2 * t2 + 1, 1)
                    step(2 * t2 + 2, 0)
                step(N1 - 1, 1)

            @block.sync
            def _(sp):
                for t in range(N1):
                    if t >= 2:
                        sp.wait_ge(x_in[t % 2], 16 * (t // 2))
                    sp.dma_start(X[:, t * W:(t + 1) * W].rearrange("p (i d) -> p i d", d=D),
                                 xv[:, t * QT:(t + 1) * QT, :]).then_inc(x_in[t % 2], 16)
                    if t == 1:
                        sp.dma_start(Wd[:, :, :], Wc_down.rearrange("(c p) n -> p c n", p=P)).then_inc(w_in, 16)
                        sp.dma_start(Wq[:, :], Wq_up[:, :]).then_inc(w_in, 16)
                        sp.dma_start(Wkv[:, :], Wkv_up[:, :]).then_inc(w_in, 16)

            @block.gpsimd
            def _(pool):
                pool.memset(ident[:, :], 0.0).then_inc(masks_made, 1)
                pool.memset(identb[:, :], 0.0).then_inc(masks_made, 1)
                pool.memset(causal[:, :], 0.0).then_inc(masks_made, 1)
                pool.wait_ge(masks_made, 3)
                for m in (ident, identb):
                    pool.affine_select(out=m[:, :], in_=m[:, :], compare_op=ALU.not_equal, fill=1.0, base=0,
                                       pattern=[[-1, P]], channel_multiplier=1).then_inc(masks_made, 1)
                m = causal[:, NQ - P:NQ]
                pool.affine_select(out=m, in_=m, compare_op=ALU.is_ge, fill=LOWEST, base=0,
                                   pattern=[[-1, P]], channel_multiplier=1).then_inc(masks_made, 1)
                pool.memset(KN[:, :], 1.0).then_inc(ones_set, 1)
                pool.memset(VN[:, :, :], 1.0).then_inc(ones_set, 1)
                for k in range(2):
                    pool.memset(MP[k][:, :, :, :], LOWEST).then_inc(ones_set, 1)

            @block.vector
            def _(dve):
                dve.memset(eps[:, :], EPS).then_inc(eps_set, 1)

                def x_of(t, i):
                    return X[:, ds(t * W + i * D, D)]

                def statistics(t, k, seen):
                    dve.wait_ge(x_in[k], seen)
                    alone(dve, spare)
                    for i in range(QT):
                        last = dve.bn_stats(st[k][:, i, :], x_of(t, i))
                    last.then_inc(stats, 1)
                    dve.wait_ge(stats, t + 1)
                    past(dve, xn_ready, QT * (t - 1))
                    alone(dve, spare)
                    for i in range(QT):
                        last = dve.bn_aggr(mv[k][:, i, :], st[k][:, i, :])
                    last.then_inc(aggr, 1)

                def inverse(t, k):
                    dve.wait_ge(sd_ready, t + 1)
                    dve.reciprocal(rs[k][:, :], sd[k][:, :]).then_inc(rstd, 1)

                def step(t, k):
                    more = inside(t, N1 - 1)
                    if more:
                        statistics(t + 1, 1 - k, 8 * (t + 2 + k))
                    dve.wait_ge(rstd, t + 1)
                    past(dve, xt_ready, t)
                    for i in range(QT):
                        dve.tensor_scalar(XN[k][:, i, :], x_of(t, i), mv[k][:, i, 0:1], rs[k][:, i:i + 1],
                                          ALU.subtract, ALU.mult).then_inc(xn_ready, 1)
                    if more:
                        inverse(t + 1, 1 - k)

                statistics(0, 0, 16)
                inverse(0, 0)
                passes(dve, step)

            @block.tensor
            def _(pe):
                pe.wait_ge(masks_made, 6)
                pe.wait_ge(w_in, 48)
                pe.sem_inc(xt_ready, 1)

                def down(t, k):
                    pe.wait_ge(xt_copied, DC * (t + 1))
                    pe.wait_ge(lt_copied, t + 1)
                    for c in range(DC):
                        mm = pe.matmul(ltp[k][:, :], Wd[:, c, :], XT[k][:, c, :], start=c == 0, stop=c == DC - 1)
                    mm.then_inc(lt_ready, 1)

                def step(t, k):
                    for i in range(QT):
                        pe.wait_ge(xn_ready, QT * t + i + 1)
                        for c in range(DC):
                            last = pe.transpose(xtp[k][:, c, i * P:(i + 1) * P], XN[k][:, i, c * P:(c + 1) * P],
                                                ident[:, :])
                    last.then_inc(xt_ready, 1)
                    if beyond(t, 0):
                        down(t - 1, 1 - k)

                passes(pe, step)
                down(N1 - 1, 1)

            @block.scalar
            def _(act):
                act.wait_ge(eps_set, 1)

                act.sem_inc(lt_copied, 2)

                def root(t, k):
                    act.wait_ge(aggr, t + 1)
                    act.activation(sd[k][:, :], mv[k][:, :, 1], ACT.Sqrt, bias=eps[:, :]).then_inc(sd_ready, 1)

                def latent(t, k):
                    act.wait_ge(lt_ready, t + 1)
                    act.activation(LT[:, ds(t * (QT * P), QT * P)], ltp[k][:, :], ACT.Copy).then_inc(lt_copied, 1)

                def step(t, k):
                    if inside(t, N1 - 1):
                        root(t + 1, 1 - k)
                    act.wait_ge(xt_ready, t + 2)
                    for c in range(DC):
                        act.activation(XT[k][:, c, :], xtp[k][:, c, :], ACT.Copy).then_inc(xt_copied, 1)
                    if beyond(t, 0):
                        latent(t - 1, 1 - k)

                root(0, 0)
                step(0, 0)
                for e in range(E):
                    act.dma_start(W1s[:, :, e * F:(e + 1) * F], w1_v[e]).then_inc(w1_in, 16)
                passes(act, step, 1)
                latent(N1 - 1, 1)

        PR = [sb(f"PR{k}", [P, GH, NQ]) for k in range(RB)]
        OS = sb("OS", [P, NQ])
        ST = [psum(f"ST{k}", [P, NQ]) for k in range(RB)]
        SM = [psum(f"SM{k}", [P, NQ]) for k in range(RB)]
        OB = psum("OB", [P, NQ])
        misc = psum("misc", [P, NQ])

        misc_ready = sem("misc_ready")
        misc_free = sem("misc_free")
        part1 = sem("part1")
        kv_copied = sem("kv_copied")
        resid = sem("resid")
        part2 = sem("part2")
        part3 = sem("part3")
        k_in = sem("k_in")
        q_in = [[sem(f"q_in{g}_{h}") for h in range(GH)] for g in range(NG)]
        first_ready = sem("first_ready")
        m_in = [sem(f"m_in{g}") for g in range(NG)]
        v_next = sem("v_next")
        kv_now = sem("kv_now")
        sm_ready = sem("sm_ready")
        sm_done = sem("sm_done")
        m_step = sem("m_step")
        mt_ready = sem("mt_ready")
        st_ready = sem("st_ready")
        exp_done = sem("exp_done")
        masked = sem("masked")
        pv_done = sem("pv_done")
        o_copied = sem("o_copied")
        o_step = sem("o_step")
        NMS = 5

        block = ctx.enter_context(nc.Block())

        def piece_no(b, name):
            return b * len(PIECES) + PIECES.index(name) if beyond(b, 0) else FIRST.index(name)

        def is_kv(name):
            return name.startswith("kv")

        def parts(name):
            c = int(name[-1])
            if is_kv(name):
                return [t[:, c * NQ:(c + 1) * NQ] for t in (K1, K2, K3)]
            return [t[:, int(name[1]), c * NQ:(c + 1) * NQ] for t in (T1, T2, T3)]

        def rows_of(name):
            return 2 * HD if is_kv(name) else P

        def queries_in(eng, g, n, heads=range(GH)):
            for h in heads:
                eng.wait_ge(q_in[g][h], 16 * len(QPART) * n)

        def room(name, first):
            i = FIRST.index(name)
            return ((ST + SM)[i], PR[i // GH][:, i % GH, :]) if first else (misc, R1)

        def parts_sent(eng, bn, name):
            if is_kv(name):
                eng.wait_ge(k_in, 16 * len(QPART) * bn)
            else:
                for g in (2 * int(name[1]), 2 * int(name[1]) + 1):
                    queries_in(eng, g, bn)

        def loops(eng, body):
            with eng.Fori(0, B - 1) as b:
                for g in range(NG):
                    body(b, g, True)
            for g in range(NG):
                body(B - 1, g, False)

        @block.tensor
        def _(pe):
            def misc_use(k):
                past(pe, misc_free, k)

            def piece(bn, name, k, first=False):
                if not first:
                    misc_use(k)
                    alone(pe, spare)
                c = int(name[-1])
                w = Wkv[:, :] if is_kv(name) else Wq[:, int(name[1]) * P:(int(name[1]) + 1) * P]
                bank, _ = room(name, first)
                pe.matmul(bank[0:rows_of(name), :], w, LT[:, ds(bn * T + c * NQ, NQ)], start=True, stop=True)\
                  .then_inc(first_ready if first else misc_ready, 1)

            def values(bn, k):
                misc_use(k)
                pe.wait_ge(kv_copied, 2 * (bn + 1))
                alone(pe, spare)
                for j in range(TB):
                    last = pe.transpose(misc[:, j * 2 * HD:(j + 1) * 2 * HD], KV[:, j * P:(j + 1) * P],
                                        ident[0:2 * HD, 0:2 * HD])
                last.then_inc(misc_ready, 1)

            def neg_max(r, k):
                misc_use(k)
                pe.wait_ge(m_step, NMS * (r + 1))
                pe.transpose(misc[0:3 * GH * TB, 0:P // 2].bitcast(BF16), NMX[:, :, :], identb[:, :])\
                  .then_inc(misc_ready, 1)

            def maxes(r, b, g, key, n):
                if n % len(MAXES) == 0:
                    queries_in(pe, g, b + 1, [n // len(MAXES)])
                if n >= RB or beyond(r, 0):
                    pe.wait_ge(sm_done, NM * r + n - RB + 1)
                h, at = n // len(MAXES), 0
                for i, c, w, _ in MAXES[n % len(MAXES)]:
                    last = pe.matmul(SM[n % RB][:, at:at + w], Q[0:NR, g * GH + h, i * P:(i + 1) * P],
                                     key[0:NR, c * NQ:c * NQ + w], start=True, stop=True)
                    at += w
                last.then_inc(sm_ready, 1)

            def out_t(n, c, k):
                misc_use(k)
                pe.wait_ge(o_copied, QC * n + c + 1)
                for t in range(NQ // P):
                    last = pe.transpose(misc[:, t * P:(t + 1) * P], OS[:, t * P:(t + 1) * P], ident[:, :])
                last.then_inc(misc_ready, 1)

            def pv(n, s, values=None, flush=False):
                c, j, off = STEPS[s]
                if flush:
                    pe.wait_ge(exp_done, NU * n + UNIT_AT[s + 1])
                if s in DIAG:
                    pe.wait_ge(masked, len(DIAG) * n + DIAG.index(s) + 1)
                if s == C0 + 1:
                    pe.wait_ge(o_copied, QC * n + 1)
                if s == 0 and values is not None:
                    pe.wait_ge(kv_now, values)
                elif s == 0:
                    pe.wait_ge(o_copied, QC * n)
                for h in range(GH):
                    last = pe.matmul(OB[32 * h:32 * h + 32, off:NQ], VC[:, j, :], PR[s % RB][:, h, off:NQ],
                                     start=j == 0, stop=s in (C0, LAST))
                last.then_inc(pv_done, 1)

            def group(b, g, more):
                n = b * NG + g
                after = g + 2
                bm, gm, key = (b, after, KC) if after < NG else (b + 1, after - NG, KN)
                take = after < NG or more
                if gm == 0 and take:
                    pe.wait_ge(k_in, 16 * len(QPART) * (bm + 1))
                if g == 0:
                    pe.wait_ge(kv_now, 2 * b + 1)
                pe.wait_ge(m_in[g], 3 * 16 * (b + 1))
                done = 0
                for s, (c, j, off) in enumerate(STEPS):
                    for k, heads in enumerate(UNITS[s]):
                        u = NU * g + UNIT_AT[s] + k
                        if u >= RB:
                            pe.wait_ge(exp_done, NU * NG * b + u - RB + 1)
                        for h in heads:
                            at = (h - heads[0]) * (NQ - off)
                            last = pe.matmul(ST[u % RB][:, at:at + NQ - off], KC[0:KR, j * P:(j + 1) * P],
                                             Q[0:KR, g * GH + h, c * NQ + off:(c + 1) * NQ], start=True, stop=True)
                        last.then_inc(st_ready, 1)
                        if take and done < MAX_AT[s]:
                            maxes(n + 2, bm, gm, key, done)
                            done += 1
                    for name, at in misc_events(g, more):
                        k = misc_at(b, g, name, more)
                        if at == s:
                            if name == "m":
                                neg_max(n + 1, k)
                            elif name == "o0":
                                out_t(n, 0, k)
                            elif name == "p1":
                                out_t(n - 1, 1, k)
                            elif name == "vt":
                                values(b + 1, k)
                            else:
                                piece(b + 1, name, k)
                    if s >= LAG:
                        pv(n, s - LAG, None if g else 2 * (b + 1))
                    elif g:
                        pv(n - 1, len(STEPS) - LAG + s)
                    while take and done < MAX_AT[s]:
                        maxes(n + 2, bm, gm, key, done)
                        done += 1
                if g == NG - 1:
                    for s in range(len(STEPS) - LAG, len(STEPS)):
                        pv(n, s, flush=True)
                    out_t(n, 1, misc_at(b, g, "o1", more))

            pe.wait_ge(masks_made, 6)
            for name in FIRST:
                piece(0, name, None, True)
            values(0, 0)
            pe.wait_ge(k_in, 16 * len(QPART))
            pe.wait_ge(resid, len(PIECES))
            for g in range(2):
                for n in range(NM):
                    maxes(g, 0, g, KN, n)
                    if g == 1 and n == NMS:
                        neg_max(0, 1)
            loops(pe, group)

        @block.scalar
        def _(act):
            def piece(bn, name, k, first=False):
                if first:
                    act.wait_ge(first_ready, FIRST.index(name) + 1)
                else:
                    act.wait_ge(misc_ready, k + 1)
                    parts_sent(act, bn, name)
                p1, _, _ = parts(name)
                bank, _ = room(name, first)
                act.activation(p1, bank[0:rows_of(name), :], ACT.Copy).then_inc(part1, 1)
                if is_kv(name):
                    c = int(name[-1])
                    past(act, v_next, bn)
                    act.activation(KV[:, c * NQ:(c + 1) * NQ], bank[0:2 * HD, :], ACT.Copy).then_inc(kv_copied, 1)

            def piece2(bn, name, first=False):
                act.wait_ge(resid, piece_no(bn, name) + 1)
                _, p2, _ = parts(name)
                _, left = room(name, first)
                act.activation(p2, left[0:rows_of(name), :], ACT.Copy).then_inc(part2, 1)

            def out_copy(n, c, s):
                act.wait_ge(pv_done, len(STEPS) * n + s + 1)
                act.activation(OS[:, :], OB[:, :], ACT.Copy).then_inc(o_copied, 1)

            def group(b, g, more):
                n = b * NG + g
                for s, (c, j, off) in enumerate(STEPS):
                    for k, heads in enumerate(UNITS[s]):
                        u = NU * g + UNIT_AT[s] + k
                        act.wait_ge(st_ready, NU * NG * b + u + 1)
                        if k == 0 and (g or s >= RB):
                            act.wait_ge(pv_done, len(STEPS) * n + s - RB + 1)
                        act.activation(PR[s % RB][:, heads[0]:heads[-1] + 1, off:NQ],
                                       ST[u % RB][:, 0:len(heads) * (NQ - off)].rearrange("p (h q) -> p h q", h=len(heads)),
                                       ACT.Exp, scale=SCALE).then_inc(exp_done, 1)
                    for name, at in misc_events(g, more):
                        if name in PIECES and s == at:
                            piece(b + 1, name, misc_at(b, g, name, more))
                        if name in PIECES and s == at + 1:
                            piece2(b + 1, name)
                    if s == C0 + LAG:
                        out_copy(n, 0, C0)
                    if g and s == LAG - 1:
                        out_copy(n - 1, 1, LAST)
                if g == NG - 1:
                    out_copy(n, 1, LAST)

            piece(0, FIRST[0], None, True)
            for name, last in zip(FIRST[1:], FIRST):
                piece(0, name, None, True)
                piece2(0, last, True)
            piece2(0, FIRST[-1], True)
            act.wait_ge(part3, len(PIECES))
            loops(act, group)

        @block.vector
        def _(dve):
            def piece(bn, name, k, stage, first=False):
                if stage == 0:
                    dve.wait_ge(part1, piece_no(bn, name) + 1)
                    if is_kv(name):
                        dve.wait_ge(kv_copied, 2 * bn + int(name[-1]) + 1)
                    if not first:
                        dve.wait_ge(part3, piece_no(bn, name))
                    p1, _, _ = parts(name)
                    rows = rows_of(name)
                    bank, left = room(name, first)
                    dve.tensor_tensor(left[0:rows, :], bank[0:rows, :], p1, ALU.subtract).then_inc(resid, 1)
                else:
                    dve.wait_ge(resid, piece_no(bn, name) + 1)
                    dve.sem_inc(misc_free, 1)

            def values(bn, k, stage):
                if stage == 0:
                    dve.wait_ge(misc_ready, k + 1)
                    past(dve, kv_now, 2 * bn)
                    v = misc[:, 0:TB * 2 * HD].rearrange("p (j d) -> p j d", j=TB)
                    dve.tensor_copy(VN[:, :, 0:HD], v[:, :, HD:2 * HD]).then_inc(v_next, 1)
                else:
                    dve.wait_ge(v_next, bn + 1)
                    dve.sem_inc(misc_free, 1)

            def take_max(r, n, par):
                chunks = MAXES[n % len(MAXES)]
                dve.wait_ge(sm_ready, NM * r + n + 1)
                if any(diag for _, _, _, diag in chunks):
                    if n >= 2 or beyond(r, 0):
                        dve.wait_ge(sm_done, NM * r + n - 1)
                    alone(dve, spare)
                h, at = n // len(MAXES), 0
                for i, c, w, diag in chunks:
                    dst, src = MP[par][:, c, h, i:i + 1], SM[n % RB][:, at:at + w]
                    if diag:
                        op = dve.tensor_tensor_reduce(junk[:, n % 2, at:at + w], src, causal[:, NQ - w:NQ], 1.0, LOWEST,
                                                      ALU.add, ALU.max, dst)
                    else:
                        op = dve.tensor_reduce(dst, src, AX, ALU.max)
                    at += w
                op.then_inc(sm_done, 1)

            def neg_max(r, par, stage):
                if stage == 0:
                    dve.wait_ge(sm_done, NM * (r + 1))
                    past(dve, mt_ready, r)
                    m0, m1 = (MP[par][:, c, :, :].rearrange("p h i -> p (h i)") for c in range(2))
                    op = dve.tensor_tensor(mx[:, :], m0, m1, ALU.max)
                else:
                    dve.wait_ge(m_step, NMS * r + stage)
                if stage == 1:
                    op = dve.tensor_scalar(NMX[:, 0, :], mx[:, :], -1.0, None, ALU.mult)
                if stage == 2:
                    op = dve.scalar_tensor_tensor(out=mr[:, :], in0=mx[:, :], scalar=-1.0, in1=NMX[:, 0, :],
                                                  op0=ALU.mult, op1=ALU.subtract)
                if stage == 3:
                    op = dve.tensor_copy(NMX[:, 1, :], mr[:, :])
                if stage == 4:
                    op = dve.tensor_tensor(NMX[:, 2, :], mr[:, :], NMX[:, 1, :], ALU.subtract)
                op.then_inc(m_step, 1)

            def max_rows(r, g, k, stage):
                if stage == 0:
                    dve.wait_ge(misc_ready, k + 1)
                    if g is not None:
                        dve.wait_ge(m_in[g[0]], 3 * 16 * (g[1] + 1))
                    dve.tensor_copy(MT[:, :], misc[0:3 * GH * TB, 0:P // 2].bitcast(BF16)).then_inc(mt_ready, 1)
                else:
                    dve.wait_ge(mt_ready, r + 1)
                    dve.sem_inc(misc_free, 1)

            def out_norm(b, g, c, k, stage):
                o = misc[:, :].rearrange("p (t h d) -> p t h d", t=NQ // P, h=GH)
                if stage == 0:
                    dve.wait_ge(misc_ready, k + 1)
                    dve.wait_ge(misc_free, k)
                    dve.reciprocal(rden[:, :, :], o[:, :, :, HD]).then_inc(o_step, 1)
                else:
                    dve.wait_ge(o_step, QC * (b * NG + g) + c + 1)
                    y = Y[:, ds((b * TB + c * (NQ // P)) * D, (NQ // P) * D)]\
                        .rearrange("p (t h d) -> p t h d", t=NQ // P, d=HD)[:, :, g * GH:(g + 1) * GH, :]
                    rb = rden[:, :, :].rearrange("p t (h u) -> p t h u", u=1).broadcast_to([P, NQ // P, GH, HD])
                    dve.tensor_tensor(y, o[:, :, :, 0:HD], rb, ALU.mult).then_inc(misc_free, 1)

            def keys_now(b):
                dve.wait_ge(k_in, 16 * len(QPART) * (b + 1))
                past(dve, st_ready, NU * NG * b)
                dve.tensor_copy(KC[0:KR, :], KN[0:KR, :]).then_inc(kv_now, 1)

            def values_now(b):
                dve.wait_ge(v_next, b + 1)
                past(dve, pv_done, len(STEPS) * NG * b)
                dve.tensor_copy(VC[:, :, :], VN[:, :, :]).then_inc(kv_now, 1)

            def group(b, g, more):
                n = b * NG + g
                take = g + 2 < NG or more

                def use(name, stage):
                    k = misc_at(b, g, name, more)
                    if name == "m":
                        max_rows(n + 1, (g, b), k, stage)
                    elif name == "vt":
                        values(b + 1, k, stage)
                    elif name in PIECES:
                        piece(b + 1, name, k, stage)
                    else:
                        out_norm(b, g - 1 if name == "p1" else g, 0 if name == "o0" else 1, k, stage)

                have_m = g < NG - 1 or more
                done = 0
                for s in range(len(STEPS)):
                    count = MAX_OF[s] if take else 0
                    chain = NMS if have_m and s == 0 else 0
                    names = [name for name, at in misc_events(g, more) if at == s and name not in PIECES]
                    pieces = [name for name, at in misc_events(g, more) if at == s - 1 and name in PIECES]
                    for i in range(max(count, chain, 2 if names else 0)):
                        if i < count:
                            take_max(n + 2, done, g % 2)
                            done += 1
                        if i < chain:
                            neg_max(n + 1, (g + 1) % 2, i)
                        for name in pieces:
                            if i < 2:
                                use(name, i)
                        for name in names:
                            if i >= max(count, 2) - 2:
                                use(name, i - max(count, 2) + 2)
                if g == NG - 1:
                    if more:
                        keys_now(b + 1)
                        values_now(b + 1)
                    for stage in range(2):
                        use("o1", stage)

            dve.wait_ge(ones_set, 4)
            for name in FIRST:
                piece(0, name, None, 0, True)
            for stage in range(2):
                values(0, 0, stage)
            for g in range(2):
                if g == 1:
                    keys_now(0)
                    values_now(0)
                for n in range(NM):
                    take_max(g, n, g)
                    if g == 1 and n < NMS:
                        neg_max(0, 0, n)
                    if g == 1 and NMS < n < NMS + 3:
                        max_rows(0, None, 1, n - NMS - 1)
            loops(dve, group)

        @block.gpsimd
        def _(pool):
            def piece(bn, name, first=False):
                k = piece_no(bn, name)
                rows = rows_of(name)
                _, p2, p3 = parts(name)
                if not first:
                    parts_sent(pool, bn, name)
                pool.wait_ge(part2, k + 1)
                _, left = room(name, first)
                pool.tensor_tensor(p3, left[0:rows, :], p2, ALU.subtract).then_inc(part3, 1)

            def group(b, g, more):
                n = b * NG + g
                for s, (c, j, off) in enumerate(STEPS):
                    if s in DIAG:
                        pool.wait_ge(exp_done, NU * n + UNIT_AT[s + 1])
                        alone(pool, spare)
                        p = PR[s % RB][:, :, off:off + P]
                        pool.affine_select(out=p, in_=p, compare_op=ALU.is_ge, fill=0.0, base=0,
                                           pattern=[[0, GH], [1, P]], channel_multiplier=-1).then_inc(masked, 1)
                    for name, at in misc_events(g, more):
                        if s == at + 1 and name in PIECES:
                            piece(b + 1, name)

            for name in FIRST:
                piece(0, name, True)
            loops(pool, group)

        @block.sync
        def _(sp):
            def all_made(b, name):
                if beyond(b, 0):
                    sp.wait_ge(part3, piece_no(b, name) + 1)

            def made(b, name, part):
                if not beyond(b, 0):
                    sp.wait_ge((part1, part2, part3)[part], piece_no(b, name) + 1)

            def send_keys(b):
                sp.wait_ge(ones_set, 4)
                all_made(b, "kv1")
                for r, part in sorted(enumerate(KPART), key=lambda row: row[1]):
                    made(b, "kv1", part)
                    sp.dma_start(KN[r * HD:(r + 1) * HD, :], (K1, K2, K3)[part][0:HD, :]).then_inc(k_in, 16)

            def send_queries(b, g):
                half, quarter = divmod(g, 2)
                all_made(b, f"q{half}1")
                for h in range(GH):
                    row = (quarter * GH + h) * HD
                    for r, part in enumerate(QPART):
                        made(b, f"q{half}1", part)
                        sp.dma_start(Q[r * HD:(r + 1) * HD, g * GH + h, :],
                                     (T1, T2, T3)[part][row:row + HD, half, :]).then_inc(q_in[g][h], 16)

            def send_max(r, g):
                sp.wait_ge(mt_ready, r + 1)
                for a in range(3):
                    sp.dma_start(Q[NR + a:NR + a + 1, g * GH:(g + 1) * GH, :].rearrange("u h (i q) -> u (h i) q", i=TB),
                                 MT[a * GH * TB:(a + 1) * GH * TB, :]).then_inc(m_in[g], 16)

            def group(b, g, more):
                n = b * NG + g
                if g < NG - 1:
                    send_max(n + 1, g + 1)
                elif more:
                    send_max(n + 1, 0)
                if more:
                    if g == 1:
                        sp.wait_ge(kv_now, 2 * (b + 1))
                        alone(sp, spare)
                        send_keys(b + 1)
                    sp.wait_ge(exp_done, NU * (n + 1))
                    alone(sp, spare)
                    send_queries(b + 1, g)

            send_keys(0)
            for g in range(2):
                send_queries(0, g)
            send_max(0, 0)
            for g in range(2, NG):
                send_queries(0, g)
            loops(sp, group)


def route(nc, spare, x, Wc_proj, centroids, params, ident, eps, Y, W2s, w2_v, w2_in, x1_rows, IDX, EX, PT):
    with ExitStack() as ctx:
        sb = lambda name, shape, dt=F32: ctx.enter_context(nc.sbuf_tensor(name, shape, dt))
        sem = lambda name: ctx.enter_context(nc.semaphore(name))
        psum = lambda name, shape, dt=F32: ctx.enter_context(nc.psum_tensor(name, shape, dt))
        QT = 4
        NQD = NT // QT
        CT = sb("CT", [P, DC, E])
        ef = sb("ef", [P, NT])
        G = sb("G", [E, NPAR * P])
        below = sb("below", [P, P], BF16)
        ones = sb("ones", [P, P], BF16)
        ints = sb("ints", [P, P], I32)
        intp = sb("intp", [P, 1], I32)
        keep = sb("keep", [P, E, NT])
        par_in = sem("par_in")
        made = sem("made")
        with ExitStack() as c2:
            sb2 = lambda name, shape, dt=F32: c2.enter_context(nc.sbuf_tensor(name, shape, dt))
            sem2 = lambda name: c2.enter_context(nc.semaphore(name))
            ps2 = lambda name, shape, dt=F32: c2.enter_context(nc.psum_tensor(name, shape, dt))
            YS = sb2("YS", [P, QT, D])
            YT = sb2("YT", [P, DC, QT * P])
            Wp = sb2("Wp", [P, DC, D])
            Cn = sb2("Cn", [E, D])
            X = [sb2(f"XQ{k}", [P, QT, D]) for k in range(2)]
            XA = sb2("XA", [P, QT, D])
            XF = sb2("XF", [P, QT, D])
            XFT = sb2("XFT", [P, DC, QT * P])
            st = sb2("st2", [P, 2 * QT, 6])
            mv = sb2("mv2", [P, 2 * QT, 2])
            sd = sb2("sd2", [P, 2 * QT])
            rs = sb2("rs2", [P, 2 * QT])
            nt = [sb2(f"nt{k}", [P, 2 * QT]) for k in range(3)]
            shift = sb2("shift", [P, QT])
            m8 = sb2("m8", [P, QT, 8])
            i8 = sb2("i8", [P, QT, 8], U32)
            lg = sb2("lg", [P, QT, E])
            ytp = ps2("ytp", [P, QT * P])
            pj = [ps2(f"pj{k}", [P, QT, D]) for k in range(2)]
            xtp = [ps2(f"xftp{c}", [P, QT * P]) for c in range(DC)]
            lgp = ps2("lgp", [P, QT * E])
            w_in = sem2("wp_in")
            c_ready = sem2("c_ready")
            c_copied = sem2("c_copied")
            x_in = [sem2(f"xq_in{k}") for k in range(2)]
            ys_ready = sem2("ys_ready")
            yt_ready = sem2("yt_ready")
            yt_copied = sem2("yt_copied")
            pj_ready = sem2("pj_ready")
            stats = sem2("stats2")
            aggr = sem2("aggr2")
            sd_ready = sem2("sd2_ready")
            root = sem2("root2")
            shifted = sem2("shifted")
            xa_ready = sem2("xa_ready")
            x1_ready = sem2("x1_ready")
            x1_out = [sem2(f"x1_out{k}") for k in range(2)]
            xf_ready = sem2("xf_ready")
            xft_ready = sem2("xft_ready")
            xft_copied = sem2("xft_copied")
            lg_ready = sem2("lg_ready")
            top = sem2("top")
            xv = x.rearrange("b (i p) d -> p (b i) d", p=P)
            x1v = x1_rows.rearrange("(i p) d -> p i d", p=P)
            ROOT = 5
            TOP = 2 * QT + 2

            def steps(eng, step):
                step(0, 0)
                with eng.Fori(0, NQD // 2 - 2) as t2:
                    step(2 * t2 + 1, 1)
                    step(2 * t2 + 2, 0)
                for t in range(NQD - 3, NQD):
                    step(t, t % 2)

            block = c2.enter_context(nc.Block())

            @block.sync
            def _(sp):
                sp.dma_start(Wp[:, :, :], Wc_proj.rearrange("(c p) n -> p c n", p=P)).then_inc(w_in, 16)
                sp.dma_start(Cn[:, :], centroids[:, :]).then_inc(w_in, 16)
                for k in range(2):
                    sp.dma_start(X[k][:, :, :], xv[:, k * QT:(k + 1) * QT, :]).then_inc(x_in[k], 16)

                for t in range(NQD):
                    k = t % 2
                    sp.wait_ge(x1_ready, QT * (t + 1))
                    sp.dma_start(x1v[:, t * QT:(t + 1) * QT, :], X[k][:, :, :]).then_inc(x1_out[k], 16)
                    if t + 2 < NQD:
                        sp.wait_ge(x1_out[k], 16 * (t // 2 + 1))
                        sp.wait_ge(xf_ready, t + 1)
                        sp.dma_start(X[k][:, :, :], xv[:, (t + 2) * QT:(t + 3) * QT, :]).then_inc(x_in[k], 16)
                at = 0
                for part in params:
                    sp.dma_start(G[:, at:at + part.shape[1]], part[:, :]).then_inc(par_in, 16)
                    at += part.shape[1]
                for k in range(2):
                    sp.wait_ge(x1_out[k], 16 * (NQD // 2))

            @block.gpsimd
            def _(pool):
                pool.memset(below[:, :], 1.0).then_inc(made, 1)
                pool.memset(ones[:, :], 1.0).then_inc(made, 1)
                pool.memset(keep[:, :, :], 1.0).then_inc(made, 1)
                pool.iota(ints[:, :], pattern=[[1, P]], base=0, channel_multiplier=0).then_inc(made, 1)
                pool.iota(intp[:, :], pattern=[[0, 1]], base=0, channel_multiplier=1).then_inc(made, 1)
                pool.wait_ge(made, 5)
                pool.affine_select(out=below[:, :], in_=below[:, :], compare_op=ALU.is_gt, fill=0.0, base=0,
                                   pattern=[[1, P]], channel_multiplier=-1).then_inc(made, 1)
                pool.memset(keep[:, :, 0:1], 0.0).then_inc(made, 1)
                with pool.Fori(0, NQD // 2) as t2:
                    for k in range(2):
                        t = 2 * t2 + k
                        pool.wait_ge(x_in[k], 16 * (t2 + 1))
                        for i in range(QT):
                            pool.wait_ge(xa_ready, QT * t + i + 1)
                            pool.tensor_tensor(X[k][:, i, :], X[k][:, i, :], XA[:, i, :], ALU.add)\
                                .then_inc(x1_ready, 1)

            @block.tensor
            def _(pe):
                pe.wait_ge(w_in, 32)
                for c in range(DC):
                    last = pe.transpose(lgp[:, c * E:(c + 1) * E], Cn[:, c * P:(c + 1) * P], ident[0:E, 0:E])
                last.then_inc(c_ready, 1)

                def turn_y(t, c):
                    pe.wait_ge(ys_ready, t + 1)
                    past(pe, yt_copied, DC * t + c)
                    for i in range(QT):
                        last = pe.transpose(ytp[:, i * P:(i + 1) * P], YS[:, i, c * P:(c + 1) * P], ident[:, :])
                    last.then_inc(yt_ready, 1)

                def project(t, k):
                    pe.wait_ge(yt_copied, DC * (t + 1))
                    past(pe, xa_ready, QT * (t - 1))
                    for i in range(QT):
                        for c in range(DC):
                            mm = pe.matmul(pj[k][:, i, :], YT[:, c, i * P:(i + 1) * P], Wp[:, c, :],
                                           start=c == 0, stop=c == DC - 1)
                    mm.then_inc(pj_ready, 1)

                def turn_x(t):
                    pe.wait_ge(xf_ready, t + 1)
                    for c in range(DC):
                        for i in range(QT):
                            last = pe.transpose(xtp[c][:, i * P:(i + 1) * P], XF[:, i, c * P:(c + 1) * P], ident[:, :])
                    last.then_inc(xft_ready, 1)

                def logits(t):
                    pe.wait_ge(xft_copied, DC * (t + 1))
                    past(pe, top, TOP * (t - 1) + 2)
                    for i in range(QT):
                        for c in range(DC):
                            mm = pe.matmul(lgp[:, i * E:(i + 1) * E], XFT[:, c, i * P:(i + 1) * P], CT[:, c, :],
                                           start=c == 0, stop=c == DC - 1)
                    mm.then_inc(lg_ready, 1)

                def step(t, k):
                    if inside(t + 2, NQD):
                        project(t + 2, k)
                    turn = inside(t + 3, NQD)
                    if turn:
                        turn_y(t + 3, 0)
                    turn_x(t)
                    if turn:
                        turn_y(t + 3, 1)
                    logits(t)

                for t in range(3):
                    for c in range(DC):
                        turn_y(t, c)
                    if t < 2:
                        project(t, t)
                pe.wait_ge(c_copied, 1)
                steps(pe, step)

            @block.scalar
            def _(act):
                def ys(t):
                    past(act, yt_ready, DC * t)
                    act.activation(YS[:, :, :].rearrange("p t d -> p (t d)"), Y[:, ds(t * (QT * D), QT * D)],
                                   ACT.Copy).then_inc(ys_ready, 1)

                def yt(t, c):
                    act.wait_ge(yt_ready, DC * t + c + 1)
                    past(act, pj_ready, t)
                    act.activation(YT[:, c, :], ytp[:, :], ACT.Copy).then_inc(yt_copied, 1)

                def xft(t):
                    act.wait_ge(xft_ready, t + 1)
                    past(act, lg_ready, t)
                    for c in range(DC):
                        act.activation(XFT[:, c, :], xtp[c][:, :], ACT.Copy).then_inc(xft_copied, 1)

                def roots(t, lo, hi):
                    act.wait_ge(aggr, t + 2)
                    act.activation(sd[:, lo:hi], mv[:, lo:hi, 1], ACT.Sqrt, bias=eps[:, :]).then_inc(sd_ready, 1)

                def apply(t, k):
                    act.wait_ge(shifted, t + 1)
                    past(act, x1_ready, QT * t)
                    for i in range(QT):
                        act.activation(XA[:, i, :], pj[k][:, i, :], ACT.Identity, scale=nt[0][:, i:i + 1],
                                       bias=shift[:, i:i + 1]).then_inc(xa_ready, 1)

                def step(t, k):
                    more = inside(t, NQD - 1)
                    turn = inside(t + 3, NQD)
                    if turn:
                        ys(t + 3)
                    roots(t, 0 if more else QT, 2 * QT)
                    if more:
                        apply(t + 1, 1 - k)
                    if turn:
                        yt(t + 3, 0)
                    xft(t)
                    if turn:
                        yt(t + 3, 1)

                ys(0)
                yt(0, 0)
                yt(0, 1)
                ys(1)
                for e in range(E):
                    act.dma_start(W2s[:, e, :].rearrange("p (c d) -> p c d", c=FC), w2_v[e]).then_inc(w2_in, 16)
                yt(1, 0)
                yt(1, 1)
                ys(2)
                roots(-1, 0, QT)
                apply(0, 0)
                yt(2, 0)
                yt(2, 1)
                steps(act, step)

            @block.vector
            def _(dve):
                dve.sem_inc(top, 1)
                dve.wait_ge(c_ready, 1)
                dve.tensor_copy(CT[:, :, :].rearrange("p c e -> p (c e)"), lgp[:, 0:DC * E]).then_inc(c_copied, 1)

                def argmax(t, stage):
                    base = TOP * t + 1
                    if stage == 0:
                        dve.wait_ge(lg_ready, t + 1)
                        dve.wait_ge(top, base)
                        dve.tensor_copy(lg[:, :, :].rearrange("p t e -> p (t e)"), lgp[:, :]).then_inc(top, 1)
                    if stage == 1:
                        dve.wait_ge(top, base + 1)
                        alone(dve, spare)
                        for i in range(QT):
                            dve.max(m8[:, i, :], lg[:, i, :]).then_inc(top, 1)
                    if stage == 2:
                        dve.wait_ge(top, base + 1 + QT)
                        alone(dve, spare)
                        for i in range(QT):
                            dve.max_index(i8[:, i, :], m8[:, i, :], lg[:, i, :]).then_inc(top, 1)
                    if stage == 3:
                        dve.wait_ge(top, base + 1 + 2 * QT)
                        dve.tensor_copy(ef[:, ds(t * QT, QT)], i8[:, :, 0]).then_inc(top, 1)

                def step(t, k, lo=0, hi=2 * QT, seen=True):
                    if seen:
                        argmax(t - 2, 0)
                    if hi > QT:
                        past(dve, xa_ready, QT * (t + 1))
                        past(dve, xf_ready, t)
                        for i in range(QT):
                            dve.wait_ge(x1_ready, QT * t + i + 1)
                            alone(dve, spare)
                            last = dve.bn_stats(st[:, QT + i, :], X[k][:, i, :])
                            if seen and i:
                                argmax(t - 2, i)
                    if lo == 0:
                        dve.wait_ge(pj_ready, t + 2)
                        alone(dve, spare)
                        for i in range(QT):
                            last = dve.bn_stats(st[:, i, :], pj[1 - k][:, i, :])
                    last.then_inc(stats, 1)
                    dve.wait_ge(stats, t + 2)
                    alone(dve, spare)
                    for i in range(lo, hi):
                        last = dve.bn_aggr(mv[:, i, :], st[:, i, :])
                    last.then_inc(aggr, 1)
                    n = ROOT * (t + 1)
                    dve.wait_ge(sd_ready, t + 2)
                    dve.reciprocal(rs[:, lo:hi], sd[:, lo:hi]).then_inc(root, 1)
                    dve.wait_ge(root, n + 1)
                    dve.scalar_tensor_tensor(out=nt[0][:, lo:hi], in0=mv[:, lo:hi, 1], scalar=EPS, in1=rs[:, lo:hi],
                                             op0=ALU.add, op1=ALU.mult).then_inc(root, 1)
                    dve.wait_ge(root, n + 2)
                    dve.tensor_tensor(nt[1][:, lo:hi], nt[0][:, lo:hi], rs[:, lo:hi], ALU.mult).then_inc(root, 1)
                    dve.wait_ge(root, n + 3)
                    dve.tensor_scalar(nt[2][:, lo:hi], nt[1][:, lo:hi], -0.5, 1.5, ALU.mult, ALU.add).then_inc(root, 1)
                    dve.wait_ge(root, n + 4)
                    dve.tensor_tensor(nt[0][:, lo:hi], nt[2][:, lo:hi], rs[:, lo:hi], ALU.mult).then_inc(root, 1)
                    dve.wait_ge(root, n + 5)

                    def apply(dst, src, j):
                        return dve.tensor_scalar(dst, src, mv[:, j, 0:1], nt[0][:, j:j + 1], ALU.subtract, ALU.mult)

                    if lo == 0:
                        dve.scalar_tensor_tensor(out=shift[:, :], in0=mv[:, 0:QT, 0], scalar=-1.0, in1=nt[0][:, 0:QT],
                                                 op0=ALU.mult, op1=ALU.mult).then_inc(shifted, 1)
                    if hi > QT:
                        past(dve, xft_ready, t)
                        for i in range(QT):
                            last = apply(XF[:, i, :], X[k][:, i, :], QT + i)
                        last.then_inc(xf_ready, 1)

                step(-1, 1, hi=QT, seen=False)
                step(0, 0, seen=False)
                step(1, 1, seen=False)
                with dve.Fori(0, NQD // 2 - 2) as t2:
                    step(2 * t2 + 2, 0)
                    step(2 * t2 + 3, 1)
                step(NQD - 2, 0)
                step(NQD - 1, 1, lo=QT)
                for t in (NQD - 2, NQD - 1):
                    for stage in range(4):
                        argmax(t, stage)

        with ExitStack() as c3:
            sb3 = lambda name, shape, dt=F32: c3.enter_context(nc.sbuf_tensor(name, shape, dt))
            sem3 = lambda name: c3.enter_context(nc.semaphore(name))
            ps3 = lambda name, shape, dt=F32: c3.enter_context(nc.psum_tensor(name, shape, dt))
            iota = sb3("iota", [P, P])
            part = sb3("part", [P, 1])
            OH = sb3("OH", [P, NT, E], BF16)
            cum = sb3("cum", [P, E * NT])
            cnt = sb3("cnt", [P, E, NT])
            slot = sb3("slot", [P, E, NT])
            full = sb3("full", [P, E, NT])
            tiles = sb3("tiles", [P, E])
            tend = sb3("tend", [P, E])
            tbeg = sb3("tbeg", [P, E])
            dest = sb3("dest", [P, NT])
            di = sb3("di", [P, NT], I32)
            ai = sb3("ai", [P, NT], I32)
            bi = sb3("bi", [P, NT], I32)
            af = sb3("af", [P, NT])
            bf = sb3("bf", [P, NT])
            OB = sb3("OBs", [P, NT, P], BF16)
            OA = sb3("OAs", [P, NT, 3 * NS], BF16)
            sl = sb3("sl", [P, 3 * NS])
            tok = sb3("tok", [P, NS])
            gap = sb3("gap", [P, NS])
            exc = sb3("exc", [P, NS, E - 1])
            exf = sb3("exf", [P, NS])
            pfx = ps3("pfx", [P, E * NT])
            tot = ps3("tot", [P, E * NT])
            slp = ps3("slp", [P, 3 * NS])
            ptp = ps3("ptp", [P, NPAR * E])
            par_t = sem3("par_t")
            rt = sem3("rt")
            oh_ready = sem3("oh_ready")
            counts = sem3("counts")
            oa_ready = sem3("oa_ready")
            ob_ready = sem3("ob_ready")
            OBT = 8
            sl_ready = sem3("sl_ready")
            block = c3.enter_context(nc.Block())

            @block.tensor
            def _(pe):
                pe.wait_ge(par_in, 48)
                for k in range(NPAR):
                    last = pe.transpose(ptp[:, k * E:(k + 1) * E], G[:, k * P:(k + 1) * P], ident[0:E, 0:E])
                last.then_inc(par_t, 1)
                pe.wait_ge(made, 7)
                pe.wait_ge(oh_ready, 1)
                oh = OH[:, :, :].rearrange("p t e -> p e t")
                pe.matmul(pfx[:, :], below[:, :], oh, start=True, stop=True).then_inc(counts, 1)
                pe.matmul(tot[:, :], ones[:, :], oh, start=True, stop=True).then_inc(counts, 1)
                pe.wait_ge(oa_ready, 3)
                for t in range(NT):
                    if t % OBT == 0:
                        pe.wait_ge(ob_ready, t // OBT + 1)
                    mm = pe.matmul(slp[:, :], OB[:, t, :], OA[:, t, :], start=t == 0, stop=t == NT - 1)
                mm.then_inc(sl_ready, 1)

            @block.vector
            def _(dve):
                n = [0]

                def then(ins):
                    n[0] += 1
                    ins.then_inc(rt, 1)
                    dve.wait_ge(rt, n[0])

                def over(ap, shape, axis):
                    return ap.unsqueeze(axis).broadcast_to(shape)

                dve.wait_ge(made, 7)
                dve.tensor_copy(iota[:, :], ints[:, :]).then_inc(rt, 1)
                dve.tensor_copy(part[:, :], intp[:, :]).then_inc(rt, 1)
                n[0] = 2
                dve.wait_ge(rt, n[0])
                dve.tensor_tensor(OH[:, :, :], over(ef[:, :], [P, NT, E], 2), over(iota[:, 0:E], [P, NT, E], 1),
                                  ALU.is_equal).then_inc(oh_ready, 1)
                dve.wait_ge(oh_ready, 1)
                dve.wait_ge(counts, 2)
                then(dve.tensor_tensor_scan(cum[:, :], keep[:, :, :].rearrange("p e t -> p (e t)"), tot[:, :], 0.0,
                                            ALU.mult, ALU.add))
                cv = cum[:, :].rearrange("p (e t) -> p e t", e=E)
                then(dve.tensor_tensor(cnt[:, :, :], cv, tot[:, :].rearrange("p (e t) -> p e t", e=E), ALU.subtract))
                then(dve.tensor_tensor(slot[:, :, :], cnt[:, :, :], pfx[:, :].rearrange("p (e t) -> p e t", e=E),
                                       ALU.add))
                then(dve.tensor_scalar(dest[:, :], iota[:, 0:NT], float(P), None, ALU.mult))
                then(dve.tensor_tensor(full[:, :, :], cv[:, :, NT - 1:NT].broadcast_to([P, E, NT]),
                                       over(dest[:, :], [P, E, NT], 1), ALU.is_gt))
                then(dve.tensor_reduce(tiles[:, :], full[:, :, :], AX, ALU.add))
                then(dve.tensor_tensor_scan(tend[:, :], ones[:, 0:E], tiles[:, :], 0.0, ALU.mult, ALU.add))
                then(dve.tensor_tensor(tbeg[:, :], tend[:, :], tiles[:, :], ALU.subtract))
                then(dve.scalar_tensor_tensor(out=cnt[:, :, :], in0=over(tbeg[:, :], [P, E, NT], 2), scalar=float(P),
                                              in1=slot[:, :, :], op0=ALU.mult, op1=ALU.add))
                then(dve.tensor_tensor(full[:, :, :], cnt[:, :, :], OH[:, :, :].rearrange("p t e -> p e t"),
                                       ALU.mult))
                then(dve.tensor_reduce(dest[:, :], full[:, :, :].rearrange("p e t -> p t e"), AX, ALU.add))
                then(dve.tensor_copy(di[:, :], dest[:, :]))
                then(dve.tensor_single_scalar(ai[:, :], di[:, :], 7, ALU.arith_shift_right))
                then(dve.tensor_single_scalar(bi[:, :], di[:, :], P - 1, ALU.bitwise_and))
                then(dve.tensor_copy(af[:, :], ai[:, :]))
                then(dve.tensor_copy(bf[:, :], bi[:, :]))
                dve.tensor_tensor(OA[:, :, 0:NS], over(af[:, :], [P, NT, NS], 2), over(iota[:, 0:NS], [P, NT, NS], 1),
                                  ALU.is_equal).then_inc(oa_ready, 1)
                dve.wait_ge(oa_ready, 1)
                dve.tensor_scalar(OA[:, :, NS:2 * NS], OA[:, :, 0:NS], part[:, 0:1], None, ALU.mult)\
                   .then_inc(oa_ready, 1)
                dve.tensor_tensor(OA[:, :, 2 * NS:3 * NS], OA[:, :, 0:NS], over(iota[:, 0:NT], [P, NT, NS], 2),
                                  ALU.mult).then_inc(oa_ready, 1)
                for t in range(0, NT, OBT):
                    dve.tensor_tensor(OB[:, t:t + OBT, :], over(bf[:, t:t + OBT], [P, OBT, P], 2),
                                      over(iota[:, :], [P, OBT, P], 1), ALU.is_equal).then_inc(ob_ready, 1)
                then(dve.tensor_tensor(exc[:, :, :], over(iota[:, 0:NS], [P, NS, E - 1], 2),
                                       over(tend[:, 0:E - 1], [P, NS, E - 1], 1), ALU.is_ge))
                then(dve.tensor_reduce(exf[:, :], exc[:, :, :], AX, ALU.add))
                then(dve.tensor_copy(EX[:, :], exf[:, :]))
                dve.wait_ge(par_t, 1)
                then(dve.tensor_copy(PT[:, :, :].rearrange("p k e -> p (k e)"), ptp[:, :]))
                dve.wait_ge(sl_ready, 1)
                then(dve.tensor_copy(sl[:, :], slp[:, :]))
                then(dve.scalar_tensor_tensor(out=tok[:, :], in0=sl[:, 2 * NS:3 * NS], scalar=float(P),
                                              in1=sl[:, NS:2 * NS], op0=ALU.mult, op1=ALU.add))
                then(dve.tensor_scalar(gap[:, :], sl[:, 0:NS], -float(NTOK), float(NTOK), ALU.mult, ALU.add))
                then(dve.tensor_tensor(exf[:, :], tok[:, :], gap[:, :], ALU.add))
                then(dve.tensor_copy(IDX[:, :], exf[:, :]))


def experts(nc, spare, b2, ident, eps, Y, W1s, w1_in, W2s, w2_in, x1_rows, IDX, EX, PT, out):
    with ExitStack() as ctx:
        sb = lambda name, shape, dt=F32: ctx.enter_context(nc.sbuf_tensor(name, shape, dt))
        sem = lambda name: ctx.enter_context(nc.semaphore(name))
        psum = lambda name, shape, dt=F32: ctx.enter_context(nc.psum_tensor(name, shape, dt))
        RING = 8
        FH = F // NQ
        b2s = sb("b2s", [P, E * D])
        XG = sb("XG", [P, D])
        X1, XF = Y[:, 0:RING * D], Y[:, RING * D:2 * RING * D]
        XN = sb("XNf", [P, D])
        XNT = sb("XNT", [P, DC, P])
        WS = sb("WS", [P, DC, F])
        HT = [sb(f"HT{k}", [P, FC, P]) for k in range(2)]
        z0 = sb("z0", [P, D])
        z1 = sb("z1", [P, D])
        on = sb("on", [P, D])
        O = sb("O", [P, D])
        ig = sb("ig", [P, 1], I32)
        ig0 = sb("ig0", [P, RING], I32)
        io = sb("io", [P, 1], I32)
        st = sb("stf", [P, 3, 6])
        mv = sb("mvf", [P, 3, 2])
        sd = sb("sdf", [P, 3])
        rs = sb("rsf", [P, 3])
        xp = psum("xp", [P, DC * P])
        hp = [[psum(f"hp{k}{i}", [P, FC // 2, P]) for i in range(FH)] for k in range(2)]
        yp = psum("yp", [P, D])
        b2_in = sem("b2_in")
        first_x = [sem(f"first_x{t}") for t in range(RING)]
        zeroed = sem("zeroed")
        ig_set = sem("ig_set")
        gathered = sem("gathered")
        x1_kept = sem("x1_kept")
        stats = sem("stats3")
        aggr = sem("aggr3")
        rooted = sem("rooted")
        inverted = sem("inverted")
        xf_ready = sem("xf3_ready")
        xn_ready = sem("xn3_ready")
        on_ready = sem("on_ready")
        xt_ready = sem("xt2_ready")
        xnt_ready = sem("xnt_ready")
        h_ready = sem("h_ready")
        ws_ready = sem("ws_ready")
        relued = sem("relued")
        y_ready = sem("y_ready")
        z0_ready = sem("z0_ready")
        z1_ready = sem("z1_ready")
        o_ready = sem("o_ready")
        io_set = sem("io_set")
        scattered = sem("scattered")
        AHEAD = 4

        block = ctx.enter_context(nc.Block())

        def expert(eng, t):
            return eng.value_load(EX[0:1, ds(t, 1)], min_val=0, max_val=E - 1)

        def norms_of(t):
            have = [k for k, u in enumerate((t + AHEAD, t + AHEAD - 1, t - 1)) if 0 <= u < NS]
            return have[0], have[-1] + 1

        def steps(eng, step, first, end):
            for t in range(first):
                step(t, t % 2)
            with eng.Fori(0, (end - first) // 2) as t2:
                for i in range(first, first + 2):
                    step(2 * t2 + i, i % 2)
            for t in range(first + (end - first) // 2 * 2, NS):
                step(t, t % 2)

        def ring(buf, t):
            return buf[:, ds((t % RING) * D, D)]

        @block.sync
        def _(sp):
            sp.dma_start(b2s[:, :], b2.rearrange("(u e) d -> u (e d)", u=1).broadcast_to([P, E * D])).then_inc(b2_in, 16)

        @block.gpsimd
        def _(pool):
            pool.memset(XG[:, :], 0.0).then_inc(zeroed, 1)
            pool.wait_ge(zeroed, 1)

            def gather(t):
                pool.wait_ge(x1_kept, t)
                alone(pool, spare)
                pool.tensor_copy(ig[:, :], IDX[:, ds(t, 1)]).then_inc(ig_set, 1)
                pool.wait_ge(ig_set, t - RING + 2)
                alone(pool, spare)
                pool.indirect_dma_start(out=XG[:, :], out_offset=None, in_=x1_rows[:, :],
                                        in_offset=bass.IndirectOffsetOnAxis(ap=ig[:, :], axis=0),
                                        bounds_check=NTOK - 1, oob_is_err=False).then_inc(gathered, 16)

            def keep(t):
                pool.wait_ge(gathered, 16 * (t - RING + 1))
                alone(pool, spare)
                pool.tensor_copy(ring(X1, t), XG[:, :]).then_inc(x1_kept, 1)

            def scatter(t):
                past(pool, scattered, 16 * t)
                alone(pool, spare)
                pool.tensor_copy(io[:, :], IDX[:, ds(t, 1)]).then_inc(io_set, 1)
                pool.wait_ge(io_set, t + 1)
                pool.wait_ge(o_ready, t + 1)
                alone(pool, spare)
                pool.indirect_dma_start(out=out.rearrange("b t d -> (b t) d"),
                                        out_offset=bass.IndirectOffsetOnAxis(ap=io[:, :], axis=0),
                                        in_=O[:, :], in_offset=None,
                                        bounds_check=NTOK - 1, oob_is_err=False).then_inc(scattered, 16)

            pool.tensor_copy(ig0[:, :], IDX[:, 0:RING]).then_inc(ig_set, 1)
            pool.wait_ge(ig_set, 1)
            for t in range(RING):
                pool.indirect_dma_start(out=X1[:, t * D:(t + 1) * D], out_offset=None, in_=x1_rows[:, :],
                                        in_offset=bass.IndirectOffsetOnAxis(ap=ig0[:, t:t + 1], axis=0),
                                        bounds_check=NTOK - 1, oob_is_err=False).then_inc(first_x[t], 16)
            for t in range(RING):
                pool.wait_ge(first_x[t], 16)
                pool.sem_inc(x1_kept, 1)
            gather(RING)
            scatter(0)
            with pool.Fori(1, NS - RING) as t:
                keep(t + RING - 1)
                gather(t + RING)
                scatter(t)
            keep(NS - 1)
            with pool.Fori(NS - RING, NS) as t:
                scatter(t)
            pool.wait_ge(scattered, 16 * NS)

        @block.tensor
        def _(pe):
            pe.wait_ge(w2_in, 16 * E)

            def turn_x(t):
                pe.wait_ge(xn_ready, t + 1)
                past(pe, xnt_ready, DC * t)
                for c in range(DC):
                    last = pe.transpose(xp[:, c * P:(c + 1) * P], XN[:, c * P:(c + 1) * P], ident[:, :])
                last.then_inc(xt_ready, 1)

            def up(t, k):
                pe.wait_ge(xnt_ready, DC * (t + 1))
                for i in range(FH):
                    pe.wait_ge(ws_ready, FH * t + i + 1)
                    for f in range(FC // FH):
                        at = (i * (FC // FH) + f) * P
                        for c in range(DC):
                            mm = pe.matmul(hp[k][i][:, f, :], WS[:, c, at:at + P], XNT[:, c, :],
                                           start=c == 0, stop=c == DC - 1)
                    mm.then_inc(h_ready, 1)

            def down(t, k, e):
                past(pe, z0_ready, t)
                pe.wait_ge(relued, FC * (t + 1))
                for f in range(FC):
                    mm = pe.matmul(yp[:, :], HT[k][:, f, :], W2s[:, ds(e, 1), f * D:(f + 1) * D],
                                   start=f == 0, stop=f == FC - 1)
                mm.then_inc(y_ready, 1)

            def step(t, k):
                e = expert(pe, t)
                if inside(t + 1, NS):
                    up(t + 1, 1 - k)
                if inside(t + 2, NS):
                    turn_x(t + 2)
                down(t, k, e)

            turn_x(0)
            up(0, 0)
            turn_x(1)
            steps(pe, step, 1, NS - 2)

        @block.scalar
        def _(act):
            def roots(t, lo, hi):
                act.wait_ge(aggr, t + AHEAD + 1)
                act.activation(sd[:, lo:hi], mv[:, lo:hi, 1], ACT.Sqrt, bias=eps[:, :]).then_inc(rooted, 1)

            def copy_w(t):
                e = expert(act, t)
                for i in range(FH):
                    past(act, h_ready, FH * (t - 1) + i + 1 if beyond(t, 0) else 0)
                    act.activation(WS[:, :, i * NQ:(i + 1) * NQ], W1s[:, :, ds(e * F + i * NQ, NQ)], ACT.Copy)\
                       .then_inc(ws_ready, 1)

            def relu(t, k):
                e = expert(act, t)
                past(act, y_ready, t - 1)
                for i in range(FH):
                    act.wait_ge(h_ready, FH * t + i + 1)
                    for f in range(FC // FH):
                        ff = i * (FC // FH) + f
                        act.activation(HT[k][:, ff, :], hp[k][i][:, f, :], ACT.Relu,
                                       bias=PT[:, 2 * DC + ff, ds(e, 1)]).then_inc(relued, 1)

            def step(t, k):
                roots(t, *(norms_of(t) if isinstance(t, int) else (0, 3)))
                if inside(t + 2, NS):
                    copy_w(t + 2)
                if inside(t + 1, NS):
                    relu(t + 1, 1 - k)

            act.wait_ge(w1_in, 16 * E)
            copy_w(0)
            for t in range(-AHEAD, 0):
                roots(t, *norms_of(t))
            copy_w(1)
            relu(0, 0)
            steps(act, step, 1, NS - AHEAD)
            roots(NS, *norms_of(NS))

        @block.vector
        def _(dve):
            def affine(t, e):
                dve.wait_ge(xt_ready, t + 1)
                past(dve, h_ready, FH * t)
                for c in range(DC):
                    dve.tensor_scalar(XNT[:, c, :], xp[:, c * P:(c + 1) * P], PT[:, c, ds(e, 1)],
                                      PT[:, DC + c, ds(e, 1)], ALU.mult, ALU.add).then_inc(xnt_ready, 1)

            def step(t, lo, hi, turn=True):
                k = t + AHEAD
                a, b, c = t + AHEAD, t + AHEAD - 1, t - 1
                if hi == 3:
                    e = expert(dve, c)
                    if not beyond(c, 0):
                        dve.wait_ge(b2_in, 16)
                    dve.wait_ge(y_ready, c + 1)
                    dve.tensor_tensor(z0[:, :], yp[:, :], b2s[:, ds(e * D, D)], ALU.add).then_inc(z0_ready, 1)
                turned = expert(dve, t + 2) if turn else None
                if lo == 0:
                    dve.wait_ge(x1_kept, a + 1)
                    past(dve, xf_ready, a)
                    alone(dve, spare)
                    last = dve.bn_stats(st[:, 0, :], ring(X1, a))
                if lo <= 1 < hi:
                    dve.wait_ge(xf_ready, b + 1)
                    past(dve, xn_ready, b)
                    alone(dve, spare)
                    last = dve.bn_stats(st[:, 1, :], ring(XF, b))
                if hi == 3:
                    dve.wait_ge(z0_ready, c + 1)
                    past(dve, on_ready, c)
                    dve.tensor_tensor(z1[:, :], z0[:, :], ring(XF, c), ALU.add).then_inc(z1_ready, 1)
                    dve.wait_ge(z1_ready, c + 1)
                    alone(dve, spare)
                    last = dve.bn_stats(st[:, 2, :], z1[:, :])
                last.then_inc(stats, 1)
                dve.wait_ge(stats, k + 1)
                alone(dve, spare)
                for i in range(lo, hi):
                    last = dve.bn_aggr(mv[:, i, :], st[:, i, :])
                last.then_inc(aggr, 1)
                if turn:
                    affine(t + 2, turned)
                dve.wait_ge(rooted, k + 1)
                dve.reciprocal(rs[:, lo:hi], sd[:, lo:hi]).then_inc(inverted, 1)
                dve.wait_ge(inverted, k + 1)

                def apply(i, dst, src):
                    return dve.tensor_scalar(dst, src, mv[:, i, 0:1], rs[:, i:i + 1], ALU.subtract, ALU.mult)

                if hi == 3:
                    past(dve, o_ready, c)
                    apply(2, on[:, :], z1[:, :]).then_inc(on_ready, 1)
                if lo == 0:
                    apply(0, ring(XF, a), ring(X1, a)).then_inc(xf_ready, 1)
                if lo <= 1 < hi:
                    past(dve, xt_ready, b)
                    apply(1, XN[:, :], ring(XF, b)).then_inc(xn_ready, 1)
                if hi == 3:
                    dve.wait_ge(on_ready, c + 1)
                    past(dve, scattered, 16 * c)
                    dve.tensor_tensor(O[:, :], on[:, :], ring(X1, c), ALU.add).then_inc(o_ready, 1)

            for t in range(-AHEAD, 2):
                step(t, *norms_of(t), t + 2 >= 0)
            with dve.Fori(2, NS - AHEAD) as t:
                step(t, 0, 3)
            for t in range(NS - AHEAD, NS + 1):
                step(t, *norms_of(t), t + 2 < NS)


_INS = ['L0_attn_x', 'L0_attn_Wc_down', 'L0_attn_Wq_up', 'L0_attn_Wkv_up', 'L0_attn_Wc_proj', 'L0_ffn_centroids',
        'L0_ffn_ln_g', 'L0_ffn_ln_b', 'L0_ffn_W1', 'L0_ffn_b1', 'L0_ffn_W2', 'L0_ffn_b2']
_OUTS = [((4, 1024, 256), 'float32')]


def kernel(**inputs):
    import numpy as _np
    import concourse.bacc as _bacc
    from concourse import mybir as _mybir
    from concourse.bass_utils import run_bass_kernel_spmd as _run

    nc = _bacc.Bacc("TRN2", target_bir_lowering=False, num_devices=1)
    arrays, args = {}, []
    for name in _INS:
        a = _np.ascontiguousarray(inputs[name])
        arrays[f"in_{name}_dram"] = a
        args.append(nc.dram_tensor(f"in_{name}_dram", a.shape, _mybir.dt.from_np(a.dtype), kind="ExternalInput").ap())
    for i, (shape, dtype) in enumerate(_OUTS):
        dt = _mybir.dt.from_np(_np.dtype(dtype))
        args.append(nc.dram_tensor(f"out_{i}_dram", shape, dt, kind="ExternalOutput").ap())
    build(nc, *args)
    r = _run(nc, [arrays], core_ids=[0])
    got = tuple(r.results[0][f"out_{i}_dram"] for i in range(len(_OUTS)))
    return got[0]
```
